# Optimizing a Trainium2 kernel written in Bass

```python
import numpy as np
import jax
import jax.numpy as jnp

def _softmax(x, axis=-1):
    return jax.nn.softmax(x, axis=axis)

def _gelu(x):
    return jax.nn.gelu(x, approximate=True)

def _silu(x):
    return jax.nn.silu(x)

def _sigmoid(x):
    return jax.nn.sigmoid(x)

def _layernorm(x, axis=-1, eps=1e-05):
    m = jnp.mean(x, axis=axis, keepdims=True)
    v = jnp.var(x, axis=axis, keepdims=True)
    return (x - m) / jnp.sqrt(v + eps)

def _scatter_add(tgt, idx, src, axis=0):
    return tgt.at[idx].add(src)

def _segment_sum(src, seg, n):
    return jax.ops.segment_sum(src, seg, n)
kernel_name = 'mk_adaln_d2_jaxref_r8_4572e6'

def setup_inputs(seed: int=0):
    np.random.seed(seed)
    _w = jnp.asarray

    def _L0_attn_setup():
        import jax, jax.numpy as jnp
        import numpy as np
        BETA = 0.3
        THRESH = 0.05
        ATAN_ALPHA = 2.0
        EPS = 1e-06

        @jax.custom_vjp
        def spike_fn(u):
            return (u > 0).astype(u.dtype)

        def _spike_fwd(u):
            return (spike_fn(u), u)

        def _spike_bwd(u, g):
            return (g * (ATAN_ALPHA / 2) / (1 + (jnp.pi / 2 * ATAN_ALPHA * u) ** 2),)
        spike_fn.defvjp(_spike_fwd, _spike_bwd)
        key = jax.random.key(seed)
        ks = jax.random.split(key, 10)
        B, T, D = (4, 512, 128)
        s = 1.0 / np.sqrt(D)
        u = lambda k, shape: jax.random.uniform(k, shape, jnp.float32, -s, s)
        return {'x': jax.random.normal(ks[0], (B, T, D), jnp.float32), 'W_r': u(ks[1], (D, D)), 'b_r': u(ks[2], (D,)), 'W_k': u(ks[3], (D, D)), 'b_k': u(ks[4], (D,)), 'W_v': u(ks[5], (D, D)), 'b_v': u(ks[6], (D,)), 'W_td': u(ks[7], (D, D)), 'b_td': u(ks[8], (D,)), 'global_decay': jax.random.normal(ks[9], (D,), jnp.float32)}
    _L0_attn_in = _L0_attn_setup()

    def _L0_ffn_setup():
        import jax, jax.numpy as jnp
        import numpy as np
        DIM = 128
        DEPTH = 2
        HEADS = 8
        DIM_HEAD = 64
        WINDOW = 64
        INNER = HEADS * DIM_HEAD
        HID = int(DIM * 4 * 2 / 3)
        B, N = (2, 1024)
        QK_SCALE = 8.0

        def shift_token(t):
            t1, t2 = jnp.split(t, 2, axis=-1)
            t2 = jnp.pad(t2, ((0, 0), (1, 0), (0, 0)))[:, :-1]
            return jnp.concatenate([t1, t2], axis=-1)

        def l2norm(t):
            return t / jnp.clip(jnp.linalg.norm(t, axis=-1, keepdims=True), 1e-12)

        def rotate_half(x):
            x1, x2 = jnp.split(x, 2, axis=-1)
            return jnp.concatenate([-x2, x1], axis=-1)

        def rotary_xpos(q, k):
            n = q.shape[-2]
            half_idx = jnp.arange(0, DIM_HEAD, 2, dtype=jnp.float32)
            inv_freq = 1.0 / 10000.0 ** (half_idx / DIM_HEAD)
            t = jnp.arange(n, dtype=jnp.float32)
            freqs = t[:, None] * inv_freq[None, :]
            freqs = jnp.concatenate([freqs, freqs], axis=-1)
            base = (half_idx + 0.4 * DIM_HEAD) / (1.4 * DIM_HEAD)
            power = (t - n // 2) / float(WINDOW // 2)
            scale = base[None, :] ** power[:, None]
            scale = jnp.concatenate([scale, scale], axis=-1)
            cos, sin = (jnp.cos(freqs), jnp.sin(freqs))
            q = q * cos * scale + rotate_half(q) * sin * scale
            k = k * cos / scale + rotate_half(k) * sin / scale
            return (q, k)

        def local_attention(q, k, v):
            b, h, n, d = q.shape
            w = n // WINDOW
            bq = q.reshape(b, h, w, WINDOW, d) * QK_SCALE
            bk = k.reshape(b, h, w, WINDOW, d)
            bv = v.reshape(b, h, w, WINDOW, d)

            def look_around(t):
                p = jnp.pad(t, ((0, 0), (0, 0), (1, 0), (0, 0), (0, 0)))
                return jnp.concatenate([p[:, :, :w], p[:, :, 1:]], axis=3)
            bk, bv = (look_around(bk), look_around(bv))
            bt = jnp.arange(n).reshape(w, WINDOW)
            btp = jnp.pad(bt, ((1, 0), (0, 0)), constant_values=-1)
            btk = jnp.concatenate([btp[:w], btp[1:]], axis=1)
            sim = jnp.einsum('bhwid,bhwjd->bhwij', bq, bk)
            i = bt[:, :, None]
            j = btk[:, None, :]
            mask = (i < j) | (i > j + WINDOW) | (j == -1)
            sim = jnp.where(mask, -jnp.finfo(sim.dtype).max, sim)
            attn = jax.nn.softmax(sim, axis=-1)
            out = jnp.einsum('bhwij,bhwjd->bhwid', attn, bv)
            return out.reshape(b, h, n, d)

        def _layer(x, wqkv, qs, ksc, wo, lg, lb, w1, b1, w2, b2):
            b, n, _ = x.shape
            h = shift_token(x)
            qkv = h @ wqkv
            q, k, v = jnp.split(qkv, 3, axis=-1)
            to_heads = lambda t: t.reshape(b, n, HEADS, DIM_HEAD).transpose(0, 2, 1, 3)
            q, k, v = (to_heads(q), to_heads(k), to_heads(v))
            q = l2norm(q) * qs
            k = l2norm(k) * ksc
            q, k = rotary_xpos(q, k)
            o = local_attention(q, k, v)
            o = o.transpose(0, 2, 1, 3).reshape(b, n, INNER)
            x = x + o @ wo
            h = shift_token(x)
            mu = h.mean(-1, keepdims=True)
            var = h.var(-1, keepdims=True)
            h = (h - mu) / jnp.sqrt(var + 1e-05) * lg + lb
            h = h @ w1 + b1
            a, g = jnp.split(h, 2, axis=-1)
            h = a * jax.nn.gelu(g, approximate=False)
            x = x + h @ w2 + b2
            return x
        key = jax.random.key(seed)
        ks = jax.random.split(key, 6)
        return {'x': jax.random.normal(ks[0], (B, N, DIM), jnp.float32), 'wqkv': jax.random.normal(ks[1], (DEPTH, DIM, 3 * INNER), jnp.float32) * 0.02, 'q_scale': jnp.ones((DEPTH, DIM_HEAD), jnp.float32), 'k_scale': jnp.ones((DEPTH, DIM_HEAD), jnp.float32), 'wo': jax.random.normal(ks[2], (DEPTH, INNER, DIM), jnp.float32) * 0.02, 'ln_g': jnp.ones((DEPTH, DIM), jnp.float32), 'ln_b': jnp.zeros((DEPTH, DIM), jnp.float32), 'w1': jax.random.normal(ks[3], (DEPTH, DIM, 2 * HID), jnp.float32) * 0.02, 'b1': jnp.zeros((DEPTH, 2 * HID), jnp.float32), 'w2': jax.random.normal(ks[4], (DEPTH, HID, DIM), jnp.float32) * 0.02, 'b2': jnp.zeros((DEPTH, DIM), jnp.float32)}
    _L0_ffn_in = _L0_ffn_setup()
    _L0_c = _w((lambda *s: np.random.randn(*s).astype(np.float32) * 0.05)(2, 128))
    _L0_wmod = _w((lambda *s: np.random.randn(*s).astype(np.float32) * 0.05)(128, 6 * 128) * 128 ** (-0.5))

    def _L1_attn_setup():
        import jax, jax.numpy as jnp
        import numpy as np
        import math
        B_SZ, T, D_IN, D_OUT, N = (8, 512, 128, 128, 64)
        RMIN, RMAX, MAX_PHASE = (0.9, 1.0, 6.283)
        key = jax.random.key(seed)
        ks = jax.random.split(key, 9)
        x = jax.random.normal(ks[0], (B_SZ, T, D_IN), dtype=jnp.float32)
        u1 = jax.random.uniform(ks[1], (N,), dtype=jnp.float32)
        u2 = jax.random.uniform(ks[2], (N,), dtype=jnp.float32)
        nu_log = jnp.log(-0.5 * jnp.log(u1 * (RMAX + RMIN) * (RMAX - RMIN) + RMIN ** 2))
        theta_log = jnp.log(MAX_PHASE * u2)
        lam_mod = jnp.exp(-jnp.exp(nu_log))
        gamma_log = jnp.log(jnp.sqrt(1.0 - jnp.square(lam_mod)))
        B_re = jax.random.normal(ks[3], (N, D_IN), dtype=jnp.float32) / math.sqrt(2 * D_IN)
        B_im = jax.random.normal(ks[4], (N, D_IN), dtype=jnp.float32) / math.sqrt(2 * D_IN)
        C_re = jax.random.normal(ks[5], (D_OUT, N), dtype=jnp.float32) / math.sqrt(N)
        C_im = jax.random.normal(ks[6], (D_OUT, N), dtype=jnp.float32) / math.sqrt(N)
        D = jax.random.normal(ks[7], (D_OUT, D_IN), dtype=jnp.float32) / math.sqrt(D_IN)
        return {'x': x, 'nu_log': nu_log, 'theta_log': theta_log, 'gamma_log': gamma_log, 'B_re': B_re, 'B_im': B_im, 'C_re': C_re, 'C_im': C_im, 'D': D}
    _L1_attn_in = _L1_attn_setup()

    def _L1_ffn_setup():
        import jax, jax.numpy as jnp
        import numpy as np
        D_MODEL = 128
        H_SHARED = 256
        H_ROUTED = 128
        N_EXPERTS = 8
        TOP_K = 2
        key = jax.random.key(seed)
        ks = jax.random.split(key, 8)
        B, T = (2, 256)
        sc_d = 1.0 / np.sqrt(D_MODEL)
        sc_hs = 1.0 / np.sqrt(H_SHARED)
        sc_hr = 1.0 / np.sqrt(H_ROUTED)
        return {'x': jax.random.normal(ks[0], (B, T, D_MODEL), dtype=jnp.float32), 'router_w': jax.random.normal(ks[1], (N_EXPERTS, D_MODEL), dtype=jnp.float32) * sc_d, 'router_bias': jnp.zeros((N_EXPERTS,), dtype=jnp.float32), 'sw1': jax.random.normal(ks[2], (D_MODEL, H_SHARED), dtype=jnp.float32) * sc_d, 'sw3': jax.random.normal(ks[3], (D_MODEL, H_SHARED), dtype=jnp.float32) * sc_d, 'sw2': jax.random.normal(ks[4], (H_SHARED, D_MODEL), dtype=jnp.float32) * sc_hs, 'ew1': jax.random.normal(ks[5], (N_EXPERTS, D_MODEL, H_ROUTED), dtype=jnp.float32) * sc_d, 'ew2': jax.random.normal(ks[6], (N_EXPERTS, H_ROUTED, D_MODEL), dtype=jnp.float32) * sc_hr}
    _L1_ffn_in = _L1_ffn_setup()
    _L1_c = _w((lambda *s: np.random.randn(*s).astype(np.float32) * 0.05)(2, 128))
    _L1_wmod = _w((lambda *s: np.random.randn(*s).astype(np.float32) * 0.05)(128, 6 * 128) * 128 ** (-0.5))
    _d = {'L0_attn_x': _L0_attn_in['x'], 'L0_attn_W_r': _L0_attn_in['W_r'], 'L0_attn_b_r': _L0_attn_in['b_r'], 'L0_attn_W_k': _L0_attn_in['W_k'], 'L0_attn_b_k': _L0_attn_in['b_k'], 'L0_attn_W_v': _L0_attn_in['W_v'], 'L0_attn_b_v': _L0_attn_in['b_v'], 'L0_attn_W_td': _L0_attn_in['W_td'], 'L0_attn_b_td': _L0_attn_in['b_td'], 'L0_attn_global_decay': _L0_attn_in['global_decay'], 'L0_ffn_wqkv': _L0_ffn_in['wqkv'], 'L0_ffn_q_scale': _L0_ffn_in['q_scale'], 'L0_ffn_k_scale': _L0_ffn_in['k_scale'], 'L0_ffn_wo': _L0_ffn_in['wo'], 'L0_ffn_ln_g': _L0_ffn_in['ln_g'], 'L0_ffn_ln_b': _L0_ffn_in['ln_b'], 'L0_ffn_w1': _L0_ffn_in['w1'], 'L0_ffn_b1': _L0_ffn_in['b1'], 'L0_ffn_w2': _L0_ffn_in['w2'], 'L0_ffn_b2': _L0_ffn_in['b2'], 'L0_c': _L0_c, 'L0_wmod': _L0_wmod, 'L1_attn_nu_log': _L1_attn_in['nu_log'], 'L1_attn_theta_log': _L1_attn_in['theta_log'], 'L1_attn_gamma_log': _L1_attn_in['gamma_log'], 'L1_attn_B_re': _L1_attn_in['B_re'], 'L1_attn_B_im': _L1_attn_in['B_im'], 'L1_attn_C_re': _L1_attn_in['C_re'], 'L1_attn_C_im': _L1_attn_in['C_im'], 'L1_attn_D': _L1_attn_in['D'], 'L1_ffn_router_w': _L1_ffn_in['router_w'], 'L1_ffn_router_bias': _L1_ffn_in['router_bias'], 'L1_ffn_sw1': _L1_ffn_in['sw1'], 'L1_ffn_sw3': _L1_ffn_in['sw3'], 'L1_ffn_sw2': _L1_ffn_in['sw2'], 'L1_ffn_ew1': _L1_ffn_in['ew1'], 'L1_ffn_ew2': _L1_ffn_in['ew2'], 'L1_c': _L1_c, 'L1_wmod': _L1_wmod}
    _x0 = _d['L0_attn_x']
    _d['L0_attn_x'] = jax.random.normal(jax.random.fold_in(jax.random.key(seed), 1), (2, 1024, 128), dtype=_x0.dtype)
    del _x0
    return _d

def reference(L0_attn_x, L0_attn_W_r, L0_attn_b_r, L0_attn_W_k, L0_attn_b_k, L0_attn_W_v, L0_attn_b_v, L0_attn_W_td, L0_attn_b_td, L0_attn_global_decay, L0_ffn_wqkv, L0_ffn_q_scale, L0_ffn_k_scale, L0_ffn_wo, L0_ffn_ln_g, L0_ffn_ln_b, L0_ffn_w1, L0_ffn_b1, L0_ffn_w2, L0_ffn_b2, L0_c, L0_wmod, L1_attn_nu_log, L1_attn_theta_log, L1_attn_gamma_log, L1_attn_B_re, L1_attn_B_im, L1_attn_C_re, L1_attn_C_im, L1_attn_D, L1_ffn_router_w, L1_ffn_router_bias, L1_ffn_sw1, L1_ffn_sw3, L1_ffn_sw2, L1_ffn_ew1, L1_ffn_ew2, L1_c, L1_wmod):

    def _L0_attn_ref(x, W_r, b_r, W_k, b_k, W_v, b_v, W_td, b_td, global_decay):
        import jax, jax.numpy as jnp
        import numpy as np
        BETA = 0.3
        THRESH = 0.05
        ATAN_ALPHA = 2.0
        EPS = 1e-06

        @jax.custom_vjp
        def spike_fn(u):
            return (u > 0).astype(u.dtype)

        def _spike_fwd(u):
            return (spike_fn(u), u)

        def _spike_bwd(u, g):
            return (g * (ATAN_ALPHA / 2) / (1 + (jnp.pi / 2 * ATAN_ALPHA * u) ** 2),)
        spike_fn.defvjp(_spike_fwd, _spike_bwd)
        B, T, D = x.shape
        r = jax.nn.sigmoid(jnp.einsum('btd,ed->bte', x, W_r) + b_r)
        ek = jnp.exp(jnp.einsum('btd,ed->bte', x, W_k) + b_k)
        v = jnp.einsum('btd,ed->bte', x, W_v) + b_v
        td = jnp.exp(b_td)
        g = jnp.exp(global_decay)

        def step(carry, inputs):
            sa, sb, mem = carry
            ek_t, v_t, r_t = inputs
            sa = ek_t * v_t + td * sa
            sb = ek_t + td * sb
            wkv = (g * ek_t * v_t + sa) / (g * ek_t + sb + EPS)
            inp_t = r_t * wkv
            reset = spike_fn(mem - THRESH)
            mem = BETA * mem + inp_t - reset * THRESH
            spk = spike_fn(mem - THRESH)
            return ((sa, sb, mem), spk)
        z = jnp.zeros((B, D), x.dtype)
        xs = (jnp.swapaxes(ek, 0, 1), jnp.swapaxes(v, 0, 1), jnp.swapaxes(r, 0, 1))
        _, spks = jax.lax.scan(step, (z, z, z), xs)
        return jnp.swapaxes(spks, 0, 1)

    def _L0_ffn_ref(x, wqkv, q_scale, k_scale, wo, ln_g, ln_b, w1, b1, w2, b2):
        import jax, jax.numpy as jnp
        import numpy as np
        DIM = 128
        DEPTH = 2
        HEADS = 8
        DIM_HEAD = 64
        WINDOW = 64
        INNER = HEADS * DIM_HEAD
        HID = int(DIM * 4 * 2 / 3)
        B, N = (2, 1024)
        QK_SCALE = 8.0

        def shift_token(t):
            t1, t2 = jnp.split(t, 2, axis=-1)
            t2 = jnp.pad(t2, ((0, 0), (1, 0), (0, 0)))[:, :-1]
            return jnp.concatenate([t1, t2], axis=-1)

        def l2norm(t):
            return t / jnp.clip(jnp.linalg.norm(t, axis=-1, keepdims=True), 1e-12)

        def rotate_half(x):
            x1, x2 = jnp.split(x, 2, axis=-1)
            return jnp.concatenate([-x2, x1], axis=-1)

        def rotary_xpos(q, k):
            n = q.shape[-2]
            half_idx = jnp.arange(0, DIM_HEAD, 2, dtype=jnp.float32)
            inv_freq = 1.0 / 10000.0 ** (half_idx / DIM_HEAD)
            t = jnp.arange(n, dtype=jnp.float32)
            freqs = t[:, None] * inv_freq[None, :]
            freqs = jnp.concatenate([freqs, freqs], axis=-1)
            base = (half_idx + 0.4 * DIM_HEAD) / (1.4 * DIM_HEAD)
            power = (t - n // 2) / float(WINDOW // 2)
            scale = base[None, :] ** power[:, None]
            scale = jnp.concatenate([scale, scale], axis=-1)
            cos, sin = (jnp.cos(freqs), jnp.sin(freqs))
            q = q * cos * scale + rotate_half(q) * sin * scale
            k = k * cos / scale + rotate_half(k) * sin / scale
            return (q, k)

        def local_attention(q, k, v):
            b, h, n, d = q.shape
            w = n // WINDOW
            bq = q.reshape(b, h, w, WINDOW, d) * QK_SCALE
            bk = k.reshape(b, h, w, WINDOW, d)
            bv = v.reshape(b, h, w, WINDOW, d)

            def look_around(t):
                p = jnp.pad(t, ((0, 0), (0, 0), (1, 0), (0, 0), (0, 0)))
                return jnp.concatenate([p[:, :, :w], p[:, :, 1:]], axis=3)
            bk, bv = (look_around(bk), look_around(bv))
            bt = jnp.arange(n).reshape(w, WINDOW)
            btp = jnp.pad(bt, ((1, 0), (0, 0)), constant_values=-1)
            btk = jnp.concatenate([btp[:w], btp[1:]], axis=1)
            sim = jnp.einsum('bhwid,bhwjd->bhwij', bq, bk)
            i = bt[:, :, None]
            j = btk[:, None, :]
            mask = (i < j) | (i > j + WINDOW) | (j == -1)
            sim = jnp.where(mask, -jnp.finfo(sim.dtype).max, sim)
            attn = jax.nn.softmax(sim, axis=-1)
            out = jnp.einsum('bhwij,bhwjd->bhwid', attn, bv)
            return out.reshape(b, h, n, d)

        def _layer(x, wqkv, qs, ksc, wo, lg, lb, w1, b1, w2, b2):
            b, n, _ = x.shape
            h = shift_token(x)
            qkv = h @ wqkv
            q, k, v = jnp.split(qkv, 3, axis=-1)
            to_heads = lambda t: t.reshape(b, n, HEADS, DIM_HEAD).transpose(0, 2, 1, 3)
            q, k, v = (to_heads(q), to_heads(k), to_heads(v))
            q = l2norm(q) * qs
            k = l2norm(k) * ksc
            q, k = rotary_xpos(q, k)
            o = local_attention(q, k, v)
            o = o.transpose(0, 2, 1, 3).reshape(b, n, INNER)
            x = x + o @ wo
            h = shift_token(x)
            mu = h.mean(-1, keepdims=True)
            var = h.var(-1, keepdims=True)
            h = (h - mu) / jnp.sqrt(var + 1e-05) * lg + lb
            h = h @ w1 + b1
            a, g = jnp.split(h, 2, axis=-1)
            h = a * jax.nn.gelu(g, approximate=False)
            x = x + h @ w2 + b2
            return x
        for l in range(DEPTH):
            x = _layer(x, wqkv[l], q_scale[l], k_scale[l], wo[l], ln_g[l], ln_b[l], w1[l], b1[l], w2[l], b2[l])
        return x

    def _L1_attn_ref(x, nu_log, theta_log, gamma_log, B_re, B_im, C_re, C_im, D):
        import jax, jax.numpy as jnp
        import numpy as np
        import math
        B_SZ, T, D_IN, D_OUT, N = (8, 512, 128, 128, 64)
        RMIN, RMAX, MAX_PHASE = (0.9, 1.0, 6.283)
        lam = jnp.exp(-jnp.exp(nu_log) + 1j * jnp.exp(theta_log))
        gamma = jnp.exp(gamma_log)
        Bmat = B_re + 1j * B_im
        Bu = jnp.einsum('bti,ni->btn', x.astype(Bmat.dtype), Bmat) * gamma
        A = jnp.broadcast_to(lam, Bu.shape)

        def combine(e1, e2):
            a1, b1 = e1
            a2, b2 = e2
            return (a1 * a2, a2 * b1 + b2)
        _, states = jax.lax.associative_scan(combine, (A, Bu), axis=1)
        Cmat = C_re + 1j * C_im
        y = jnp.einsum('btn,on->bto', states, Cmat).real + jnp.einsum('bti,oi->bto', x, D)
        return y

    def _L1_ffn_ref(x, router_w, router_bias, sw1, sw3, sw2, ew1, ew2):
        import jax, jax.numpy as jnp
        import numpy as np
        D_MODEL = 128
        H_SHARED = 256
        H_ROUTED = 128
        N_EXPERTS = 8
        TOP_K = 2
        B, T, C = x.shape
        xf = x.reshape(-1, C)
        shared_out = jax.nn.silu(xf @ sw1) * (xf @ sw3) @ sw2
        s = jax.nn.sigmoid((xf @ router_w.T).astype(jnp.float32))
        sel_scores = s + router_bias.astype(jnp.float32)
        _, topk_idx = jax.lax.top_k(sel_scores, TOP_K)
        s_sel = jnp.take_along_axis(s, topk_idx, axis=1)
        denom = s_sel.sum(axis=1, keepdims=True)
        gates = jnp.where(denom > 1e-09, s_sel / (denom + 1e-09), 1.0 / TOP_K).astype(x.dtype)
        one_hot = jax.nn.one_hot(topk_idx, N_EXPERTS, dtype=x.dtype)
        comb = jnp.einsum('nke,nk->ne', one_hot, gates)
        h = jax.nn.gelu(jnp.einsum('nd,edh->neh', xf, ew1), approximate=False)
        y = jnp.einsum('neh,ehd->ned', h, ew2)
        routed_out = jnp.einsum('ned,ne->nd', y, comb)
        return (shared_out + routed_out).reshape(B, T, C)
    x = L0_attn_x
    mod = (_silu(L0_c) @ L0_wmod).reshape(L0_c.shape[0], 6, 1, -1)
    sa, ca, ga, sb, cb, gb = (mod[:, 0], mod[:, 1], mod[:, 2], mod[:, 3], mod[:, 4], mod[:, 5])
    ga = (2 * (ga >= 0) - 1) * jnp.maximum(jnp.abs(ga), 0.25)
    gb = (2 * (gb >= 0) - 1) * jnp.maximum(jnp.abs(gb), 0.25)
    h = _layernorm(x, axis=-1) * (1 + ca) + sa
    x = x + ga * _L0_attn_ref(h, L0_attn_W_r, L0_attn_b_r, L0_attn_W_k, L0_attn_b_k, L0_attn_W_v, L0_attn_b_v, L0_attn_W_td, L0_attn_b_td, L0_attn_global_decay)
    h = _layernorm(x, axis=-1) * (1 + cb) + sb
    x = x + gb * _L0_ffn_ref(h, L0_ffn_wqkv, L0_ffn_q_scale, L0_ffn_k_scale, L0_ffn_wo, L0_ffn_ln_g, L0_ffn_ln_b, L0_ffn_w1, L0_ffn_b1, L0_ffn_w2, L0_ffn_b2)
    mod = (_silu(L1_c) @ L1_wmod).reshape(L1_c.shape[0], 6, 1, -1)
    sa, ca, ga, sb, cb, gb = (mod[:, 0], mod[:, 1], mod[:, 2], mod[:, 3], mod[:, 4], mod[:, 5])
    ga = (2 * (ga >= 0) - 1) * jnp.maximum(jnp.abs(ga), 0.25)
    gb = (2 * (gb >= 0) - 1) * jnp.maximum(jnp.abs(gb), 0.25)
    h = _layernorm(x, axis=-1) * (1 + ca) + sa
    x = x + ga * _L1_attn_ref(h, L1_attn_nu_log, L1_attn_theta_log, L1_attn_gamma_log, L1_attn_B_re, L1_attn_B_im, L1_attn_C_re, L1_attn_C_im, L1_attn_D)
    h = _layernorm(x, axis=-1) * (1 + cb) + sb
    x = x + gb * _L1_ffn_ref(h, L1_ffn_router_w, L1_ffn_router_bias, L1_ffn_sw1, L1_ffn_sw3, L1_ffn_sw2, L1_ffn_ew1, L1_ffn_ew2)
    return x

_drawn_inputs = setup_inputs


def setup_inputs(seed=0):
    import zlib

    import numpy as np

    out = dict(_drawn_inputs(seed))
    spreads = {'L0_ffn_q_scale': (1.0, 0.6),
     'L0_ffn_k_scale': (1.0, 0.6),
     'L0_ffn_ln_g': (1.0, 0.6),
     'L0_ffn_ln_b': (0.0, 0.8),
     'L0_ffn_b1': (0.0, 0.8),
     'L0_ffn_b2': (0.0, 0.757),
     'L1_ffn_router_bias': (0.0, 0.8)}
    factors = {'L0_ffn_wqkv': 5.154,
     'L0_ffn_wo': 5.245,
     'L0_ffn_w1': 8.0,
     'L0_ffn_w2': 7.84,
     'L1_attn_nu_log': 3.39,
     'L1_attn_gamma_log': 2.831,
     'L1_attn_B_re': 3.476,
     'L1_attn_B_im': 3.465,
     'L1_attn_C_re': 3.447,
     'L1_attn_C_im': 3.488,
     'L1_ffn_router_w': 5.265,
     'L1_ffn_sw1': 3.753,
     'L1_ffn_sw3': 3.576,
     'L1_ffn_sw2': 3.562,
     'L1_ffn_ew1': 5.125,
     'L1_ffn_ew2': 4.642}
    for name, (base, spread) in spreads.items():
        noise = np.random.default_rng([zlib.crc32(name.encode()), seed]).standard_normal(out[name].shape)
        drawn = base * np.exp(spread * noise) if base else spread * noise
        out[name] = jnp.asarray(drawn.astype(out[name].dtype))
    for name, factor in factors.items():
        out[name] = (out[name] * factor).astype(out[name].dtype)
    return out
```

```python
from contextlib import ExitStack

import numpy as np
import concourse.bass as bass
from concourse import mybir

F32 = mybir.dt.float32
BF16 = mybir.dt.bfloat16
I32 = mybir.dt.int32
ALU = mybir.AluOpType
ACT = mybir.ActivationFunctionType
AX = mybir.AxisListType

P = 128
B, T = 2, 1024
NTOK = B * T
NT = NTOK // P
GW = 512
NG = NTOK // GW
GPB = NG // B
TPG = GW // P
LAYERS = 2
H, DH = 8, 64
W = 64
INNER = H * DH
HID = 341
HCH = [(0, 128), (128, 128), (256, 85)]
NE = 8
SEQ = 16
NCH = T // SEQ
PASSES = 4
EPS = 1e-5
TWO_PI = 6.283185

V_BR, V_BK, V_BV, V_BTD, V_GD = range(5)
V_LNG, V_LNB, V_B2 = 5, 7, 9
V_B1 = 11
V_C = 23
V_NU, V_TH, V_GAM, V_SGN = 27, 28, 29, 30
NV = 31

SA, CA, GA, SB, CB, GB = range(6)


class Steps:

    def __init__(self, eng, sem):
        self.eng, self.sem, self.base, self.n = eng, sem, 0, 0

    def did(self, ins):
        ins.then_inc(self.sem, 1)
        self.n += 1

    def sync(self):
        self.eng.wait_ge(self.sem, self.base + self.n)

    def one(self, ins):
        self.did(ins)
        self.sync()

    def enter(self, i, per):
        self.start, self.per = self.base + self.n, per
        self.base, self.n = self.start + i * per, 0

    def leave(self, times):
        assert self.n == self.per, (self.n, self.per)
        self.base, self.n = self.start + times * self.per, 0


def program(nc, a, out):
    with ExitStack() as ctx:
        def sb(name, shape, dt=F32):
            return ctx.enter_context(nc.sbuf_tensor(name, shape, dt))

        def ps(name, shape):
            return ctx.enter_context(nc.psum_tensor(name, shape, F32))

        def sem(name):
            return ctx.enter_context(nc.semaphore(name))

        ident = sb("ident", [P, P])
        identb = sb("identb", [P, P], BF16)
        masks = sb("masks", [P, NT, P], BF16)
        vec = sb("vec", [P, NV])
        wrkv = sb("wrkv", [P, 3, P])
        wmod = sb("wmod", [P, 2, 6 * P])
        wqkv = sb("wqkv", [P, 3 * INNER])
        wo = sb("wo", [P, 4, P])
        w1 = sb("w1", [P, 2 * HID])
        w2 = sb("w2", [P, 3, P])
        wlru = sb("wlru", [P, 5, P])
        wcs = sb("wcs", [P, 2, P])
        wsh = sb("wsh", [P, 2, 256])
        wsh2 = sb("wsh2", [P, 2, P])
        wrt = sb("wrt", [P, NE])
        rbias = sb("rbias", [P, NE])
        before = sb("before", [P, NE, NE])
        ropeb = sb("ropeb", [P, NT // B, 4, DH])
        qks = sb("qks", [P, 2, 2, DH])
        rope = sb("rope", [P, NT, 4, DH])
        half = sb("half", [P, 16])
        mod = sb("mod", [P, 2, 6, 2])
        modt = sb("modt", [P, 2, 2, 4])
        silc = sb("silc", [P, 4])
        sc = sb("sc", [P, 16])
        fr = sb("fr", [P, 16])
        zero = sb("zero", [P, 1])
        zeros = sb("zeros", [P, P])
        zeros2 = sb("zeros2", [P, 4])

        x_cm = sb("x_cm", [P, NTOK])
        z = sb("z", [P, NTOK])
        hsA = sb("hsA", [P, NTOK])
        big = sb("big", [P, 7, NTOK])
        xt = big[:, 6, :].rearrange("p (n d) -> p n d", n=NT)
        tvec = big[:, 5, 0:T]
        ek, gek, ekv, sab, sbb, _, rsg = (big[:, i, :] for i in range(7))
        oT = big[:, 0:4, :]
        hsM = big[:, 4, :]
        ew1 = big[:, 6, 0:NE * P].rearrange("p (e n) -> p e n", e=NE)
        ew2 = big[:, 6, NE * P:].rearrange("p (e n) -> p e n", e=NE)
        tcos = big[:, 5, T:]
        tsin = sb("tsin", [P, T])
        ph = sb("ph", [P, B, T + 1])

        lnx = sb("lnx", [P, TPG, P])
        st6 = sb("st6", [P, TPG, 6])
        mv = sb("mv", [P, TPG, 2])
        rst = sb("rst", [P, TPG])
        hn = sb("hn", [P, 2, GW])

        hst = sb("hst", [P, P])
        sq = sb("sq", [P, 2 * INNER])
        ra = sb("ra", [P, 2 * INNER])
        rb = sb("rb", [P, 2 * INNER])
        qkn = sb("qkn", [P, 2 * INNER])
        nw = sb("nw", [P, 4, 16])
        nwi = sb("nwi", [P, 16], I32)
        qTp = sb("qTp", [P, H, P])
        kTb = sb("kTb", [P, 4, W + P])
        nmx = sb("nmx", [P, H])
        prob = sb("prob", [P, H, P])
        pT = sb("pT", [P, H, P])
        vA = sb("vA", [P, H, DH + 1])
        vB = sb("vB", [P, H, DH + 1])
        orc = sb("orc", [P, H])
        osb = sb("osb", [P, INNER])

        gel = sb("gel", [P, 2, GW])
        hg = sb("hg", [P, 3, GW])

        vst = sb("vst", [P, B, NCH])
        cend = sb("cend", [P, B, NCH])
        cnt = sb("cnt", [P, 32])
        cntT = sb("cntT", [P, 32])
        cnti = sb("cnti", [1, 8], I32)
        cntf = sb("cntf", [1, 8])

        psQK = ps("psQK", [P, 2, GW])
        psS = ps("psS", [P, 2, GW])
        psO = ps("psO", [P, 2, GW])
        psT0 = ps("psT0", [P, GW])
        psT1 = ps("psT1", [P, GW])

        names = """ld_x ld_ew ld_c ld_wa ld_wq ld_wl ld_lru ld_moe ld_out st_out
            init silu_c mod_mm mod_fin mod_sc
            ln_t1 ln_var ln_rstd ln_norm ln_t2 ln_out
            xT_fill xT_evac
            kv_mm ek_ready gek_ready ekv_ready sb_ready den_ready r_mm r_ready u_ready mem_done x_mixed
            dve act_own pool_own fallback rope_ready tabs_phase tabs_ready z_ready hsA_ready
            staged qk_mm v_mm sq_done rope_ab rope_c rn_ready q_ready k_ready
            t_filled t_evac kprev s_done negmax p_ready pv_done va_prev va_cur o_norm attn_done
            wo_done zmid hsM_ready g_mm a_mm gelu_done hg_done w2_done
            bu_mm bu_half lru_g lru_m1 lru_m2 lru_a y_done xmid_ready
            rt_mm sig_done comb_ready sh_mm sh_act sh_h ey_done eh_mm eh_act ey_used acc_done
            gb_mm gb_ready fx_t out_ready""".split()
        s = {n: sem(n) for n in names}

        block = ctx.enter_context(nc.Block())

        def gsl(g):
            return slice(g * GW, (g + 1) * GW)

        def bof(g):
            return g // GPB

        def ln_no(stage, g):
            return stage * NG + g

        TE0, TF0 = 0, 0
        TE_PER, TF_PER = 2 + 7 * (NT - 1) + 6, 1 + 6 * (NT - 1) + 5
        UNR = 3

        @block.sync
        def _(sp):
            xr = a["x"].rearrange("b t d -> (b t) d").rearrange("(n p) d -> p n d", p=P)
            for g in range(NG):
                sp.dma_start(xt[:, g * TPG:(g + 1) * TPG, :], xr[:, g * TPG:(g + 1) * TPG, :]).then_inc(s["ld_x"], 16)
            sp.dma_start(wrkv[:, :, :], a["wrkv"]).then_inc(s["ld_wa"], 16)
            sp.dma_start(ropeb[:, :, :, :], a["rope"]).then_inc(s["ld_wa"], 16)
            sp.dma_start(masks[:, :, :], a["masks"]).then_inc(s["ld_wa"], 16)
            sp.dma_start(qks[:, :, :, :], a["qks"].to_broadcast([P, 2, 2, DH])).then_inc(s["ld_wa"], 16)
            for l in range(LAYERS):
                if l:
                    sp.wait_ge(s["t_filled"], TF_PER * l)
                sp.dma_start(wqkv[:, :], a["wqkv"][l]).then_inc(s["ld_wq"], 16)
                if l:
                    sp.wait_ge(s["z_ready"], NG * l)
                sp.dma_start(wo[:, :, :], a["wo"][l].rearrange("(c p) n -> p c n", p=P)).then_inc(s["ld_wl"], 16)
                sp.dma_start(w1[:, :], a["w1"][l]).then_inc(s["ld_wl"], 16)
                sp.dma_start(w2[:, 0:2, :], a["w2"][l, 0:256, :].rearrange("(c p) n -> p c n", p=P)).then_inc(s["ld_wl"], 16)
                sp.dma_start(w2[0:HID - 256, 2, :], a["w2"][l, 256:HID, :]).then_inc(s["ld_wl"], 16)
                if l == 0:
                    sp.wait_ge(s["x_mixed"], NG)
                    sp.dma_start(ew1, a["ew1"]).then_inc(s["ld_ew"], 16)
                    sp.dma_start(ew2, a["ew2"]).then_inc(s["ld_ew"], 16)
            outr = out.rearrange("b t d -> (b t) d").rearrange("(n p) d -> p n d", p=P)
            for g in range(NG):
                sp.wait_ge(s["out_ready"], TPG * (g + 1))
                sp.dma_start(outr[:, g * TPG:(g + 1) * TPG, :], big[:, 4, gsl(g)].rearrange("p (n d) -> p n d", n=TPG)).then_inc(s["st_out"], 16)
            sp.wait_ge(s["st_out"], 16 * NG)

        @block.scalar
        def _(act):
            act.dma_start(ident[:, :], a["ident"]).then_inc(s["ld_c"], 16)
            act.dma_start(vec[:, :], a["vec"]).then_inc(s["ld_c"], 16)
            act.dma_start(wmod[:, :, :], a["wmod"]).then_inc(s["ld_c"], 16)
            act.dma_start(identb[:, :], a["identb"]).then_inc(s["ld_c"], 16)
            act.dma_start(tvec, a["tvec"].to_broadcast([P, T])).then_inc(s["ld_lru"], 16)
            act.dma_start(wlru[:, :, :], a["wlru"]).then_inc(s["ld_lru"], 16)
            for dst, name in ((wsh[:, :, :], "wsh"), (wsh2[:, :, :], "wsh2"), (wrt[:, :], "wrt"),
                              (before[:, :, :], "before")):
                act.dma_start(dst, a[name]).then_inc(s["ld_moe"], 16)
            act.dma_start(rbias[:, :], a["rbias"].to_broadcast([P, NE])).then_inc(s["ld_moe"], 16)
            own = Steps(act, s["act_own"])

            act.wait_ge(s["ld_c"], 64)
            act.activation(silc[:, :], vec[:, V_C:V_C + 4], ACT.Silu).then_inc(s["silu_c"], 1)

            def ln_out(n, dst, scale, bias):
                act.wait_ge(s["ln_t2"], n + 1)
                act.activation(dst, psT1[:, :], ACT.Identity, bias=bias, scale=scale).then_inc(s["ln_out"], 1)

            for g in range(NG):
                act.wait_ge(s["xT_fill"], g + 1)
                act.activation(x_cm[:, gsl(g)], psT0[:, :], ACT.Copy).then_inc(s["xT_evac"], 1)
                if g == 0:
                    act.wait_ge(s["mod_sc"], 1)
                b = bof(g)
                ln_out(ln_no(0, g), hsA[:, gsl(g)], mod[:, 0, CA, b:b + 1], mod[:, 0, SA, b:b + 1])
                act.wait_ge(s["kv_mm"], 2 * g + 1)
                own.one(act.activation(ek[:, gsl(g)], psS[:, g % 2, :], ACT.Exp, bias=vec[:, V_BK:V_BK + 1]))
                act.activation(ek[:, gsl(g)], ek[:, gsl(g)], ACT.Identity, bias=0.0, scale=sc[:, 1:2]).then_inc(s["ek_ready"], 1)
                act.wait_ge(s["ek_ready"], g + 1)
                act.activation(gek[:, gsl(g)], ek[:, gsl(g)], ACT.Identity, bias=sc[:, 3:4], scale=sc[:, 2:3]).then_inc(s["gek_ready"], 1)
            for g in range(NG):
                act.wait_ge(s["r_mm"], g + 1)
                act.activation(rsg[:, gsl(g)], psQK[:, g % 2, :], ACT.Sigmoid, bias=vec[:, V_BR:V_BR + 1]).then_inc(s["r_ready"], 1)

            for g in range(NG):
                b = bof(g)
                ln_out(ln_no(1, g), z[:, gsl(g)], mod[:, 0, CB, b:b + 1], mod[:, 0, SB, b:b + 1])

            def squares(n, part):
                act.wait_ge(s["qk_mm"], 2 * n + part + 1)
                act.activation(sq[:, part * INNER:(part + 1) * INNER], psQK[:, part, :], ACT.Square).then_inc(s["sq_done"], 1)

            def evac(dst, src):
                act.activation(dst, src, ACT.Copy).then_inc(s["t_evac"], 1)

            def attn_body(l, i, has_next):
                n = l * NT + i
                f = l * TF_PER + 1 + 6 * i
                act.wait_ge(s["t_filled"], f + 1)
                qv = psT1[:, :].rearrange("p (c t) -> p c t", c=4)
                qd = qTp[:, :, :].rearrange("p (c e) t -> p c e t", e=2)
                evac(qd[0:64, :, 0, :], qv[0:64])
                evac(qd[64:128, :, 1, :], qv[64:128])
                act.wait_ge(s["t_filled"], f + 2)
                act.wait_ge(s["kprev"], n + 1)
                evac(kTb[:, :, W:W + P], psT0[:, :].rearrange("p (c t) -> p c t", c=4))
                for hb in range(2):
                    act.wait_ge(s["negmax"], 2 * n + hb + 1)
                    for h in range(4 * hb, 4 * hb + 4):
                        act.activation(prob[:, h, :], psS[:, hb, (h % 4) * P:(h % 4 + 1) * P], ACT.Exp,
                                       bias=nmx[:, h:h + 1]).then_inc(s["p_ready"], 1)
                    if has_next:
                        squares(n + 1, hb)
                act.wait_ge(s["t_filled"], f + 3)
                evac(pT[:, 0:4, :], psT1[:, :].rearrange("p (c t) -> p c t", c=4))
                act.wait_ge(s["t_filled"], f + 4)
                evac(pT[:, 4:8, :], psT0[:, :].rearrange("p (c t) -> p c t", c=4))
                if has_next:
                    act.wait_ge(s["t_filled"], f + 5)
                    act.wait_ge(s["va_prev"], n + 2)
                    evac(vB[:, :, 0:DH], psT1[:, :].rearrange("p (h d) -> p h d", h=H))
                act.wait_ge(s["t_filled"], f + (6 if has_next else 5))
                evac(oT[:, :, bass.ds(i * P, P)], psT0[:, :].rearrange("p (c t) -> p c t", c=4))

            def mlp_act(l, g):
                n = ln_no(2 + l, g)
                ln_out(n, hn[:, g % 2, :], vec[:, V_LNG + l:V_LNG + l + 1], vec[:, V_LNB + l:V_LNB + l + 1])
                for j, (o, m) in enumerate(HCH):
                    k = (l * NG + g) * 3 + j
                    act.wait_ge(s["g_mm"], k + 1)
                    if k >= 2:
                        act.wait_ge(s["hg_done"], k - 1)
                    c = V_B1 + 6 * l + 3 + j
                    act.activation(gel[0:m, k % 2, :], psS[0:m, k % 2, :], ACT.Gelu, bias=vec[0:m, c:c + 1]).then_inc(s["gelu_done"], 1)

            for l in range(LAYERS):
                squares(l * NT, 0)
                squares(l * NT, 1)
                act.wait_ge(s["t_filled"], l * TF_PER + 1)
                act.wait_ge(s["va_prev"], l * NT + 1)
                evac(vB[:, :, 0:DH], psT1[:, :].rearrange("p (h d) -> p h d", h=H))
                evac(zero[:, :], vec[:, V_BR:V_BR + 1])
                with act.Fori(0, NT - 1) as i:
                    attn_body(l, i, True)
                attn_body(l, NT - 1, False)
                for g in range(NG):
                    mlp_act(l, g)

            act.wait_ge(s["tabs_phase"], 1)
            act.activation(tcos, tcos, ACT.Sin, scale=TWO_PI).then_inc(s["tabs_ready"], 1)
            act.activation(tsin[:, :], tsin[:, :], ACT.Sin, scale=sc[:, 8:9]).then_inc(s["tabs_ready"], 1)
            for g in range(NG):
                b = bof(g)
                ln_out(ln_no(4, g), hn[:, g % 2, :], mod[:, 1, CA, b:b + 1], mod[:, 1, SA, b:b + 1])

            for g in range(NG):
                b = bof(g)
                ln_out(ln_no(5, g), hsA[:, gsl(g)], mod[:, 1, CB, b:b + 1], mod[:, 1, SB, b:b + 1])
            act.wait_ge(s["rt_mm"], 1)
            act.activation(sq[:, 0:P], psT0[:, 0:P], ACT.Sigmoid).then_inc(s["sig_done"], 1)
            for g in range(NG):
                for j in range(2):
                    k = 2 * g + j
                    act.wait_ge(s["sh_mm"], 2 * k + 1)
                    if k >= 2:
                        act.wait_ge(s["sh_h"], k - 1)
                    act.activation(gel[:, k % 2, :], psS[:, k % 2, :], ACT.Silu).then_inc(s["sh_act"], 1)
            for g in range(NG):
                for e in range(NE):
                    k = g * NE + e
                    act.wait_ge(s["eh_mm"], k + 1)
                    if k >= 2:
                        act.wait_ge(s["ey_done"], NG + k - 1)
                    else:
                        act.wait_ge(s["sh_h"], 2 * NG)
                    act.activation(gel[:, k % 2, :], psQK[:, k % 2, :], ACT.Gelu).then_inc(s["eh_act"], 1)

        @block.gpsimd
        def _(pool):
            own = Steps(pool, s["pool_own"])
            pool.memset(zeros[:, :], 0.0).then_inc(s["init"], 1)
            pool.memset(half[:, :], -0.5).then_inc(s["init"], 1)
            pool.memset(kTb[:, :, :], 0.0).then_inc(s["init"], 1)
            pool.memset(qTp[:, :, :], 0.0).then_inc(s["init"], 1)
            pool.memset(vA[:, :, :], 1.0).then_inc(s["init"], 1)
            pool.memset(vB[:, :, :], 1.0).then_inc(s["init"], 1)
            pool.wait_ge(s["init"], 6)

            def copy(dst, src):
                return pool.tensor_scalar(dst, src, 1.0, 0.0, ALU.mult, ALU.add)

            def alone(k):
                pool.tensor_tensor(zeros2[:, k:k + 1], zeros[:, 0:1], zeros[:, 1:2], ALU.add)

            def ln_rstd(n):
                pool.wait_ge(s["ln_var"], n + 1)
                pool.tensor_tensor(rst[:, :], mv[:, :, 1], half[:, 0:TPG], ALU.pow).then_inc(s["ln_rstd"], 1)

            def rope_tables(l):
                for b in range(B):
                    for c in range(4):
                        dst = rope[:, b * 8:(b + 1) * 8, c, :]
                        src = ropeb[:, :, c, :]
                        scl = qks[:, l, c // 2, :]
                        if c % 2 == 0:
                            i = pool.tensor_tensor(dst, src, scl.unsqueeze(1).to_broadcast([P, 8, DH]), ALU.mult)
                        else:
                            r = scl.rearrange("p (a d) -> p a d", a=2)[:, ::-1, :]
                            i = pool.tensor_tensor(dst.rearrange("p n (a d) -> p n a d", a=2),
                                                   src.rearrange("p n (a d) -> p n a d", a=2),
                                                   r.unsqueeze(1).to_broadcast([P, 8, 2, DH // 2]), ALU.mult)
                        i.then_inc(s["rope_ready"], 1)

            pool.wait_ge(s["ld_c"], 64)
            own.one(pool.memset(fr[:, 0:1], float(np.e)))
            for dst, src in ((4, V_NU), (5, V_TH), (6, V_GAM)):
                own.did(pool.tensor_tensor(sc[:, dst:dst + 1], fr[:, 0:1], vec[:, src:src + 1], ALU.pow))
            own.did(pool.tensor_tensor(sc[:, 0:1], fr[:, 0:1], vec[:, V_BTD:V_BTD + 1], ALU.pow))
            own.did(pool.tensor_tensor(sc[:, 2:3], fr[:, 0:1], vec[:, V_GD:V_GD + 1], ALU.pow))
            own.one(pool.tensor_scalar(fr[:, 1:2], vec[:, V_BTD:V_BTD + 1], 0.0, -T / 2, ALU.max, ALU.mult))
            own.one(pool.tensor_tensor(sc[:, 1:2], fr[:, 0:1], fr[:, 1:2], ALU.pow))
            own.did(pool.tensor_scalar(sc[:, 3:4], sc[:, 1:2], 1e-6, 0.0, ALU.mult, ALU.add))
            own.one(pool.tensor_scalar(fr[:, 2:3], sc[:, 4:5], -1.0, 0.0, ALU.mult, ALU.add))
            own.one(pool.tensor_tensor(sc[:, 7:8], fr[:, 0:1], fr[:, 2:3], ALU.pow))
            pool.wait_ge(s["mod_fin"], 1)
            copy(fr[:, 3:4], sc[:, 7:8]).then_inc(s["mod_sc"], 1)
            for g in range(NG):
                ln_rstd(ln_no(0, g))
                pool.wait_ge(s["gek_ready"], g + 1)
                pool.wait_ge(s["sb_ready"], g + 1)
                pool.tensor_tensor(gek[:, gsl(g)], gek[:, gsl(g)], sbb[:, gsl(g)], ALU.add).then_inc(s["den_ready"], 1)
            pool.wait_ge(s["ld_wa"], 64)
            rope_tables(0)
            pool.wait_ge(s["ld_lru"], 32)
            C1 = 1.0 / (2 * np.pi)
            CH = float(np.round(C1 * 4096 * 4) / (4096 * 4))
            CL = C1 - CH
            MAGIC = 1.5 * 2 ** 23
            th = sc[:, 5:6]

            def ts(dst, src, s1, s2, o0, o1):
                own.one(pool.tensor_scalar(dst, src, s1, s2, o0, o1))

            def tt(dst, x0, x1, op):
                own.one(pool.tensor_tensor(dst, x0, x1, op))

            c = lambda i: fr[:, i:i + 1]
            ts(sc[:, 8:9], vec[:, V_SGN:V_SGN + 1], TWO_PI, 0.0, ALU.mult, ALU.add)
            ts(c(4), th, 4097.0, 0.0, ALU.mult, ALU.add)
            tt(c(5), c(4), th, ALU.subtract)
            tt(c(4), c(4), c(5), ALU.subtract)
            tt(c(5), th, c(4), ALU.subtract)
            ts(c(6), c(4), CH, 0.0, ALU.mult, ALU.add)
            ts(c(7), c(4), CL, 0.0, ALU.mult, ALU.add)
            ts(c(8), c(5), C1, 0.0, ALU.mult, ALU.add)
            tt(c(7), c(7), c(8), ALU.add)
            ts(c(8), c(6), 4096.0, MAGIC, ALU.mult, ALU.add)
            ts(c(8), c(8), -MAGIC, 1.0 / 4096, ALU.add, ALU.mult)
            tt(c(6), c(6), c(8), ALU.subtract)
            tt(c(9), c(6), c(7), ALU.add)
            ts(tcos[:, :], tvec, c(8), 0.0, ALU.mult, ALU.add)
            ts(tsin[:, :], tcos[:, :], MAGIC, -MAGIC, ALU.add, ALU.add)
            tt(tcos[:, :], tcos[:, :], tsin[:, :], ALU.subtract)
            ts(tsin[:, :], tvec, c(9), 0.0, ALU.mult, ALU.add)
            tt(tsin[:, :], tcos[:, :], tsin[:, :], ALU.add)
            ts(tcos[:, :], tsin[:, :], MAGIC, -MAGIC, ALU.add, ALU.add)
            tt(tsin[:, :], tsin[:, :], tcos[:, :], ALU.subtract)
            ts(tcos[:, :], tsin[:, :], 1.0, 0.25, ALU.mult, ALU.add)
            ts(tvec, tcos[:, :], MAGIC, -MAGIC, ALU.add, ALU.add)
            pool.tensor_tensor(tcos[:, :], tcos[:, :], tvec, ALU.subtract).then_inc(s["tabs_phase"], 1)
            ts(c(10), sc[:, 6:7], vec[:, V_SGN:V_SGN + 1], 1.0, ALU.mult, ALU.mult)
            ts(c(11), c(10), -1.0, 0.0, ALU.mult, ALU.add)
            ts(wcs[:, 0, :], wlru[:, 2, :], c(10), 0.0, ALU.mult, ALU.add)
            ts(wcs[:, 1, :], wlru[:, 3, :], c(11), 0.0, ALU.mult, ALU.add)
            for g in range(NG):
                ln_rstd(ln_no(1, g))

            def stage(l, i):
                if i is not None:
                    pool.wait_ge(s["t_filled"], l * TF_PER + 1 + 6 * i)
                alone(1)
                pool.tensor_tensor(hst[:, :], hsA[:, bass.ds((i + 1) * P if i is not None else 0, P)], zeros[:, :],
                                   ALU.add).then_inc(s["staged"], 1)

            def rope_sum(n):
                for part in range(2):
                    r = slice(part * INNER, (part + 1) * INNER)
                    pool.wait_ge(s["rope_ab"], 4 * n + 2 * part + 2)
                    pool.tensor_tensor(ra[:, r], ra[:, r], rb[:, r], ALU.add).then_inc(s["rope_c"], 1)
                pool.wait_ge(s["rope_c"], 2 * n + 2)
                pool.wait_ge(s["rn_ready"], n + 1)
                pool.tensor_tensor(qkn[:, INNER:].rearrange("p (h d) -> p h d", h=H),
                                   ra[:, INNER:].rearrange("p (h d) -> p h d", h=H),
                                   nw[:, 0, 8:16].unsqueeze(2).to_broadcast([P, H, DH]), ALU.mult).then_inc(s["k_ready"], 1)

            def shift_copy(dst, src, nil):
                return pool.tensor_tensor(dst, src, nil.unsqueeze(2).to_broadcast([64, H, DH + 1]), ALU.add)

            def pool_body(l, i, has_next):
                n = l * NT + i
                pool.wait_ge(s["va_cur"], n + 1)
                pool.wait_ge(s["s_done"], 2 * n)
                alone(0)
                copy(kTb[:, :, 0:W], kTb[:, :, P:P + W]).then_inc(s["kprev"], 1)
                if has_next:
                    stage(l, i)
                    rope_sum(n + 1)
                    pool.wait_ge(s["pv_done"], n + 1)
                    pool.wait_ge(s["k_ready"], n + 2)
                    shift_copy(vA[0:64, :, :], vB[64:128, :, :], zeros[64:128, 0:1]).then_inc(s["va_prev"], 1)
                    pool.wait_ge(s["t_evac"], l * TE_PER + 2 + 7 * i + 6)
                    pool.wait_ge(s["va_prev"], n + 2)
                    shift_copy(vA[64:128, :, :], vB[0:64, :, :], zeros[0:64, 0:1]).then_inc(s["va_cur"], 1)

            for l in range(LAYERS):
                pool.wait_ge(s["hsA_ready"], 2 * NG * (l + 1))
                stage(l, None)
                rope_sum(l * NT)
                if l:
                    pool.wait_ge(s["pv_done"], l * NT)
                pool.wait_ge(s["k_ready"], l * NT + 1)
                shift_copy(vA[0:64, :, :], vB[64:128, :, :], zeros[64:128, 0:1]).then_inc(s["va_prev"], 1)
                pool.wait_ge(s["t_evac"], l * TE_PER + 1)
                pool.wait_ge(s["va_prev"], l * NT + 1)
                shift_copy(vA[64:128, :, :], vB[0:64, :, :], zeros[0:64, 0:1]).then_inc(s["va_cur"], 1)
                with pool.Fori(0, NT - 1) as i:
                    pool_body(l, i, True)
                pool_body(l, NT - 1, False)
                if l + 1 < LAYERS:
                    pool.wait_ge(s["t_filled"], TF_PER * (l + 1))
                    rope_tables(l + 1)
                for g in range(NG):
                    ln_rstd(ln_no(2 + l, g))

            for g in range(NG):
                ln_rstd(ln_no(4, g))
                t = slice((g % GPB) * GW, (g % GPB + 1) * GW)
                pool.wait_ge(s["bu_half"], 2 * g + 2)
                pool.tensor_tensor(ra[:, 0:GW], ra[:, 0:GW], rb[:, 0:GW], ALU.add).then_inc(s["lru_a"], 1)
                pool.wait_ge(s["lru_g"], g + 1)
                if g:
                    pool.wait_ge(s["y_done"], g)
                pool.tensor_tensor(hg[:, 1, :], z[:, gsl(g)], tsin[:, t], ALU.mult).then_inc(s["lru_m2"], 1)
            for g in range(NG):
                ln_rstd(ln_no(5, g))

        @block.vector
        def _(dve):
            own = Steps(dve, s["dve"])
            own.one(dve.memset(ph[:, :, :], 0.0))
            own.one(dve.memset(cnt[:, :], 0.0))
            dve.wait_ge(s["ld_c"], 64)
            dve.wait_ge(s["mod_mm"], 1)
            own.one(dve.tensor_copy(mod[:, :, :, :], psT1[:, 0:24].rearrange("p (b k n) -> p b k n", b=2, k=6)))
            for k in (CA, CB):
                own.did(dve.tensor_scalar(mod[:, :, k, :], mod[:, :, k, :], 1.0, None, ALU.add))
            for k in (GA, GB):
                gk = mod[:, :, k, :]
                own.one(dve.tensor_scalar(modt[:, 0, :, 0:2], gk, 0.0, 2.0, ALU.is_ge, ALU.mult))
                own.did(dve.tensor_scalar(modt[:, 0, :, 2:4], modt[:, 0, :, 0:2], -1.0, None, ALU.add))
                own.one(dve.scalar_tensor_tensor(out=modt[:, 1, :, 0:2], in0=gk, scalar=-1.0, in1=gk, op0=ALU.mult, op1=ALU.max))
                own.one(dve.scalar_tensor_tensor(out=gk, in0=modt[:, 1, :, 0:2], scalar=0.25, in1=modt[:, 0, :, 2:4],
                                                 op0=ALU.max, op1=ALU.mult))
            own.sync()
            dve.tensor_copy(modt[:, 0, 0, 0:1], mod[:, 0, 0, 0:1]).then_inc(s["mod_fin"], 1)

            def ln_stats(n, src):
                for k in range(TPG):
                    own.did(dve.bn_stats(st6[:, k, :], src[:, k, :]))
                own.sync()
                for k in range(TPG):
                    own.did(dve.bn_aggr(mv[:, k, :], st6[:, k, :]))
                own.sync()
                dve.tensor_scalar(mv[:, :, 1], mv[:, :, 1], EPS, None, ALU.add).then_inc(s["ln_var"], 1)

            def ln_norm(n, src):
                dve.wait_ge(s["ln_rstd"], n + 1)
                if n:
                    dve.wait_ge(s["ln_t2"], n)
                for k in range(TPG):
                    dve.tensor_scalar(lnx[:, k, :], src[:, k, :], mv[:, k, 0:1], rst[:, k:k + 1],
                                      ALU.subtract, ALU.mult).then_inc(s["ln_norm"], 1)

            def ln(n):
                src = psT0[:, :].rearrange("p (n d) -> p n d", n=TPG)
                dve.wait_ge(s["ln_t1"], n - NG + 1)
                ln_stats(n, src)
                ln_norm(n, src)

            for g in range(NG):
                n = ln_no(0, g)
                dve.wait_ge(s["ld_x"], 16 * NG)
                src = xt[:, g * TPG:(g + 1) * TPG, :]
                ln_stats(n, src)
                ln_norm(n, src)
                c = gsl(g)
                dve.wait_ge(s["kv_mm"], 2 * g + 2)
                dve.wait_ge(s["ek_ready"], g + 1)
                dve.scalar_tensor_tensor(out=ekv[:, c], in0=psO[:, g % 2, :], scalar=vec[:, V_BV:V_BV + 1],
                                         in1=ek[:, c], op0=ALU.add, op1=ALU.mult).then_inc(s["ekv_ready"], 1)
                dve.wait_ge(s["ekv_ready"], g + 1)
                td = sc[:, 0:1].to_broadcast([P, GW])
                last = g * GW - 1
                first = g % GPB == 0
                dve.tensor_tensor_scan(sbb[:, c], td, ek[:, c], 0.0 if first else sbb[:, last:last + 1],
                                       ALU.mult, ALU.add).then_inc(s["sb_ready"], 1)
                own.did(dve.tensor_tensor_scan(sab[:, c], td, ekv[:, c], 0.0 if first else sab[:, last:last + 1],
                                               ALU.mult, ALU.add))
                own.sync()
                own.one(dve.scalar_tensor_tensor(out=sab[:, c], in0=ekv[:, c], scalar=sc[:, 2:3], in1=sab[:, c],
                                                 op0=ALU.mult, op1=ALU.add) if False else
                        dve.scalar_tensor_tensor(out=ekv[:, c], in0=ekv[:, c], scalar=sc[:, 2:3], in1=sab[:, c],
                                                 op0=ALU.mult, op1=ALU.add))
                dve.wait_ge(s["den_ready"], g + 1)
                own.one(dve.reciprocal(gek[:, c], gek[:, c]))
                own.did(dve.tensor_tensor(ekv[:, c], ekv[:, c], gek[:, c], ALU.mult))
            own.sync()
            for g in range(NG):
                c = gsl(g)
                dve.wait_ge(s["r_ready"], g + 1)
                own.did(dve.scalar_tensor_tensor(out=ekv[:, c], in0=ekv[:, c], scalar=20.0, in1=rsg[:, c],
                                                 op0=ALU.mult, op1=ALU.mult))
            own.sync()

            cur = ekv.rearrange("p (b c j) -> p b c j", b=B, c=NCH)

            def at(j):
                return ph[:, :, j:j + SEQ * (NCH - 1) + 1:SEQ]

            def membrane_pass(steps):
                for j in range(SEQ):
                    steps.one(dve.scalar_tensor_tensor(out=vst[:, :, :], in0=at(j), scalar=-0.3, in1=cur[:, :, :, j],
                                                       op0=ALU.mult, op1=ALU.add))
                    steps.one(dve.scalar_tensor_tensor(out=at(j + 1), in0=at(j), scalar=-1.0, in1=vst[:, :, :],
                                                       op0=ALU.is_lt, op1=ALU.subtract))

            with dve.Fori(0, PASSES - 1) as k:
                own.enter(k, 2 * SEQ)
                membrane_pass(own)
            own.leave(PASSES - 1)
            own.one(dve.tensor_copy(cend[:, :, :], at(0)))
            membrane_pass(own)
            own.one(dve.tensor_tensor(cend[:, :, :], cend[:, :, :], at(0), ALU.not_equal))
            own.one(dve.tensor_reduce(cnt[:, 0:1], cend[:, :, :], AX.XY, ALU.add))
            own.one(dve.transpose(cntT[:, :], cnt[:, :]))
            for q in range(4):
                own.did(dve.tensor_reduce(cntf[0:1, q:q + 1], cntT[32 * q:32 * q + 1, :], AX.X, ALU.add))
            own.sync()
            own.one(dve.tensor_reduce(cntf[0:1, 4:5], cntf[0:1, 0:4], AX.X, ALU.add))
            own.one(dve.tensor_copy(cnti[0:1, 0:1], cntf[0:1, 4:5]))
            changed = dve.value_load(cnti[0:1, 0:1], min_val=0, max_val=P * B * NCH)
            with dve.If(changed != 0):
                again = Steps(dve, s["fallback"])
                with dve.Fori(0, NCH) as k:
                    again.enter(k, 2 * SEQ)
                    membrane_pass(again)
                again.leave(NCH)
            for g in range(NG):
                b, o = bof(g), (g % GPB) * GW
                own.did(dve.tensor_scalar(ekv[:, gsl(g)], ph[:, b, 1 + o:1 + o + GW], -1.0, mod[:, 0, GA, b:b + 1],
                                          ALU.is_lt, ALU.mult))
            own.sync()
            for g in range(NG):
                dve.wait_ge(s["xT_evac"], g + 1)
                dve.tensor_tensor(x_cm[:, gsl(g)], x_cm[:, gsl(g)], ekv[:, gsl(g)], ALU.add).then_inc(s["x_mixed"], 1)
            dve.wait_ge(s["x_mixed"], NG)

            def shifted(dst, src, g, name):
                o = g * GW
                dve.tensor_copy(dst[0:64, o:o + GW], src[0:64, o:o + GW]).then_inc(s[name], 1)
                w = GW - (g % GPB == GPB - 1)
                dve.tensor_copy(dst[64:128, o + 1:o + 1 + w], src[64:128, o:o + w]).then_inc(s[name], 1)

            own.did(dve.memset(hsA[64:128, T:T + 1], 0.0))
            own.did(dve.memset(hsA[64:128, 0:1], 0.0))
            own.did(dve.memset(hsM[64:128, T:T + 1], 0.0))
            own.did(dve.memset(hsM[64:128, 0:1], 0.0))
            own.sync()
            for g in range(NG):
                ln(ln_no(1, g))
                dve.wait_ge(s["ln_out"], ln_no(1, g) + 1)
                shifted(hsA, z, g, "hsA_ready")

            def rope_and_norm(n, slot):
                for part in range(2):
                    r = slice(part * INNER, (part + 1) * INNER)
                    dve.wait_ge(s["sq_done"], 2 * n + part + 1)
                    if part == 0:
                        dve.wait_ge(s["k_ready"], n)
                    dve.tensor_tensor(ra[:, r].rearrange("p (h d) -> p h d", h=H),
                                      psQK[:, part, :].rearrange("p (h d) -> p h d", h=H),
                                      rope[:, slot, 2 * part, :].unsqueeze(1).to_broadcast([P, H, DH]),
                                      ALU.mult).then_inc(s["rope_ab"], 1)
                    dve.tensor_tensor(rb[:, r].rearrange("p (h a d) -> p h a d", h=H, a=2),
                                      psQK[:, part, :].rearrange("p (h a d) -> p h a d", h=H, a=2)[:, :, ::-1, :],
                                      rope[:, slot, 2 * part + 1, :].rearrange("p (a d) -> p a d", a=2).unsqueeze(1)
                                      .to_broadcast([P, H, 2, DH // 2]), ALU.mult).then_inc(s["rope_ab"], 1)
                for part in range(2):
                    own.did(dve.tensor_reduce(nw[:, 1, 8 * part:8 * part + 8],
                                              sq[:, part * INNER:(part + 1) * INNER].rearrange("p (h d) -> p h d", h=H),
                                              AX.X, ALU.add))
                own.sync()
                own.one(dve.tensor_scalar(nw[:, 1, :], nw[:, 1, :], 1e-24, None, ALU.max))
                own.did(dve.tensor_scalar(nwi[:, :], nw[:, 1, :].bitcast(I32), 1, None, ALU.logical_shift_right))
                own.did(dve.tensor_scalar(nw[:, 3, :], nw[:, 1, :], -0.5, None, ALU.mult))
                own.sync()
                own.one(dve.tensor_scalar(nw[:, 2, :].bitcast(I32), nwi[:, :], -1.0, float(0x5F3759DF), ALU.mult, ALU.add))
                y = nw[:, 2, :]
                for k in range(UNR):
                    own.one(dve.tensor_tensor(nw[:, 1, :], y, y, ALU.mult))
                    own.one(dve.tensor_tensor(nw[:, 1, :], nw[:, 1, :], nw[:, 3, :], ALU.mult))
                    last = k == UNR - 1
                    dst = nw[:, 0, :] if last else y
                    i = dve.scalar_tensor_tensor(out=dst, in0=nw[:, 1, :], scalar=1.5, in1=y, op0=ALU.add, op1=ALU.mult)
                    if last:
                        i.then_inc(s["rn_ready"], 1)
                    else:
                        own.one(i)
                dve.wait_ge(s["rn_ready"], n + 1)
                dve.wait_ge(s["rope_c"], 2 * n + 1)
                dve.tensor_tensor(qkn[:, 0:INNER].rearrange("p (h d) -> p h d", h=H),
                                  ra[:, 0:INNER].rearrange("p (h d) -> p h d", h=H),
                                  nw[:, 0, 0:8].unsqueeze(2).to_broadcast([P, H, DH]), ALU.mult).then_inc(s["q_ready"], 1)

            ROPE_STEPS = 2 + 1 + 2 + 1 + 3 * UNR - 1
            BODY_STEPS = ROPE_STEPS + 1

            def attn_body(l, i, has_next):
                n = l * NT + i
                for hb in range(2):
                    dve.wait_ge(s["s_done"], 2 * n + hb + 1)
                    dve.tensor_reduce(nmx[:, 4 * hb:4 * hb + 4], psS[:, hb, :].rearrange("p (h k) -> p h k", h=4),
                                      AX.X, ALU.max, negate=True).then_inc(s["negmax"], 1)
                if has_next:
                    rope_and_norm(n + 1, i + 1)
                ov = psO[:, :, 0:4 * (DH + 1)].rearrange("p b (h d) -> p b h d", h=4)
                dve.wait_ge(s["pv_done"], n + 1)
                own.one(dve.reciprocal(orc[:, :].rearrange("p (b h) -> p b h", b=2), ov[:, :, :, DH]))
                dve.tensor_tensor(osb[:, :].rearrange("p (b h d) -> p b h d", b=2, h=4), ov[:, :, :, 0:DH],
                                  orc[:, :].rearrange("p (b h) -> p b h", b=2).unsqueeze(3).to_broadcast([P, 2, 4, DH]),
                                  ALU.mult).then_inc(s["o_norm"], 1)

            for l in range(LAYERS):
                dve.wait_ge(s["rope_ready"], 8 * (l + 1))
                rope_and_norm(l * NT, 0)
                with dve.Fori(0, NT - 1) as i:
                    own.enter(i, BODY_STEPS)
                    attn_body(l, i, True)
                own.leave(NT - 1)
                attn_body(l, NT - 1, False)

                def mid(g):
                    n = l * NG + g
                    dve.wait_ge(s["wo_done"], n + 1)
                    dve.tensor_tensor(z[:, gsl(g)], z[:, gsl(g)], psQK[:, g % 2, :], ALU.add).then_inc(s["zmid"], 1)
                    dve.wait_ge(s["zmid"], n + 1)
                    shifted(hsM, z, g, "hsM_ready")

                mid(0)
                for g in range(NG):
                    n = l * NG + g
                    ln(ln_no(2 + l, g))
                    if g + 1 < NG:
                        mid(g + 1)
                    for j, (o, m) in enumerate(HCH):
                        k = n * 3 + j
                        dve.wait_ge(s["gelu_done"], k + 1)
                        dve.wait_ge(s["a_mm"], k + 1)
                        if n:
                            dve.wait_ge(s["w2_done"], n)
                        c = V_B1 + 6 * l + j
                        dve.scalar_tensor_tensor(out=hg[0:m, j, :], in0=psO[0:m, k % 2, :], scalar=vec[0:m, c:c + 1],
                                                 in1=gel[0:m, k % 2, :], op0=ALU.add, op1=ALU.mult).then_inc(s["hg_done"], 1)
                    dve.wait_ge(s["w2_done"], n + 1)
                    dve.scalar_tensor_tensor(out=z[:, gsl(g)], in0=psQK[:, g % 2, :], scalar=vec[:, V_B2 + l:V_B2 + l + 1],
                                             in1=z[:, gsl(g)], op0=ALU.add, op1=ALU.add).then_inc(s["z_ready"], 1)
                    dve.wait_ge(s["z_ready"], n + 1)
                    if l + 1 < LAYERS:
                        shifted(hsA, z, g, "hsA_ready")
                    else:
                        b = bof(g)
                        dve.scalar_tensor_tensor(out=x_cm[:, gsl(g)], in0=z[:, gsl(g)], scalar=mod[:, 0, GB, b:b + 1],
                                                 in1=x_cm[:, gsl(g)], op0=ALU.mult, op1=ALU.add).then_inc(s["x_mixed"], 1)

            dve.wait_ge(s["x_mixed"], 2 * NG)
            for g in range(NG):
                b = bof(g)
                t = slice((g % GPB) * GW, (g % GPB + 1) * GW)
                ln(ln_no(4, g))
                dve.wait_ge(s["bu_mm"], 2 * g + 1)
                if g == 0:
                    dve.wait_ge(s["tabs_ready"], 2)
                else:
                    dve.wait_ge(s["lru_g"], g)
                dve.tensor_tensor(ra[:, 0:GW], psS[:, g % 2, :], tcos[:, t], ALU.mult).then_inc(s["bu_half"], 1)
                dve.wait_ge(s["bu_mm"], 2 * g + 2)
                dve.tensor_tensor(rb[:, 0:GW], psO[:, g % 2, :], tsin[:, t], ALU.mult).then_inc(s["bu_half"], 1)
                dve.wait_ge(s["lru_a"], g + 1)
                last = g * GW - 1
                dve.tensor_tensor_scan(z[:, gsl(g)], sc[:, 7:8].to_broadcast([P, GW]), ra[:, 0:GW],
                                       0.0 if g % GPB == 0 else z[:, last:last + 1], ALU.mult, ALU.add).then_inc(s["lru_g"], 1)
                dve.wait_ge(s["lru_g"], g + 1)
                if g:
                    dve.wait_ge(s["y_done"], g)
                dve.tensor_tensor(hg[:, 0, :], z[:, gsl(g)], tcos[:, t], ALU.mult).then_inc(s["lru_m1"], 1)
                dve.wait_ge(s["y_done"], g + 1)
                dve.scalar_tensor_tensor(out=x_cm[:, gsl(g)], in0=psQK[:, g % 2, :], scalar=mod[:, 1, GA, b:b + 1],
                                         in1=x_cm[:, gsl(g)], op0=ALU.mult, op1=ALU.add).then_inc(s["xmid_ready"], 1)

            for g in range(NG):
                ln(ln_no(5, g))
            dve.wait_ge(s["sig_done"], 1)
            sg = sq[:, 0:P].rearrange("p (n e) -> p n e", n=NT)
            sel = sq[:, P:2 * P].rearrange("p (n e) -> p n e", n=NT)
            comb = sq[:, 2 * P:3 * P].rearrange("p (n e) -> p n e", n=NT)
            den = sq[:, 3 * P:3 * P + NT]
            big4 = ra[:, :].rearrange("p (n e j) -> p n e j", n=NT, e=NE)
            big5 = rb[:, :].rearrange("p (n e j) -> p n e j", n=NT, e=NE)
            sh4 = [P, NT, NE, NE]
            own.one(dve.tensor_tensor(sel, sg, rbias[:, :].unsqueeze(1).to_broadcast([P, NT, NE]), ALU.add))
            own.did(dve.tensor_tensor(big4, sel.unsqueeze(2).to_broadcast(sh4), sel.unsqueeze(3).to_broadcast(sh4), ALU.is_equal))
            own.one(dve.tensor_tensor(big5, sel.unsqueeze(2).to_broadcast(sh4), sel.unsqueeze(3).to_broadcast(sh4), ALU.is_gt))
            own.one(dve.tensor_tensor(big4, big4, before[:, :, :].unsqueeze(1).to_broadcast(sh4), ALU.mult))
            own.one(dve.tensor_tensor(big4, big4, big5, ALU.add))
            own.one(dve.tensor_reduce(sel, big4, AX.X, ALU.add))
            own.one(dve.tensor_scalar(sel, sel, 1.5, None, ALU.is_lt))
            own.one(dve.tensor_tensor(comb, sel, sg, ALU.mult))
            own.one(dve.tensor_reduce(den, comb, AX.X, ALU.add))
            dn2 = sq[:, 3 * P + NT:3 * P + 2 * NT]
            dn3 = sq[:, 3 * P + 2 * NT:3 * P + 3 * NT]
            own.did(dve.tensor_scalar(dn2, den, 1e-9, None, ALU.is_gt))
            own.one(dve.tensor_scalar(den, den, 1e-9, None, ALU.add))
            own.one(dve.reciprocal(den, den))
            own.one(dve.tensor_tensor(den, den, dn2, ALU.mult))
            own.did(dve.tensor_scalar(dn3, dn2, -0.5, 0.5, ALU.mult, ALU.add))
            own.one(dve.tensor_tensor(comb, comb, den.unsqueeze(2).to_broadcast([P, NT, NE]), ALU.mult))
            own.one(dve.tensor_tensor(sel, sel, dn3.unsqueeze(2).to_broadcast([P, NT, NE]), ALU.mult))
            dve.tensor_tensor(comb, comb, sel, ALU.add).then_inc(s["comb_ready"], 1)
            dve.wait_ge(s["comb_ready"], 1)
            dve.wait_ge(s["gb_mm"], 2)
            own.one(dve.tensor_copy(osb[:, 0:2 * P], psT0[:, 0:2 * P]))
            acc = big[:, 4, :].rearrange("p (n d) -> p n d", n=NT)
            for g in range(NG):
                for j in range(2):
                    k = 2 * g + j
                    dve.wait_ge(s["sh_act"], k + 1)
                    dve.wait_ge(s["sh_mm"], 2 * k + 2)
                    if g:
                        dve.wait_ge(s["ey_done"], g)
                    dve.tensor_tensor(hg[:, j, :], psO[:, k % 2, :], gel[:, k % 2, :], ALU.mult).then_inc(s["sh_h"], 1)
                dve.wait_ge(s["ey_done"], g + 1)
                dve.tensor_copy(big[:, 4, gsl(g)], psT1[:, :]).then_inc(s["ey_used"], 1)
            dve.wait_ge(s["ey_used"], NG)
            for g in range(NG):
                for e in range(NE):
                    k = g * NE + e
                    dve.wait_ge(s["ey_done"], NG + k + 1)
                    yb = (psS, psO)[k % 2]
                    for j in range(TPG):
                        i = dve.scalar_tensor_tensor(out=acc[:, g * TPG + j, :], in0=yb[:, 0, j * P:(j + 1) * P],
                                                     scalar=comb[:, g * TPG + j, e:e + 1], in1=acc[:, g * TPG + j, :],
                                                     op0=ALU.mult, op1=ALU.add)
                        if j == TPG - 1:
                            i.then_inc(s["ey_used"], 1)
                        else:
                            own.did(i)
                    own.sync()
                    dve.wait_ge(s["ey_used"], NG + k + 1)
                own.one(dve.tensor_tensor(acc[:, g * TPG:(g + 1) * TPG, :], acc[:, g * TPG:(g + 1) * TPG, :],
                                          osb[:, bof(g) * P:(bof(g) + 1) * P].unsqueeze(1).to_broadcast([P, TPG, P]), ALU.mult))
                dve.wait_ge(s["fx_t"], g + 1)
                i = dve.tensor_tensor(big[:, 4, gsl(g)], big[:, 4, gsl(g)], psT0[:, :], ALU.add)
                i.then_inc(s["out_ready"], TPG)

        @block.tensor
        def _(pe):
            mm = pe.matmul
            pe.wait_ge(s["ld_c"], 64)
            pe.wait_ge(s["silu_c"], 1)
            for k in range(2):
                for j in range(6):
                    i = mm(psT1[:, (k * 6 + j) * 2:(k * 6 + j) * 2 + 2], wmod[:, k, j * P:(j + 1) * P],
                           silc[:, 2 * k:2 * k + 2], start=True, stop=True)
            i.then_inc(s["mod_mm"], 1)

            def four(dst, src):
                for k in range(TPG):
                    i = pe.transpose(dst[:, k * P:(k + 1) * P], src(k), ident[:, :])
                return i

            def ln_t1(n, src):
                if n > NG:
                    pe.wait_ge(s["ln_norm"], TPG * n)
                four(psT0, lambda k: src[:, k * P:(k + 1) * P]).then_inc(s["ln_t1"], 1)

            def ln_t2(n):
                pe.wait_ge(s["ln_norm"], TPG * (n + 1))
                if n:
                    pe.wait_ge(s["ln_out"], n)
                four(psT1, lambda k: lnx[:, k, :]).then_inc(s["ln_t2"], 1)

            pe.wait_ge(s["ld_x"], 16 * NG)
            pe.wait_ge(s["ld_wa"], 64)
            pe.wait_ge(s["mod_fin"], 1)
            for g in range(NG):
                if g:
                    pe.wait_ge(s["xT_evac"], g)
                four(psT0, lambda k: xt[:, g * TPG + k, :]).then_inc(s["xT_fill"], 1)
                ln_t2(ln_no(0, g))
                pe.wait_ge(s["ln_out"], ln_no(0, g) + 1)
                if g >= 2:
                    pe.wait_ge(s["ek_ready"], g - 1)
                mm(psS[:, g % 2, :], wrkv[:, 1, :], hsA[:, gsl(g)], start=True, stop=True).then_inc(s["kv_mm"], 1)
                if g >= 2:
                    pe.wait_ge(s["ekv_ready"], g - 1)
                mm(psO[:, g % 2, :], wrkv[:, 2, :], hsA[:, gsl(g)], start=True, stop=True).then_inc(s["kv_mm"], 1)
            for g in range(NG):
                if g >= 2:
                    pe.wait_ge(s["r_ready"], g - 1)
                mm(psQK[:, g % 2, :], wrkv[:, 0, :], hsA[:, gsl(g)], start=True, stop=True).then_inc(s["r_mm"], 1)

            pe.wait_ge(s["xT_evac"], NG)
            for g in range(NG):
                pe.wait_ge(s["x_mixed"], g + 1)
                ln_t1(ln_no(1, g), x_cm[:, gsl(g)])
                ln_t2(ln_no(1, g))

            def proj_qk(n):
                pe.wait_ge(s["staged"], n + 1)
                for part in range(2):
                    pe.wait_ge(s["rope_ab"], 4 * n - 4 + 2 * part + 2)
                    pe.wait_ge(s["sq_done"], 2 * n - 2 + part + 1)
                    mm(psQK[:, part, :], hst[:, :], wqkv[:, part * INNER:(part + 1) * INNER], start=True,
                       stop=True).then_inc(s["qk_mm"], 1)

            def proj_v(evacs):
                if evacs is not None:
                    pe.wait_ge(s["t_evac"], evacs)
                i = mm(psT1[:, :], hst[:, :], wqkv[:, 2 * INNER:3 * INNER], start=True, stop=True)
                i.then_inc(s["t_filled"], 1)

            def attn_body(l, i, has_next):
                n = l * NT + i
                e = l * TE_PER + 2 + 7 * i
                pe.wait_ge(s["q_ready"], n + 1)
                pe.wait_ge(s["t_evac"], e - 1)
                four(psT1, lambda k: qkn[:, k * P:(k + 1) * P]).then_inc(s["t_filled"], 1)
                pe.wait_ge(s["k_ready"], n + 1)
                pe.wait_ge(s["t_evac"], e)
                four(psT0, lambda k: qkn[:, INNER + k * P:INNER + (k + 1) * P]).then_inc(s["t_filled"], 1)
                pe.wait_ge(s["t_evac"], e + 3)
                for hb in range(2):
                    mm(psS[:, hb, :], identb[:, :], masks[:, i, :].unsqueeze(1).to_broadcast([P, 4, P]), start=True, stop=False,
                       skip_group_check=True)
                    for h in range(4 * hb, 4 * hb + 4):
                        c = slice((h % 4) * P, (h % 4 + 1) * P)
                        mm(psS[0:64, hb, c], qTp[:, h, 0:64], kTb[:, h // 2, 0:P], start=False, stop=True,
                           skip_group_check=True)
                        j = mm(psS[64:128, hb, c], qTp[:, h, 64:128], kTb[:, h // 2, W:W + P], start=False, stop=True,
                               skip_group_check=True)
                    j.then_inc(s["s_done"], 1)
                if has_next:
                    proj_qk(n + 1)
                pe.wait_ge(s["t_evac"], e + 2)
                pe.wait_ge(s["p_ready"], 8 * n + 4)
                four(psT1, lambda k: prob[:, k, :]).then_inc(s["t_filled"], 1)
                pe.wait_ge(s["p_ready"], 8 * n + 8)
                four(psT0, lambda k: prob[:, 4 + k, :]).then_inc(s["t_filled"], 1)
                pe.wait_ge(s["va_cur"], n + 1)
                pe.wait_ge(s["o_norm"], n)
                pe.wait_ge(s["t_evac"], e + 5)
                for w in range(2):
                    for h in range(H):
                        j = mm(psO[64 * w:64 * w + 64, h // 4, (h % 4) * (DH + 1):(h % 4 + 1) * (DH + 1)],
                               pT[:, h, 64 * w:64 * w + 64], (vA, vB)[w][:, h, :], start=True, stop=True)
                j.then_inc(s["pv_done"], 1)
                if has_next:
                    proj_v(e + 4)
                pe.wait_ge(s["o_norm"], n + 1)
                four(psT0, lambda k: osb[:, k * P:(k + 1) * P]).then_inc(s["t_filled"], 1)

            for l in range(LAYERS):
                pe.wait_ge(s["ld_wq"], 16 * (l + 1))
                proj0 = l * NT
                pe.wait_ge(s["staged"], proj0 + 1)
                if l == 0:
                    pe.wait_ge(s["r_ready"], NG)
                else:
                    pe.wait_ge(s["z_ready"], NG * l)
                for part in range(2):
                    mm(psQK[:, part, :], hst[:, :], wqkv[:, part * INNER:(part + 1) * INNER], start=True,
                       stop=True).then_inc(s["qk_mm"], 1)
                pe.wait_ge(s["ln_out"], ln_no(1 + l, NG - 1) + 1)
                proj_v(None)
                with pe.Fori(0, NT - 1) as i:
                    attn_body(l, i, True)
                attn_body(l, NT - 1, False)

                def out_proj(g):
                    if g >= 2:
                        pe.wait_ge(s["z_ready"], l * NG + g - 1)
                    for c in range(4):
                        i = mm(psQK[:, g % 2, :], wo[:, c, :], oT[:, c, gsl(g)], start=(c == 0), stop=(c == 3))
                    i.then_inc(s["wo_done"], 1)

                pe.wait_ge(s["ld_wl"], 16 * 4 * (l + 1))
                pe.wait_ge(s["t_evac"], TE_PER * (l + 1))
                out_proj(0)
                for g in range(NG):
                    n = l * NG + g
                    pe.wait_ge(s["hsM_ready"], 2 * (n + 1))
                    ln_t1(ln_no(2 + l, g), hsM[:, gsl(g)])
                    if g + 1 < NG:
                        out_proj(g + 1)
                    ln_t2(ln_no(2 + l, g))
                    pe.wait_ge(s["ln_out"], ln_no(2 + l, g) + 1)
                    for j, (o, m) in enumerate(HCH):
                        k = n * 3 + j
                        if k >= 2:
                            pe.wait_ge(s["gelu_done"], k - 1)
                            pe.wait_ge(s["hg_done"], k - 1)
                        mm(psS[0:m, k % 2, :], w1[:, HID + o:HID + o + m], hn[:, g % 2, :], start=True,
                           stop=True).then_inc(s["g_mm"], 1)
                        mm(psO[0:m, k % 2, :], w1[:, o:o + m], hn[:, g % 2, :], start=True, stop=True).then_inc(s["a_mm"], 1)
                    pe.wait_ge(s["zmid"], n + 1)
                    for j, (o, m) in enumerate(HCH):
                        pe.wait_ge(s["hg_done"], 3 * n + j + 1)
                        i = mm(psQK[:, g % 2, :], w2[0:m, j, :], hg[0:m, j, :], start=(j == 0), stop=(j == 2))
                    i.then_inc(s["w2_done"], 1)

            pe.wait_ge(s["ld_lru"], 32)
            for g in range(NG):
                pe.wait_ge(s["x_mixed"], NG + g + 1)
                ln_t1(ln_no(4, g), x_cm[:, gsl(g)])
                ln_t2(ln_no(4, g))
                pe.wait_ge(s["ln_out"], ln_no(4, g) + 1)
                if g == 0:
                    pe.wait_ge(s["gelu_done"], 3 * NG * LAYERS)
                    pe.wait_ge(s["hg_done"], 3 * NG * LAYERS)
                if g >= 2:
                    pe.wait_ge(s["bu_half"], 2 * (g - 1))
                mm(psS[:, g % 2, :], wlru[:, 0, :], hn[:, g % 2, :], start=True, stop=True).then_inc(s["bu_mm"], 1)
                mm(psO[:, g % 2, :], wlru[:, 1, :], hn[:, g % 2, :], start=True, stop=True).then_inc(s["bu_mm"], 1)
                if g >= 2:
                    pe.wait_ge(s["xmid_ready"], g - 1)
                else:
                    pe.wait_ge(s["z_ready"], NG * LAYERS)
                mm(psQK[:, g % 2, :], wlru[:, 4, :], hn[:, g % 2, :], start=True, stop=False)
                pe.wait_ge(s["lru_m1"], g + 1)
                mm(psQK[:, g % 2, :], wcs[:, 0, :], hg[:, 0, :], start=False, stop=False)
                pe.wait_ge(s["lru_m2"], g + 1)
                mm(psQK[:, g % 2, :], wcs[:, 1, :], hg[:, 1, :], start=False, stop=True).then_inc(s["y_done"], 1)

            for g in range(NG):
                pe.wait_ge(s["xmid_ready"], g + 1)
                ln_t1(ln_no(5, g), x_cm[:, gsl(g)])
                ln_t2(ln_no(5, g))
            pe.wait_ge(s["ln_out"], ln_no(5, NG - 1) + 1)
            pe.wait_ge(s["ln_norm"], TPG * NG * 6)
            pe.wait_ge(s["ld_moe"], 16 * 5)
            pe.wait_ge(s["ld_ew"], 32)
            for n in range(NT):
                i = mm(psT0[:, n * NE:(n + 1) * NE], hsA[:, n * P:(n + 1) * P], wrt[:, :], start=True, stop=True)
            i.then_inc(s["rt_mm"], 1)
            pe.wait_ge(s["sig_done"], 1)
            for b in range(B):
                mm(psT0[:, b * P:(b + 1) * P], mod[:, 1, GB, b:b + 1].to_broadcast([P, P]), ident[:, :], start=True,
                   stop=True).then_inc(s["gb_mm"], 1)
            for g in range(NG):
                for j in range(2):
                    k = 2 * g + j
                    if k >= 2:
                        pe.wait_ge(s["sh_act"], k - 1)
                        pe.wait_ge(s["sh_h"], k - 1)
                    mm(psS[:, k % 2, :], wsh[:, 0, j * P:(j + 1) * P], hsA[:, gsl(g)], start=True, stop=True).then_inc(s["sh_mm"], 1)
                    mm(psO[:, k % 2, :], wsh[:, 1, j * P:(j + 1) * P], hsA[:, gsl(g)], start=True, stop=True).then_inc(s["sh_mm"], 1)
                pe.wait_ge(s["sh_h"], 2 * g + 2)
                if g:
                    pe.wait_ge(s["ey_used"], g)
                for n in range(TPG):
                    for j in range(2):
                        i = mm(psT1[:, n * P:(n + 1) * P], hg[:, j, n * P:(n + 1) * P], wsh2[:, j, :], start=(j == 0), stop=(j == 1))
                i.then_inc(s["ey_done"], 1)

            def expert_up(k):
                g, e = divmod(k, NE)
                if k >= 2:
                    pe.wait_ge(s["eh_act"], k - 1)
                mm(psQK[:, k % 2, :], ew1[:, e, :], hsA[:, gsl(g)], start=True, stop=True).then_inc(s["eh_mm"], 1)

            pe.wait_ge(s["xmid_ready"], NG)
            expert_up(0)
            for k in range(NG * NE):
                g, e = divmod(k, NE)
                if k + 1 < NG * NE:
                    expert_up(k + 1)
                if e == 0:
                    if g == 0:
                        pe.wait_ge(s["comb_ready"], 1)
                        pe.wait_ge(s["ey_used"], NG)
                    else:
                        pe.wait_ge(s["out_ready"], TPG * g)
                    four(psT0, lambda j: x_cm[:, g * GW + j * P:g * GW + (j + 1) * P]).then_inc(s["fx_t"], 1)
                pe.wait_ge(s["eh_act"], k + 1)
                pe.wait_ge(s["ey_used"], NG + k - 1)
                yb = (psS, psO)[k % 2]
                for n in range(TPG):
                    i = mm(yb[:, 0, n * P:(n + 1) * P], gel[:, k % 2, n * P:(n + 1) * P], ew2[:, e, :], start=True, stop=True)
                i.then_inc(s["ey_done"], 1)


def shape_constants():
    bf = mybir.dt.np(BF16)
    q = np.arange(P)[:, None]
    col = np.arange(P)[None, :]
    key = np.where(q < W, col - W, col)
    off = (q < key) | (q > key + W)
    masks = np.zeros((P, NT, P), np.float32)
    for n in range(NT):
        none = off | ((key < 0) if n % (NT // B) == 0 else False)
        masks[:, n, :] = np.where(none, -1e30, 0.0)
    half_idx = np.arange(0, DH, 2, dtype=np.float32)
    inv = (1.0 / np.float32(10000.0) ** (half_idx / np.float32(DH))).astype(np.float32)
    t = np.arange(T, dtype=np.float32)
    fr = t[:, None] * inv[None, :]
    fr = np.concatenate([fr, fr], -1).astype(np.float32)
    base = ((half_idx + np.float32(0.4 * DH)) / np.float32(1.4 * DH)).astype(np.float32)
    power = ((t - T // 2) / np.float32(W // 2)).astype(np.float32)
    scl = base[None, :].astype(np.float64) ** power[:, None].astype(np.float64)
    scl = np.concatenate([scl, scl], -1)
    sign = np.where(np.arange(DH) < DH // 2, -1.0, 1.0)
    cos, sin = np.cos(fr.astype(np.float64)), np.sin(fr.astype(np.float64)) * sign
    tab = np.stack([cos * scl * 8.0, sin * scl * 8.0, cos / scl, sin / scl], 1)
    rope = tab.reshape(T // P, P, 4, DH).transpose(1, 0, 2, 3).astype(np.float32)
    before = np.broadcast_to((np.arange(NE)[None, :] < np.arange(NE)[:, None]).astype(np.float32), (P, NE, NE))
    return {
        "ident": np.eye(P, dtype=np.float32), "identb": np.eye(P).astype(bf), "masks": masks.astype(bf),
        "rope": np.ascontiguousarray(rope), "before": np.ascontiguousarray(before),
        "tvec": np.arange(T, dtype=np.float32)[None, :],
    }


def layout(i):
    def pad(v):
        return np.concatenate([v, np.zeros(P - v.shape[0], np.float32)])

    def col(n):
        return np.asarray(i[n])

    cols = [col("L0_attn_b_r"), col("L0_attn_b_k"), col("L0_attn_b_v"), col("L0_attn_b_td"), col("L0_attn_global_decay")]
    cols += [*col("L0_ffn_ln_g"), *col("L0_ffn_ln_b"), *col("L0_ffn_b2")]
    for l in range(LAYERS):
        b1 = col("L0_ffn_b1")[l]
        for side in range(2):
            cols += [pad(b1[side * HID + o:side * HID + o + m]) for o, m in HCH]
    cols += [*col("L0_c"), *col("L1_c")]
    for n in ("nu_log", "theta_log", "gamma_log"):
        v = col("L1_attn_" + n)
        cols.append(np.concatenate([v, v]))
    cols.append(np.concatenate([np.ones(64, np.float32), -np.ones(64, np.float32)]))
    br, bi, cr, ci = (col("L1_attn_" + n).T for n in ("B_re", "B_im", "C_re", "C_im"))
    arr = {
        "x": col("L0_attn_x"),
        "vec": np.stack(cols, 1),
        "wrkv": np.stack([col("L0_attn_W_" + n).T for n in "rkv"], 1),
        "wmod": np.stack([col("L0_wmod"), col("L1_wmod")], 1),
        "wqkv": col("L0_ffn_wqkv"), "wo": col("L0_ffn_wo"), "w1": col("L0_ffn_w1"), "w2": col("L0_ffn_w2"),
        "qks": np.stack([col("L0_ffn_q_scale"), col("L0_ffn_k_scale")], 1)[None],
        "wlru": np.stack([np.concatenate([br, bi], 1), np.concatenate([bi, br], 1),
                          np.concatenate([cr, ci], 0), np.concatenate([ci, cr], 0), col("L1_attn_D").T], 1),
        "wsh": np.stack([col("L1_ffn_sw1"), col("L1_ffn_sw3")], 1),
        "wsh2": col("L1_ffn_sw2").reshape(2, P, P).transpose(1, 0, 2),
        "wrt": col("L1_ffn_router_w").T,
        "rbias": col("L1_ffn_router_bias")[None],
        "ew1": col("L1_ffn_ew1").transpose(1, 0, 2),
        "ew2": col("L1_ffn_ew2").transpose(1, 0, 2),
    }
    arr.update(shape_constants())
    return {k: np.ascontiguousarray(v) for k, v in arr.items()}


def kernel(**inputs):
    import concourse.bacc as _bacc
    from concourse.bass_utils import run_bass_kernel_spmd as _run

    nc = _bacc.Bacc("TRN2", target_bir_lowering=False, num_devices=1)
    arrays = layout(inputs)
    args = {n: nc.dram_tensor(f"in_{n}", v.shape, mybir.dt.from_np(v.dtype), kind="ExternalInput").ap() for n, v in arrays.items()}
    out = nc.dram_tensor("out_0", (B, T, P), F32, kind="ExternalOutput").ap()
    program(nc, args, out)
    r = _run(nc, [{f"in_{n}": v for n, v in arrays.items()}], core_ids=[0])
    return r.results[0]["out_0"]
```

```python
from contextlib import ExitStack

import numpy as np
import concourse.bass as bass
from concourse import mybir

F32 = mybir.dt.float32
BF16 = mybir.dt.bfloat16
I32 = mybir.dt.int32
ALU = mybir.AluOpType
ACT = mybir.ActivationFunctionType
AX = mybir.AxisListType

P = 128
B, T = 2, 1024
NTOK = B * T
NT = NTOK // P
GW = 512
NG = NTOK // GW
GPB = NG // B
TPG = GW // P
LAYERS = 2
H, DH = 8, 64
W = 64
INNER = H * DH
HID = 341
HCH = [(0, 128), (128, 128), (256, 85)]
NE = 8
SEQ = 16
NCH = T // SEQ
PASSES = 4
EPS = 1e-5
TWO_PI = 6.283185

V_BR, V_BK, V_BV, V_BTD, V_GD = range(5)
V_LNG, V_LNB, V_B2 = 5, 7, 9
V_B1 = 11
V_C = 23
V_NU, V_TH, V_GAM, V_SGN = 27, 28, 29, 30
NV = 31

SA, CA, GA, SB, CB, GB = range(6)


class Steps:

    def __init__(self, eng, sem):
        self.eng, self.sem, self.base, self.n = eng, sem, 0, 0

    def did(self, ins):
        ins.then_inc(self.sem, 1)
        self.n += 1

    def sync(self):
        self.eng.wait_ge(self.sem, self.base + self.n)

    def one(self, ins):
        self.did(ins)
        self.sync()

    def enter(self, i, per):
        self.start, self.per = self.base + self.n, per
        self.base, self.n = self.start + i * per, 0

    def leave(self, times):
        assert self.n == self.per, (self.n, self.per)
        self.base, self.n = self.start + times * self.per, 0


def program(nc, a, out):
    with ExitStack() as ctx:
        def sb(name, shape, dt=F32):
            return ctx.enter_context(nc.sbuf_tensor(name, shape, dt))

        def ps(name, shape):
            return ctx.enter_context(nc.psum_tensor(name, shape, F32))

        def sem(name):
            return ctx.enter_context(nc.semaphore(name))

        ident = sb("ident", [P, P])
        identb = sb("identb", [P, P], BF16)
        masks = sb("masks", [P, NT, P], BF16)
        vec = sb("vec", [P, NV])
        wrkv = sb("wrkv", [P, 3, P])
        wmod = sb("wmod", [P, 2, 6 * P])
        wqkv = sb("wqkv", [P, 3 * INNER])
        wo = sb("wo", [P, 4, P])
        w1 = sb("w1", [P, 2 * HID])
        w2 = sb("w2", [P, 3, P])
        wlru = sb("wlru", [P, 5, P])
        wcs = sb("wcs", [P, 2, P])
        wsh = sb("wsh", [P, 2, 256])
        wsh2 = sb("wsh2", [P, 2, P])
        wrt = sb("wrt", [P, NE])
        rbias = sb("rbias", [P, NE])
        before = sb("before", [P, NE, NE])
        ropeb = sb("ropeb", [P, NT // B, 4, DH])
        qks = sb("qks", [P, 2, 2, DH])
        rope = sb("rope", [P, NT, 4, DH])
        half = sb("half", [P, 16])
        mod = sb("mod", [P, 2, 6, 2])
        modt = sb("modt", [P, 2, 2, 4])
        silc = sb("silc", [P, 4])
        sc = sb("sc", [P, 16])
        fr = sb("fr", [P, 16])
        zero = sb("zero", [P, 1])
        zeros = sb("zeros", [P, P])
        zeros2 = sb("zeros2", [P, 4])

        x_cm = sb("x_cm", [P, NTOK])
        z = sb("z", [P, NTOK])
        hsA = sb("hsA", [P, NTOK])
        big = sb("big", [P, 7, NTOK])
        xt = big[:, 6, :].rearrange("p (n d) -> p n d", n=NT)
        tvec = big[:, 5, 0:T]
        ek, gek, ekv, sab, sbb, _, rsg = (big[:, i, :] for i in range(7))
        oT = big[:, 0:4, :]
        hsM = big[:, 4, :]
        ew1 = big[:, 6, 0:NE * P].rearrange("p (e n) -> p e n", e=NE)
        ew2 = big[:, 6, NE * P:].rearrange("p (e n) -> p e n", e=NE)
        tcos = big[:, 5, T:]
        tsin = sb("tsin", [P, T])

        lnx = sb("lnx", [P, TPG, P])
        st6 = sb("st6", [P, TPG, 6])
        mv = sb("mv", [P, TPG, 2])
        rst = sb("rst", [P, TPG])
        hn = sb("hn", [P, 2, GW])

        hst = sb("hst", [P, 2, P])
        sq = sb("sq", [P, 2 * INNER])
        ra = sb("ra", [P, 2 * INNER])
        rb = sb("rb", [P, 2 * INNER])
        qkn = sb("qkn", [P, 2 * INNER])
        nw = sb("nw", [P, 4, 16])
        nwi = sb("nwi", [P, 16], I32)
        qTp = sb("qTp", [P, H, P])
        kT2 = sb("kT2", [P, 4, 4, W])
        nmx = sb("nmx", [P, H])
        prob = sb("prob", [P, H, P])
        pT = sb("pT", [P, H, P])
        vAB = sb("vAB", [P, 2, 2, H * (DH + 1)])
        vA, vB = (vAB[:, k, :, :].rearrange("p u (h d) -> p u h d", h=H) for k in range(2))
        ph = vAB[:, :, :, :].rearrange("p k u n -> p (k u n)")[:, 0:B * (T + 1)].rearrange("p (b t) -> p b t", b=B)
        orc = sb("orc", [P, H])
        osb = sb("osb", [P, INNER])

        gel = sb("gel", [P, 2, GW])
        hg = sb("hg", [P, 3, GW])

        vst = sb("vst", [P, B, NCH])
        cend = sb("cend", [P, B, NCH])
        cnt = sb("cnt", [P, 32])
        cntT = sb("cntT", [P, 32])
        cnti = sb("cnti", [1, 8], I32)
        cntf = sb("cntf", [1, 8])

        psQK = ps("psQK", [P, 2, GW])
        psS = ps("psS", [P, 2, GW])
        psO = ps("psO", [P, 2, GW])
        psT0 = ps("psT0", [P, GW])
        psT1 = ps("psT1", [P, GW])

        names = """ld_x ld_ew ld_c ld_wa ld_wq ld_wl ld_lru ld_moe ld_out st_out
            init silu_c mod_mm mod_fin mod_sc
            ln_t1 ln_var ln_rstd ln_norm ln_t2 ln_out
            xT_fill xT_evac
            kv_mm ek_ready gek_ready ekv_ready sb_ready den_ready r_mm r_ready u_ready mem_done x_mixed
            dve act_own pool_own fallback rope_ready tabs_phase tabs_ready z_ready hsA_ready
            staged qk_mm sq_done ssq_done rope_ab rope_c rn_ready q_ready k_ready
            v_fill v_evac qT_fill qT_evac kT_fill kT_evac pT_fill pT_evac oT_fill oT_evac
            s_done negmax p_ready pv_done va_up o_norm
            wo_done zmid hsM_ready g_mm a_mm gelu_done hg_done w2_done
            bu_mm bu_half lru_g lru_m1 lru_m2 lru_a y_done xmid_ready
            rt_mm sig_done comb_ready sh_mm sh_act sh_h ey_done eh_mm eh_act ey_used acc_done
            gb_mm gb_ready fx_t out_ready""".split()
        s = {n: sem(n) for n in names}

        block = ctx.enter_context(nc.Block())

        def gsl(g):
            return slice(g * GW, (g + 1) * GW)

        def bof(g):
            return g // GPB

        def ln_no(stage, g):
            return stage * NG + g

        def passed(l, i):
            return l * (NT - 1) + i + 1

        def some(count):
            return not (isinstance(count, int) and count <= 0)

        UNR = 3

        @block.sync
        def _(sp):
            xr = a["x"].rearrange("b t d -> (b t) d").rearrange("(n p) d -> p n d", p=P)
            for g in range(NG):
                sp.dma_start(xt[:, g * TPG:(g + 1) * TPG, :], xr[:, g * TPG:(g + 1) * TPG, :]).then_inc(s["ld_x"], 16)
            sp.dma_start(wrkv[:, :, :], a["wrkv"]).then_inc(s["ld_wa"], 16)
            sp.dma_start(ropeb[:, :, :, :], a["rope"]).then_inc(s["ld_wa"], 16)
            sp.dma_start(masks[:, :, :], a["masks"]).then_inc(s["ld_wa"], 16)
            sp.dma_start(qks[:, :, :, :], a["qks"].to_broadcast([P, 2, 2, DH])).then_inc(s["ld_wa"], 16)
            for l in range(LAYERS):
                if l:
                    sp.wait_ge(s["v_fill"], NT * l)
                sp.dma_start(wqkv[:, :], a["wqkv"][l]).then_inc(s["ld_wq"], 16)
                if l:
                    sp.wait_ge(s["z_ready"], NG * l)
                sp.dma_start(wo[:, :, :], a["wo"][l].rearrange("(c p) n -> p c n", p=P)).then_inc(s["ld_wl"], 16)
                sp.dma_start(w1[:, :], a["w1"][l]).then_inc(s["ld_wl"], 16)
                sp.dma_start(w2[:, 0:2, :], a["w2"][l, 0:256, :].rearrange("(c p) n -> p c n", p=P)).then_inc(s["ld_wl"], 16)
                sp.dma_start(w2[0:HID - 256, 2, :], a["w2"][l, 256:HID, :]).then_inc(s["ld_wl"], 16)
                if l == 0:
                    sp.wait_ge(s["x_mixed"], NG)
                    sp.dma_start(ew1, a["ew1"]).then_inc(s["ld_ew"], 16)
                    sp.dma_start(ew2, a["ew2"]).then_inc(s["ld_ew"], 16)
            outr = out.rearrange("b t d -> (b t) d").rearrange("(n p) d -> p n d", p=P)
            for g in range(NG):
                sp.wait_ge(s["out_ready"], TPG * (g + 1))
                sp.dma_start(outr[:, g * TPG:(g + 1) * TPG, :], big[:, 4, gsl(g)].rearrange("p (n d) -> p n d", n=TPG)).then_inc(s["st_out"], 16)
            sp.wait_ge(s["st_out"], 16 * NG)

        @block.scalar
        def _(act):
            act.dma_start(ident[:, :], a["ident"]).then_inc(s["ld_c"], 16)
            act.dma_start(vec[:, :], a["vec"]).then_inc(s["ld_c"], 16)
            act.dma_start(wmod[:, :, :], a["wmod"]).then_inc(s["ld_c"], 16)
            act.dma_start(identb[:, :], a["identb"]).then_inc(s["ld_c"], 16)
            act.dma_start(tvec, a["tvec"].to_broadcast([P, T])).then_inc(s["ld_lru"], 16)
            act.dma_start(wlru[:, :, :], a["wlru"]).then_inc(s["ld_lru"], 16)
            for dst, name in ((wsh[:, :, :], "wsh"), (wsh2[:, :, :], "wsh2"), (wrt[:, :], "wrt"),
                              (before[:, :, :], "before")):
                act.dma_start(dst, a[name]).then_inc(s["ld_moe"], 16)
            act.dma_start(rbias[:, :], a["rbias"].to_broadcast([P, NE])).then_inc(s["ld_moe"], 16)
            own = Steps(act, s["act_own"])

            act.wait_ge(s["ld_c"], 64)
            act.activation(silc[:, :], vec[:, V_C:V_C + 4], ACT.Silu).then_inc(s["silu_c"], 1)

            def ln_out(n, dst, scale, bias):
                act.wait_ge(s["ln_t2"], n + 1)
                act.activation(dst, psT1[:, :], ACT.Identity, bias=bias, scale=scale).then_inc(s["ln_out"], 1)

            for g in range(NG):
                act.wait_ge(s["xT_fill"], g + 1)
                act.activation(x_cm[:, gsl(g)], psT0[:, :], ACT.Copy).then_inc(s["xT_evac"], 1)
                if g == 0:
                    act.wait_ge(s["mod_sc"], 1)
                b = bof(g)
                ln_out(ln_no(0, g), hsA[:, gsl(g)], mod[:, 0, CA, b:b + 1], mod[:, 0, SA, b:b + 1])
                act.wait_ge(s["kv_mm"], 2 * g + 1)
                own.one(act.activation(ek[:, gsl(g)], psS[:, g % 2, :], ACT.Exp, bias=vec[:, V_BK:V_BK + 1]))
                act.activation(ek[:, gsl(g)], ek[:, gsl(g)], ACT.Identity, bias=0.0, scale=sc[:, 1:2]).then_inc(s["ek_ready"], 1)
                act.wait_ge(s["ek_ready"], g + 1)
                act.activation(gek[:, gsl(g)], ek[:, gsl(g)], ACT.Identity, bias=sc[:, 3:4], scale=sc[:, 2:3]).then_inc(s["gek_ready"], 1)
            for g in range(NG):
                act.wait_ge(s["r_mm"], g + 1)
                act.activation(rsg[:, gsl(g)], psQK[:, g % 2, :], ACT.Sigmoid, bias=vec[:, V_BR:V_BR + 1]).then_inc(s["r_ready"], 1)

            for g in range(NG):
                b = bof(g)
                ln_out(ln_no(1, g), z[:, gsl(g)], mod[:, 0, CB, b:b + 1], mod[:, 0, SB, b:b + 1])

            def squares(n, part):
                act.wait_ge(s["qk_mm"], 2 * n + part + 1)
                if some(n):
                    act.wait_ge(s["ssq_done"], 2 * n - 1 + part)
                act.activation(sq[:, part * INNER:(part + 1) * INNER], psQK[:, part, :], ACT.Square).then_inc(s["sq_done"], 1)

            def four(bank):
                return bank[:, :].rearrange("p (c t) -> p c t", c=4)

            def v_copy(l, i, u):
                n = l * NT + i
                act.wait_ge(s["v_fill"], n + 1)
                src = psT1[:, :].rearrange("p (h d) -> p h d", h=H)
                if some(i - 1):
                    act.wait_ge(s["va_up"], passed(l, i - 2))
                act.activation(vB[:, u, :, 0:DH], src, ACT.Copy).then_inc(s["v_evac"], 1)
                act.activation(vA[0:64, u, :, 0:DH], src[0:64], ACT.Copy).then_inc(s["v_evac"], 1)

            def qk_copy(n, u):
                act.wait_ge(s["qT_fill"], n + 1)
                qd = qTp[:, :, :].rearrange("p (c e) t -> p c e t", e=2)
                for e in range(2):
                    r = slice(64 * e, 64 * e + 64)
                    act.activation(qd[r, :, e, :], four(psT0)[r], ACT.Copy).then_inc(s["qT_evac"], 1)
                act.wait_ge(s["kT_fill"], n + 1)
                act.activation(kT2[:, :, u::2, :], psT1[:, :].rearrange("p (c w t) -> p c w t", c=4, w=2),
                               ACT.Copy).then_inc(s["kT_evac"], 1)

            def exps(n, hb):
                act.wait_ge(s["negmax"], 2 * n + hb + 1)
                for h in range(4 * hb, 4 * hb + 4):
                    act.activation(prob[:, h, :], psS[:, hb, (h % 4) * P:(h % 4 + 1) * P], ACT.Exp,
                                   bias=nmx[:, h:h + 1]).then_inc(s["p_ready"], 1)

            def attn_body(l, i, u, left=2):
                n = l * NT + i
                exps(n, 1)
                act.wait_ge(s["pT_fill"], 2 * n + 1)
                act.activation(pT[:, 0:4, :], four(psT1), ACT.Copy).then_inc(s["pT_evac"], 1)
                if left > 1:
                    squares(n + 2, 0)
                    squares(n + 2, 1)
                act.wait_ge(s["pT_fill"], 2 * n + 2)
                act.activation(pT[:, 4:8, :], four(psT0), ACT.Copy).then_inc(s["pT_evac"], 1)
                if left:
                    v_copy(l, i + 1, 1 - u)
                    qk_copy(n + 1, 1 - u)
                    exps(n + 1, 0)
                act.wait_ge(s["oT_fill"], n + 1)
                act.activation(oT[:, :, bass.ds(i * P, P)], four(psT0), ACT.Copy).then_inc(s["oT_evac"], 1)

            def mlp_act(l, g):
                n = ln_no(2 + l, g)
                ln_out(n, hn[:, g % 2, :], vec[:, V_LNG + l:V_LNG + l + 1], vec[:, V_LNB + l:V_LNB + l + 1])
                for j, (o, m) in enumerate(HCH):
                    k = (l * NG + g) * 3 + j
                    act.wait_ge(s["g_mm"], k + 1)
                    if k >= 2:
                        act.wait_ge(s["hg_done"], k - 1)
                    c = V_B1 + 6 * l + 3 + j
                    act.activation(gel[0:m, k % 2, :], psS[0:m, k % 2, :], ACT.Gelu, bias=vec[0:m, c:c + 1]).then_inc(s["gelu_done"], 1)

            for l in range(LAYERS):
                n = l * NT
                squares(n, 0)
                squares(n, 1)
                v_copy(l, 0, 0)
                squares(n + 1, 0)
                squares(n + 1, 1)
                qk_copy(n, 0)
                exps(n, 0)
                with act.Fori(0, NT // 2 - 1) as r:
                    attn_body(l, 2 * r, 0)
                    attn_body(l, 2 * r + 1, 1)
                attn_body(l, NT - 2, 0, 1)
                attn_body(l, NT - 1, 1, 0)
                for g in range(NG):
                    mlp_act(l, g)

            act.wait_ge(s["tabs_phase"], 1)
            act.activation(tcos, tcos, ACT.Sin, scale=TWO_PI).then_inc(s["tabs_ready"], 1)
            act.activation(tsin[:, :], tsin[:, :], ACT.Sin, scale=sc[:, 8:9]).then_inc(s["tabs_ready"], 1)
            for g in range(NG):
                b = bof(g)
                ln_out(ln_no(4, g), hn[:, g % 2, :], mod[:, 1, CA, b:b + 1], mod[:, 1, SA, b:b + 1])

            for g in range(NG):
                b = bof(g)
                ln_out(ln_no(5, g), hsA[:, gsl(g)], mod[:, 1, CB, b:b + 1], mod[:, 1, SB, b:b + 1])
            act.wait_ge(s["rt_mm"], 1)
            act.activation(sq[:, 0:P], psT0[:, 0:P], ACT.Sigmoid).then_inc(s["sig_done"], 1)
            for g in range(NG):
                for j in range(2):
                    k = 2 * g + j
                    act.wait_ge(s["sh_mm"], 2 * k + 1)
                    if k >= 2:
                        act.wait_ge(s["sh_h"], k - 1)
                    act.activation(gel[:, k % 2, :], psS[:, k % 2, :], ACT.Silu).then_inc(s["sh_act"], 1)
            for g in range(NG):
                for e in range(NE):
                    k = g * NE + e
                    act.wait_ge(s["eh_mm"], k + 1)
                    if k >= 2:
                        act.wait_ge(s["ey_done"], NG + k - 1)
                    else:
                        act.wait_ge(s["sh_h"], 2 * NG)
                    act.activation(gel[:, k % 2, :], psQK[:, k % 2, :], ACT.Gelu).then_inc(s["eh_act"], 1)

        @block.gpsimd
        def _(pool):
            own = Steps(pool, s["pool_own"])
            pool.memset(zeros[:, :], 0.0).then_inc(s["init"], 1)
            pool.memset(half[:, :], -0.5).then_inc(s["init"], 1)
            pool.memset(kT2[:, :, :, :], 0.0).then_inc(s["init"], 1)
            pool.memset(qTp[:, :, :], 0.0).then_inc(s["init"], 1)
            pool.wait_ge(s["init"], 4)

            def copy(dst, src):
                return pool.tensor_scalar(dst, src, 1.0, 0.0, ALU.mult, ALU.add)

            def alone(k):
                pool.tensor_tensor(zeros2[:, k:k + 1], zeros[:, 0:1], zeros[:, 1:2], ALU.add)

            def ln_rstd(n):
                pool.wait_ge(s["ln_var"], n + 1)
                pool.tensor_tensor(rst[:, :], mv[:, :, 1], half[:, 0:TPG], ALU.pow).then_inc(s["ln_rstd"], 1)

            def rope_tables(l):
                for b in range(B):
                    for c in range(4):
                        dst = rope[:, b * 8:(b + 1) * 8, c, :]
                        src = ropeb[:, :, c, :]
                        scl = qks[:, l, c // 2, :]
                        if c % 2 == 0:
                            i = pool.tensor_tensor(dst, src, scl.unsqueeze(1).to_broadcast([P, 8, DH]), ALU.mult)
                        else:
                            r = scl.rearrange("p (a d) -> p a d", a=2)[:, ::-1, :]
                            i = pool.tensor_tensor(dst.rearrange("p n (a d) -> p n a d", a=2),
                                                   src.rearrange("p n (a d) -> p n a d", a=2),
                                                   r.unsqueeze(1).to_broadcast([P, 8, 2, DH // 2]), ALU.mult)
                        i.then_inc(s["rope_ready"], 1)

            pool.wait_ge(s["ld_c"], 64)
            own.one(pool.memset(fr[:, 0:1], float(np.e)))
            for dst, src in ((4, V_NU), (5, V_TH), (6, V_GAM)):
                own.did(pool.tensor_tensor(sc[:, dst:dst + 1], fr[:, 0:1], vec[:, src:src + 1], ALU.pow))
            own.did(pool.tensor_tensor(sc[:, 0:1], fr[:, 0:1], vec[:, V_BTD:V_BTD + 1], ALU.pow))
            own.did(pool.tensor_tensor(sc[:, 2:3], fr[:, 0:1], vec[:, V_GD:V_GD + 1], ALU.pow))
            own.one(pool.tensor_scalar(fr[:, 1:2], vec[:, V_BTD:V_BTD + 1], 0.0, -T / 2, ALU.max, ALU.mult))
            own.one(pool.tensor_tensor(sc[:, 1:2], fr[:, 0:1], fr[:, 1:2], ALU.pow))
            own.did(pool.tensor_scalar(sc[:, 3:4], sc[:, 1:2], 1e-6, 0.0, ALU.mult, ALU.add))
            own.one(pool.tensor_scalar(fr[:, 2:3], sc[:, 4:5], -1.0, 0.0, ALU.mult, ALU.add))
            own.one(pool.tensor_tensor(sc[:, 7:8], fr[:, 0:1], fr[:, 2:3], ALU.pow))
            pool.wait_ge(s["mod_fin"], 1)
            copy(fr[:, 3:4], sc[:, 7:8]).then_inc(s["mod_sc"], 1)
            for g in range(NG):
                ln_rstd(ln_no(0, g))
                pool.wait_ge(s["gek_ready"], g + 1)
                pool.wait_ge(s["sb_ready"], g + 1)
                pool.tensor_tensor(gek[:, gsl(g)], gek[:, gsl(g)], sbb[:, gsl(g)], ALU.add).then_inc(s["den_ready"], 1)
            pool.wait_ge(s["ld_wa"], 64)
            rope_tables(0)
            pool.wait_ge(s["ld_lru"], 32)
            C1 = 1.0 / (2 * np.pi)
            CH = float(np.round(C1 * 4096 * 4) / (4096 * 4))
            CL = C1 - CH
            MAGIC = 1.5 * 2 ** 23
            th = sc[:, 5:6]

            def ts(dst, src, s1, s2, o0, o1):
                own.one(pool.tensor_scalar(dst, src, s1, s2, o0, o1))

            def tt(dst, x0, x1, op):
                own.one(pool.tensor_tensor(dst, x0, x1, op))

            c = lambda i: fr[:, i:i + 1]
            ts(sc[:, 8:9], vec[:, V_SGN:V_SGN + 1], TWO_PI, 0.0, ALU.mult, ALU.add)
            ts(c(4), th, 4097.0, 0.0, ALU.mult, ALU.add)
            tt(c(5), c(4), th, ALU.subtract)
            tt(c(4), c(4), c(5), ALU.subtract)
            tt(c(5), th, c(4), ALU.subtract)
            ts(c(6), c(4), CH, 0.0, ALU.mult, ALU.add)
            ts(c(7), c(4), CL, 0.0, ALU.mult, ALU.add)
            ts(c(8), c(5), C1, 0.0, ALU.mult, ALU.add)
            tt(c(7), c(7), c(8), ALU.add)
            ts(c(8), c(6), 4096.0, MAGIC, ALU.mult, ALU.add)
            ts(c(8), c(8), -MAGIC, 1.0 / 4096, ALU.add, ALU.mult)
            tt(c(6), c(6), c(8), ALU.subtract)
            tt(c(9), c(6), c(7), ALU.add)
            ts(tcos[:, :], tvec, c(8), 0.0, ALU.mult, ALU.add)
            ts(tsin[:, :], tcos[:, :], MAGIC, -MAGIC, ALU.add, ALU.add)
            tt(tcos[:, :], tcos[:, :], tsin[:, :], ALU.subtract)
            ts(tsin[:, :], tvec, c(9), 0.0, ALU.mult, ALU.add)
            tt(tsin[:, :], tcos[:, :], tsin[:, :], ALU.add)
            ts(tcos[:, :], tsin[:, :], MAGIC, -MAGIC, ALU.add, ALU.add)
            tt(tsin[:, :], tsin[:, :], tcos[:, :], ALU.subtract)
            ts(tcos[:, :], tsin[:, :], 1.0, 0.25, ALU.mult, ALU.add)
            ts(tvec, tcos[:, :], MAGIC, -MAGIC, ALU.add, ALU.add)
            pool.tensor_tensor(tcos[:, :], tcos[:, :], tvec, ALU.subtract).then_inc(s["tabs_phase"], 1)
            ts(c(10), sc[:, 6:7], vec[:, V_SGN:V_SGN + 1], 1.0, ALU.mult, ALU.mult)
            ts(c(11), c(10), -1.0, 0.0, ALU.mult, ALU.add)
            ts(wcs[:, 0, :], wlru[:, 2, :], c(10), 0.0, ALU.mult, ALU.add)
            ts(wcs[:, 1, :], wlru[:, 3, :], c(11), 0.0, ALU.mult, ALU.add)
            for g in range(NG):
                ln_rstd(ln_no(1, g))

            pool.wait_ge(s["x_mixed"], NG)
            pool.memset(vAB[:, :, :, :], 1.0).then_inc(s["init"], 1)
            pool.wait_ge(s["init"], 5)

            def stage(l, i, u):
                n = l * NT + i
                if some(i - 1):
                    pool.wait_ge(s["v_fill"], n - 1)
                alone(u)
                pool.tensor_tensor(hst[:, u, :], hsA[:, bass.ds(i * P, P)], zeros[:, :], ALU.add).then_inc(s["staged"], 1)

            def heads(x, part):
                return x[:, part * INNER:(part + 1) * INNER].rearrange("p (h d) -> p h d", h=H)

            def rope_sum(n, part):
                r = slice(part * INNER, (part + 1) * INNER)
                pool.wait_ge(s["rope_ab"], 4 * n + 2 * part + 2)
                pool.tensor_tensor(ra[:, r], ra[:, r], rb[:, r], ALU.add).then_inc(s["rope_c"], 1)

            def k_normed(n):
                pool.wait_ge(s["rope_c"], 2 * n + 2)
                pool.wait_ge(s["rn_ready"], n + 1)
                if some(n):
                    pool.wait_ge(s["kT_fill"], n)
                pool.tensor_tensor(heads(qkn, 1), heads(ra, 1), nw[:, 0, 8:16].unsqueeze(2).to_broadcast([P, H, DH]),
                                   ALU.mult).then_inc(s["k_ready"], 1)

            def pool_body(l, i, u, left=2):
                n = l * NT + i
                if left > 1:
                    stage(l, i + 2, u)
                if left:
                    rope_sum(n + 1, 0)
                    pool.wait_ge(s["rope_c"], 2 * n + 3)
                    pool.wait_ge(s["v_evac"], 2 * n + 1)
                    if some(n):
                        pool.wait_ge(s["pv_done"], n)
                    pool.tensor_tensor(vA[64:128, 1 - u, :, 0:DH], vB[64:128, u, :, 0:DH],
                                       zeros[64:128, 0:1].unsqueeze(2).to_broadcast([64, H, DH]), ALU.add).then_inc(s["va_up"], 1)
                    pool.wait_ge(s["va_up"], passed(l, i))
                    rope_sum(n + 1, 1)
                    k_normed(n + 1)

            for l in range(LAYERS):
                pool.wait_ge(s["hsA_ready"], 2 * NG * (l + 1))
                n = l * NT
                stage(l, 0, 0)
                stage(l, 1, 1)
                for part in range(2):
                    rope_sum(n, part)
                k_normed(n)
                with pool.Fori(0, NT // 2 - 1) as r:
                    pool_body(l, 2 * r, 0)
                    pool_body(l, 2 * r + 1, 1)
                pool_body(l, NT - 2, 0, 1)
                if l + 1 < LAYERS:
                    pool.wait_ge(s["rope_ab"], 4 * NT * (l + 1))
                    rope_tables(l + 1)
                for g in range(NG):
                    ln_rstd(ln_no(2 + l, g))

            for g in range(NG):
                ln_rstd(ln_no(4, g))
                t = slice((g % GPB) * GW, (g % GPB + 1) * GW)
                pool.wait_ge(s["bu_half"], 2 * g + 2)
                pool.tensor_tensor(ra[:, 0:GW], ra[:, 0:GW], rb[:, 0:GW], ALU.add).then_inc(s["lru_a"], 1)
                pool.wait_ge(s["lru_g"], g + 1)
                if g:
                    pool.wait_ge(s["y_done"], g)
                pool.tensor_tensor(hg[:, 1, :], z[:, gsl(g)], tsin[:, t], ALU.mult).then_inc(s["lru_m2"], 1)
            for g in range(NG):
                ln_rstd(ln_no(5, g))

        @block.vector
        def _(dve):
            own = Steps(dve, s["dve"])
            own.one(dve.memset(ph[:, :, :], 0.0))
            own.one(dve.memset(cnt[:, :], 0.0))
            dve.wait_ge(s["ld_c"], 64)
            dve.wait_ge(s["mod_mm"], 1)
            own.one(dve.tensor_copy(mod[:, :, :, :], psT1[:, 0:24].rearrange("p (b k n) -> p b k n", b=2, k=6)))
            for k in (CA, CB):
                own.did(dve.tensor_scalar(mod[:, :, k, :], mod[:, :, k, :], 1.0, None, ALU.add))
            for k in (GA, GB):
                gk = mod[:, :, k, :]
                own.one(dve.tensor_scalar(modt[:, 0, :, 0:2], gk, 0.0, 2.0, ALU.is_ge, ALU.mult))
                own.did(dve.tensor_scalar(modt[:, 0, :, 2:4], modt[:, 0, :, 0:2], -1.0, None, ALU.add))
                own.one(dve.scalar_tensor_tensor(out=modt[:, 1, :, 0:2], in0=gk, scalar=-1.0, in1=gk, op0=ALU.mult, op1=ALU.max))
                own.one(dve.scalar_tensor_tensor(out=gk, in0=modt[:, 1, :, 0:2], scalar=0.25, in1=modt[:, 0, :, 2:4],
                                                 op0=ALU.max, op1=ALU.mult))
            own.sync()
            dve.tensor_copy(modt[:, 0, 0, 0:1], mod[:, 0, 0, 0:1]).then_inc(s["mod_fin"], 1)

            def ln_stats(n, src):
                for k in range(TPG):
                    own.did(dve.bn_stats(st6[:, k, :], src[:, k, :]))
                own.sync()
                for k in range(TPG):
                    own.did(dve.bn_aggr(mv[:, k, :], st6[:, k, :]))
                own.sync()
                dve.tensor_scalar(mv[:, :, 1], mv[:, :, 1], EPS, None, ALU.add).then_inc(s["ln_var"], 1)

            def ln_norm(n, src):
                dve.wait_ge(s["ln_rstd"], n + 1)
                if n:
                    dve.wait_ge(s["ln_t2"], n)
                for k in range(TPG):
                    dve.tensor_scalar(lnx[:, k, :], src[:, k, :], mv[:, k, 0:1], rst[:, k:k + 1],
                                      ALU.subtract, ALU.mult).then_inc(s["ln_norm"], 1)

            def ln(n):
                src = psT0[:, :].rearrange("p (n d) -> p n d", n=TPG)
                dve.wait_ge(s["ln_t1"], n - NG + 1)
                ln_stats(n, src)
                ln_norm(n, src)

            for g in range(NG):
                n = ln_no(0, g)
                dve.wait_ge(s["ld_x"], 16 * NG)
                src = xt[:, g * TPG:(g + 1) * TPG, :]
                ln_stats(n, src)
                ln_norm(n, src)
                c = gsl(g)
                dve.wait_ge(s["kv_mm"], 2 * g + 2)
                dve.wait_ge(s["ek_ready"], g + 1)
                dve.scalar_tensor_tensor(out=ekv[:, c], in0=psO[:, g % 2, :], scalar=vec[:, V_BV:V_BV + 1],
                                         in1=ek[:, c], op0=ALU.add, op1=ALU.mult).then_inc(s["ekv_ready"], 1)
                dve.wait_ge(s["ekv_ready"], g + 1)
                td = sc[:, 0:1].to_broadcast([P, GW])
                last = g * GW - 1
                first = g % GPB == 0
                dve.tensor_tensor_scan(sbb[:, c], td, ek[:, c], 0.0 if first else sbb[:, last:last + 1],
                                       ALU.mult, ALU.add).then_inc(s["sb_ready"], 1)
                own.did(dve.tensor_tensor_scan(sab[:, c], td, ekv[:, c], 0.0 if first else sab[:, last:last + 1],
                                               ALU.mult, ALU.add))
                own.sync()
                own.one(dve.scalar_tensor_tensor(out=sab[:, c], in0=ekv[:, c], scalar=sc[:, 2:3], in1=sab[:, c],
                                                 op0=ALU.mult, op1=ALU.add) if False else
                        dve.scalar_tensor_tensor(out=ekv[:, c], in0=ekv[:, c], scalar=sc[:, 2:3], in1=sab[:, c],
                                                 op0=ALU.mult, op1=ALU.add))
                dve.wait_ge(s["den_ready"], g + 1)
                own.one(dve.reciprocal(gek[:, c], gek[:, c]))
                own.did(dve.tensor_tensor(ekv[:, c], ekv[:, c], gek[:, c], ALU.mult))
            own.sync()
            for g in range(NG):
                c = gsl(g)
                dve.wait_ge(s["r_ready"], g + 1)
                own.did(dve.scalar_tensor_tensor(out=ekv[:, c], in0=ekv[:, c], scalar=20.0, in1=rsg[:, c],
                                                 op0=ALU.mult, op1=ALU.mult))
            own.sync()

            cur = ekv.rearrange("p (b c j) -> p b c j", b=B, c=NCH)

            def at(j):
                return ph[:, :, j:j + SEQ * (NCH - 1) + 1:SEQ]

            def membrane_pass(steps):
                for j in range(SEQ):
                    steps.one(dve.scalar_tensor_tensor(out=vst[:, :, :], in0=at(j), scalar=-0.3, in1=cur[:, :, :, j],
                                                       op0=ALU.mult, op1=ALU.add))
                    steps.one(dve.scalar_tensor_tensor(out=at(j + 1), in0=at(j), scalar=-1.0, in1=vst[:, :, :],
                                                       op0=ALU.is_lt, op1=ALU.subtract))

            with dve.Fori(0, PASSES - 1) as k:
                own.enter(k, 2 * SEQ)
                membrane_pass(own)
            own.leave(PASSES - 1)
            own.one(dve.tensor_copy(cend[:, :, :], at(0)))
            membrane_pass(own)
            own.one(dve.tensor_tensor(cend[:, :, :], cend[:, :, :], at(0), ALU.not_equal))
            own.one(dve.tensor_reduce(cnt[:, 0:1], cend[:, :, :], AX.XY, ALU.add))
            own.one(dve.transpose(cntT[:, :], cnt[:, :]))
            for q in range(4):
                own.did(dve.tensor_reduce(cntf[0:1, q:q + 1], cntT[32 * q:32 * q + 1, :], AX.X, ALU.add))
            own.sync()
            own.one(dve.tensor_reduce(cntf[0:1, 4:5], cntf[0:1, 0:4], AX.X, ALU.add))
            own.one(dve.tensor_copy(cnti[0:1, 0:1], cntf[0:1, 4:5]))
            changed = dve.value_load(cnti[0:1, 0:1], min_val=0, max_val=P * B * NCH)
            with dve.If(changed != 0):
                again = Steps(dve, s["fallback"])
                with dve.Fori(0, NCH) as k:
                    again.enter(k, 2 * SEQ)
                    membrane_pass(again)
                again.leave(NCH)
            for g in range(NG):
                b, o = bof(g), (g % GPB) * GW
                own.did(dve.tensor_scalar(ekv[:, gsl(g)], ph[:, b, 1 + o:1 + o + GW], -1.0, mod[:, 0, GA, b:b + 1],
                                          ALU.is_lt, ALU.mult))
            own.sync()
            for g in range(NG):
                dve.wait_ge(s["xT_evac"], g + 1)
                dve.tensor_tensor(x_cm[:, gsl(g)], x_cm[:, gsl(g)], ekv[:, gsl(g)], ALU.add).then_inc(s["x_mixed"], 1)
            dve.wait_ge(s["x_mixed"], NG)

            def shifted(dst, src, g, name):
                o = g * GW
                dve.tensor_copy(dst[0:64, o:o + GW], src[0:64, o:o + GW]).then_inc(s[name], 1)
                w = GW - (g % GPB == GPB - 1)
                dve.tensor_copy(dst[64:128, o + 1:o + 1 + w], src[64:128, o:o + w]).then_inc(s[name], 1)

            own.did(dve.memset(hsA[64:128, T:T + 1], 0.0))
            own.did(dve.memset(hsA[64:128, 0:1], 0.0))
            own.did(dve.memset(hsM[64:128, T:T + 1], 0.0))
            own.did(dve.memset(hsM[64:128, 0:1], 0.0))
            own.sync()
            for g in range(NG):
                ln(ln_no(1, g))
                dve.wait_ge(s["ln_out"], ln_no(1, g) + 1)
                shifted(hsA, z, g, "hsA_ready")

            def heads(x):
                return x.rearrange("p (h d) -> p h d", h=H)

            def rope_product(n, slot, part, c):
                r = slice(part * INNER, (part + 1) * INNER)
                dve.wait_ge(s["sq_done"], 2 * n + part + 1)
                if some(n):
                    dve.wait_ge(s[("q_ready", "k_ready")[part]], n)
                if c == 0:
                    i = dve.tensor_tensor(heads(ra[:, r]), heads(psQK[:, part, :]),
                                          rope[:, slot, 2 * part, :].unsqueeze(1).to_broadcast([P, H, DH]), ALU.mult)
                else:
                    i = dve.tensor_tensor(rb[:, r].rearrange("p (h a d) -> p h a d", h=H, a=2),
                                          psQK[:, part, :].rearrange("p (h a d) -> p h a d", h=H, a=2)[:, :, ::-1, :],
                                          rope[:, slot, 2 * part + 1, :].rearrange("p (a d) -> p a d", a=2).unsqueeze(1)
                                          .to_broadcast([P, H, 2, DH // 2]), ALU.mult)
                i.then_inc(s["rope_ab"], 1)

            y, y2 = nw[:, 2, :], nw[:, 1, :]

            def norm_first(n, slot):
                for part in range(2):
                    dve.wait_ge(s["sq_done"], 2 * n + part + 1)
                    dve.tensor_reduce(nw[:, 1, 8 * part:8 * part + 8], heads(sq[:, part * INNER:(part + 1) * INNER]),
                                      AX.X, ALU.add).then_inc(s["ssq_done"], 1)
                dve.wait_ge(s["ssq_done"], 2 * n + 2)
                own.did(dve.tensor_scalar(y2, y2, 1e-24, None, ALU.max))
                rope_product(n, slot, 0, 0)
                own.sync()
                own.did(dve.tensor_scalar(nwi[:, :], y2.bitcast(I32), 1, None, ALU.logical_shift_right))
                own.did(dve.tensor_scalar(nw[:, 3, :], y2, -0.5, None, ALU.mult))
                rope_product(n, slot, 0, 1)
                own.sync()
                own.did(dve.tensor_scalar(y.bitcast(I32), nwi[:, :], -1.0, float(0x5F3759DF), ALU.mult, ALU.add))

            def newton(n, k):
                own.sync()
                if k % 3 == 0:
                    own.did(dve.tensor_tensor(y2, y, y, ALU.mult))
                elif k % 3 == 1:
                    own.did(dve.tensor_tensor(y2, y2, nw[:, 3, :], ALU.mult))
                elif k < 3 * UNR - 1:
                    own.did(dve.scalar_tensor_tensor(out=y, in0=y2, scalar=1.5, in1=y, op0=ALU.add, op1=ALU.mult))
                else:
                    if some(n):
                        dve.wait_ge(s["k_ready"], n)
                    dve.scalar_tensor_tensor(out=nw[:, 0, :], in0=y2, scalar=1.5, in1=y, op0=ALU.add,
                                             op1=ALU.mult).then_inc(s["rn_ready"], 1)

            def norm_rest(n, slot, between):
                newton(n, 0)
                rope_product(n, slot, 1, 0)
                newton(n, 1)
                if between:
                    between()
                newton(n, 2)
                rope_product(n, slot, 1, 1)
                for k in range(3, 3 * UNR):
                    newton(n, k)

                dve.wait_ge(s["rn_ready"], n + 1)
                dve.wait_ge(s["rope_c"], 2 * n + 1)
                if some(n):
                    dve.wait_ge(s["qT_fill"], n)
                dve.tensor_tensor(heads(qkn[:, 0:INNER]), heads(ra[:, 0:INNER]),
                                  nw[:, 0, 0:8].unsqueeze(2).to_broadcast([P, H, DH]), ALU.mult).then_inc(s["q_ready"], 1)

            NORM_STEPS = 4 + 3 * UNR - 1

            def attn_body(l, i, left=2):
                n = l * NT + i

                def negmax(hb):
                    dve.wait_ge(s["s_done"], 2 * n + hb + 1)
                    dve.tensor_reduce(nmx[:, 4 * hb:4 * hb + 4], psS[:, hb, :].rearrange("p (h k) -> p h k", h=4),
                                      AX.X, ALU.max, negate=True).then_inc(s["negmax"], 1)
                negmax(0)
                if left:
                    norm_rest(n + 1, i + 1, lambda: negmax(1))
                else:
                    negmax(1)
                if left > 1:
                    norm_first(n + 2, i + 2)
                ov = psO[:, :, 0:4 * (DH + 1)].rearrange("p b (h d) -> p b h d", h=4)
                dve.wait_ge(s["pv_done"], n + 1)
                own.one(dve.reciprocal(orc[:, :].rearrange("p (b h) -> p b h", b=2), ov[:, :, :, DH]))
                if some(n):
                    dve.wait_ge(s["oT_fill"], n)
                dve.tensor_tensor(osb[:, :].rearrange("p (b h d) -> p b h d", b=2, h=4), ov[:, :, :, 0:DH],
                                  orc[:, :].rearrange("p (b h) -> p b h", b=2).unsqueeze(3).to_broadcast([P, 2, 4, DH]),
                                  ALU.mult).then_inc(s["o_norm"], 1)
            for l in range(LAYERS):
                dve.wait_ge(s["rope_ready"], 8 * (l + 1))
                norm_first(l * NT, 0)
                norm_rest(l * NT, 0, None)
                norm_first(l * NT + 1, 1)
                with dve.Fori(0, NT // 2 - 1) as r:
                    own.enter(r, 2 * (NORM_STEPS + 1))
                    attn_body(l, 2 * r)
                    attn_body(l, 2 * r + 1)
                own.leave(NT // 2 - 1)
                attn_body(l, NT - 2, 1)
                attn_body(l, NT - 1, 0)

                def mid(g):
                    n = l * NG + g
                    dve.wait_ge(s["wo_done"], n + 1)
                    dve.tensor_tensor(z[:, gsl(g)], z[:, gsl(g)], psQK[:, g % 2, :], ALU.add).then_inc(s["zmid"], 1)
                    dve.wait_ge(s["zmid"], n + 1)
                    shifted(hsM, z, g, "hsM_ready")

                mid(0)
                for g in range(NG):
                    n = l * NG + g
                    ln(ln_no(2 + l, g))
                    if g + 1 < NG:
                        mid(g + 1)
                    for j, (o, m) in enumerate(HCH):
                        k = n * 3 + j
                        dve.wait_ge(s["gelu_done"], k + 1)
                        dve.wait_ge(s["a_mm"], k + 1)
                        if n:
                            dve.wait_ge(s["w2_done"], n)
                        c = V_B1 + 6 * l + j
                        dve.scalar_tensor_tensor(out=hg[0:m, j, :], in0=psO[0:m, k % 2, :], scalar=vec[0:m, c:c + 1],
                                                 in1=gel[0:m, k % 2, :], op0=ALU.add, op1=ALU.mult).then_inc(s["hg_done"], 1)
                    dve.wait_ge(s["w2_done"], n + 1)
                    dve.scalar_tensor_tensor(out=z[:, gsl(g)], in0=psQK[:, g % 2, :], scalar=vec[:, V_B2 + l:V_B2 + l + 1],
                                             in1=z[:, gsl(g)], op0=ALU.add, op1=ALU.add).then_inc(s["z_ready"], 1)
                    dve.wait_ge(s["z_ready"], n + 1)
                    if l + 1 < LAYERS:
                        shifted(hsA, z, g, "hsA_ready")
                    else:
                        b = bof(g)
                        dve.scalar_tensor_tensor(out=x_cm[:, gsl(g)], in0=z[:, gsl(g)], scalar=mod[:, 0, GB, b:b + 1],
                                                 in1=x_cm[:, gsl(g)], op0=ALU.mult, op1=ALU.add).then_inc(s["x_mixed"], 1)

            dve.wait_ge(s["x_mixed"], 2 * NG)
            for g in range(NG):
                b = bof(g)
                t = slice((g % GPB) * GW, (g % GPB + 1) * GW)
                ln(ln_no(4, g))
                dve.wait_ge(s["bu_mm"], 2 * g + 1)
                if g == 0:
                    dve.wait_ge(s["tabs_ready"], 2)
                else:
                    dve.wait_ge(s["lru_g"], g)
                dve.tensor_tensor(ra[:, 0:GW], psS[:, g % 2, :], tcos[:, t], ALU.mult).then_inc(s["bu_half"], 1)
                dve.wait_ge(s["bu_mm"], 2 * g + 2)
                dve.tensor_tensor(rb[:, 0:GW], psO[:, g % 2, :], tsin[:, t], ALU.mult).then_inc(s["bu_half"], 1)
                dve.wait_ge(s["lru_a"], g + 1)
                last = g * GW - 1
                dve.tensor_tensor_scan(z[:, gsl(g)], sc[:, 7:8].to_broadcast([P, GW]), ra[:, 0:GW],
                                       0.0 if g % GPB == 0 else z[:, last:last + 1], ALU.mult, ALU.add).then_inc(s["lru_g"], 1)
                dve.wait_ge(s["lru_g"], g + 1)
                if g:
                    dve.wait_ge(s["y_done"], g)
                dve.tensor_tensor(hg[:, 0, :], z[:, gsl(g)], tcos[:, t], ALU.mult).then_inc(s["lru_m1"], 1)
                dve.wait_ge(s["y_done"], g + 1)
                dve.scalar_tensor_tensor(out=x_cm[:, gsl(g)], in0=psQK[:, g % 2, :], scalar=mod[:, 1, GA, b:b + 1],
                                         in1=x_cm[:, gsl(g)], op0=ALU.mult, op1=ALU.add).then_inc(s["xmid_ready"], 1)

            for g in range(NG):
                ln(ln_no(5, g))
            dve.wait_ge(s["sig_done"], 1)
            sg = sq[:, 0:P].rearrange("p (n e) -> p n e", n=NT)
            sel = sq[:, P:2 * P].rearrange("p (n e) -> p n e", n=NT)
            comb = sq[:, 2 * P:3 * P].rearrange("p (n e) -> p n e", n=NT)
            den = sq[:, 3 * P:3 * P + NT]
            big4 = ra[:, :].rearrange("p (n e j) -> p n e j", n=NT, e=NE)
            big5 = rb[:, :].rearrange("p (n e j) -> p n e j", n=NT, e=NE)
            sh4 = [P, NT, NE, NE]
            own.one(dve.tensor_tensor(sel, sg, rbias[:, :].unsqueeze(1).to_broadcast([P, NT, NE]), ALU.add))
            own.did(dve.tensor_tensor(big4, sel.unsqueeze(2).to_broadcast(sh4), sel.unsqueeze(3).to_broadcast(sh4), ALU.is_equal))
            own.one(dve.tensor_tensor(big5, sel.unsqueeze(2).to_broadcast(sh4), sel.unsqueeze(3).to_broadcast(sh4), ALU.is_gt))
            own.one(dve.tensor_tensor(big4, big4, before[:, :, :].unsqueeze(1).to_broadcast(sh4), ALU.mult))
            own.one(dve.tensor_tensor(big4, big4, big5, ALU.add))
            own.one(dve.tensor_reduce(sel, big4, AX.X, ALU.add))
            own.one(dve.tensor_scalar(sel, sel, 1.5, None, ALU.is_lt))
            own.one(dve.tensor_tensor(comb, sel, sg, ALU.mult))
            own.one(dve.tensor_reduce(den, comb, AX.X, ALU.add))
            dn2 = sq[:, 3 * P + NT:3 * P + 2 * NT]
            dn3 = sq[:, 3 * P + 2 * NT:3 * P + 3 * NT]
            own.did(dve.tensor_scalar(dn2, den, 1e-9, None, ALU.is_gt))
            own.one(dve.tensor_scalar(den, den, 1e-9, None, ALU.add))
            own.one(dve.reciprocal(den, den))
            own.one(dve.tensor_tensor(den, den, dn2, ALU.mult))
            own.did(dve.tensor_scalar(dn3, dn2, -0.5, 0.5, ALU.mult, ALU.add))
            own.one(dve.tensor_tensor(comb, comb, den.unsqueeze(2).to_broadcast([P, NT, NE]), ALU.mult))
            own.one(dve.tensor_tensor(sel, sel, dn3.unsqueeze(2).to_broadcast([P, NT, NE]), ALU.mult))
            dve.tensor_tensor(comb, comb, sel, ALU.add).then_inc(s["comb_ready"], 1)
            dve.wait_ge(s["comb_ready"], 1)
            dve.wait_ge(s["gb_mm"], 2)
            own.one(dve.tensor_copy(osb[:, 0:2 * P], psT0[:, 0:2 * P]))
            acc = big[:, 4, :].rearrange("p (n d) -> p n d", n=NT)
            for g in range(NG):
                for j in range(2):
                    k = 2 * g + j
                    dve.wait_ge(s["sh_act"], k + 1)
                    dve.wait_ge(s["sh_mm"], 2 * k + 2)
                    if g:
                        dve.wait_ge(s["ey_done"], g)
                    dve.tensor_tensor(hg[:, j, :], psO[:, k % 2, :], gel[:, k % 2, :], ALU.mult).then_inc(s["sh_h"], 1)
                dve.wait_ge(s["ey_done"], g + 1)
                dve.tensor_copy(big[:, 4, gsl(g)], psT1[:, :]).then_inc(s["ey_used"], 1)
            dve.wait_ge(s["ey_used"], NG)
            for g in range(NG):
                for e in range(NE):
                    k = g * NE + e
                    dve.wait_ge(s["ey_done"], NG + k + 1)
                    yb = (psS, psO)[k % 2]
                    for j in range(TPG):
                        i = dve.scalar_tensor_tensor(out=acc[:, g * TPG + j, :], in0=yb[:, 0, j * P:(j + 1) * P],
                                                     scalar=comb[:, g * TPG + j, e:e + 1], in1=acc[:, g * TPG + j, :],
                                                     op0=ALU.mult, op1=ALU.add)
                        if j == TPG - 1:
                            i.then_inc(s["ey_used"], 1)
                        else:
                            own.did(i)
                    own.sync()
                    dve.wait_ge(s["ey_used"], NG + k + 1)
                own.one(dve.tensor_tensor(acc[:, g * TPG:(g + 1) * TPG, :], acc[:, g * TPG:(g + 1) * TPG, :],
                                          osb[:, bof(g) * P:(bof(g) + 1) * P].unsqueeze(1).to_broadcast([P, TPG, P]), ALU.mult))
                dve.wait_ge(s["fx_t"], g + 1)
                i = dve.tensor_tensor(big[:, 4, gsl(g)], big[:, 4, gsl(g)], psT0[:, :], ALU.add)
                i.then_inc(s["out_ready"], TPG)

        @block.tensor
        def _(pe):
            mm = pe.matmul
            pe.wait_ge(s["ld_c"], 64)
            pe.wait_ge(s["silu_c"], 1)
            for k in range(2):
                for j in range(6):
                    i = mm(psT1[:, (k * 6 + j) * 2:(k * 6 + j) * 2 + 2], wmod[:, k, j * P:(j + 1) * P],
                           silc[:, 2 * k:2 * k + 2], start=True, stop=True)
            i.then_inc(s["mod_mm"], 1)

            def four(dst, src):
                for k in range(TPG):
                    i = pe.transpose(dst[:, k * P:(k + 1) * P], src(k), ident[:, :])
                return i

            def ln_t1(n, src):
                if n > NG:
                    pe.wait_ge(s["ln_norm"], TPG * n)
                four(psT0, lambda k: src[:, k * P:(k + 1) * P]).then_inc(s["ln_t1"], 1)

            def ln_t2(n):
                pe.wait_ge(s["ln_norm"], TPG * (n + 1))
                if n:
                    pe.wait_ge(s["ln_out"], n)
                four(psT1, lambda k: lnx[:, k, :]).then_inc(s["ln_t2"], 1)

            pe.wait_ge(s["ld_x"], 16 * NG)
            pe.wait_ge(s["ld_wa"], 64)
            pe.wait_ge(s["mod_fin"], 1)
            for g in range(NG):
                if g:
                    pe.wait_ge(s["xT_evac"], g)
                four(psT0, lambda k: xt[:, g * TPG + k, :]).then_inc(s["xT_fill"], 1)
                ln_t2(ln_no(0, g))
                pe.wait_ge(s["ln_out"], ln_no(0, g) + 1)
                if g >= 2:
                    pe.wait_ge(s["ek_ready"], g - 1)
                mm(psS[:, g % 2, :], wrkv[:, 1, :], hsA[:, gsl(g)], start=True, stop=True).then_inc(s["kv_mm"], 1)
                if g >= 2:
                    pe.wait_ge(s["ekv_ready"], g - 1)
                mm(psO[:, g % 2, :], wrkv[:, 2, :], hsA[:, gsl(g)], start=True, stop=True).then_inc(s["kv_mm"], 1)
            for g in range(NG):
                if g >= 2:
                    pe.wait_ge(s["r_ready"], g - 1)
                mm(psQK[:, g % 2, :], wrkv[:, 0, :], hsA[:, gsl(g)], start=True, stop=True).then_inc(s["r_mm"], 1)

            pe.wait_ge(s["xT_evac"], NG)
            for g in range(NG):
                pe.wait_ge(s["x_mixed"], g + 1)
                ln_t1(ln_no(1, g), x_cm[:, gsl(g)])
                ln_t2(ln_no(1, g))

            def proj_qk(n, u):
                pe.wait_ge(s["staged"], n + 1)
                for part in range(2):
                    if some(n):
                        pe.wait_ge(s["rope_ab"], 4 * n - 2 + 2 * part)
                        pe.wait_ge(s["sq_done"], 2 * n - 1 + part)
                    mm(psQK[:, part, :], hst[:, u, :], wqkv[:, part * INNER:(part + 1) * INNER], start=True,
                       stop=True).then_inc(s["qk_mm"], 1)

            def proj_v(n, u, first=False):
                if not first:
                    pe.wait_ge(s["pT_evac"], 2 * n - 1)
                mm(psT1[:, :], hst[:, u, :], wqkv[:, 2 * INNER:3 * INNER], start=True, stop=True).then_inc(s["v_fill"], 1)

            def turn_qk(n, first=False):
                pe.wait_ge(s["q_ready"], n + 1)
                if not first:
                    pe.wait_ge(s["pT_evac"], 2 * n)
                four(psT0, lambda k: qkn[:, k * P:(k + 1) * P]).then_inc(s["qT_fill"], 1)
                pe.wait_ge(s["k_ready"], n + 1)
                pe.wait_ge(s["v_evac"], 2 * n + 2)
                four(psT1, lambda k: qkn[:, INNER + k * P:INNER + (k + 1) * P]).then_inc(s["kT_fill"], 1)

            def scores(n, i, u):
                pe.wait_ge(s["qT_evac"], 2 * n + 2)
                pe.wait_ge(s["kT_evac"], n + 1)
                for hb in range(2):
                    mm(psS[:, hb, :], identb[:, :], masks[:, i, :].unsqueeze(1).to_broadcast([P, 4, P]), start=True, stop=False,
                       skip_group_check=True)
                    for h in range(4 * hb, 4 * hb + 4):
                        c = slice((h % 4) * P, (h % 4 + 1) * P)
                        kA = kT2[:, h // 2, 1:3, :] if u else kT2[:, h // 2, 0::3, :]
                        mm(psS[0:64, hb, c], qTp[:, h, 0:64], kA, start=False, stop=True, skip_group_check=True)
                        j = mm(psS[64:128, hb, c], qTp[:, h, 64:128], kT2[:, h // 2, u::2, :], start=False, stop=True,
                               skip_group_check=True)
                    j.then_inc(s["s_done"], 1)

            def attn_body(l, i, u, left=2):
                n = l * NT + i
                pe.wait_ge(s["p_ready"], 8 * n + 4)
                pe.wait_ge(s["kT_evac"], n + 1)
                four(psT1, lambda k: prob[:, k, :]).then_inc(s["pT_fill"], 1)
                if left > 1:
                    proj_qk(n + 2, u)
                pe.wait_ge(s["p_ready"], 8 * n + 8)
                if some(n):
                    pe.wait_ge(s["oT_evac"], n)
                four(psT0, lambda k: prob[:, 4 + k, :]).then_inc(s["pT_fill"], 1)
                if left:
                    proj_v(n + 1, 1 - u)
                    turn_qk(n + 1)
                if some(i):
                    pe.wait_ge(s["va_up"], passed(l, i - 1))
                if some(n):
                    pe.wait_ge(s["o_norm"], n)
                pe.wait_ge(s["pT_evac"], 2 * n + 2)
                pe.wait_ge(s["v_evac"], 2 * n + 2)
                for w in range(2):
                    for h in range(H):
                        j = mm(psO[64 * w:64 * w + 64, h // 4, (h % 4) * (DH + 1):(h % 4 + 1) * (DH + 1)],
                               pT[:, h, 64 * w:64 * w + 64], (vA, vB)[w][:, u, h, :], start=True, stop=True)
                j.then_inc(s["pv_done"], 1)
                if left:
                    scores(n + 1, i + 1, 1 - u)
                    pe.wait_ge(s["qT_evac"], 2 * n + 4)
                else:
                    pe.wait_ge(s["pT_evac"], 2 * n + 2)
                pe.wait_ge(s["o_norm"], n + 1)
                four(psT0, lambda k: osb[:, k * P:(k + 1) * P]).then_inc(s["oT_fill"], 1)

            for l in range(LAYERS):
                n = l * NT
                pe.wait_ge(s["ld_wq"], 16 * (l + 1))
                pe.wait_ge(s["r_ready"], NG)
                if l:
                    pe.wait_ge(s["z_ready"], NG * l)
                pe.wait_ge(s["ln_out"], ln_no(1 + l, NG - 1) + 1)
                proj_qk(n, 0)
                proj_v(n, 0, True)
                turn_qk(n, True)
                proj_qk(n + 1, 1)
                scores(n, 0, 0)
                with pe.Fori(0, NT // 2 - 1) as r:
                    attn_body(l, 2 * r, 0)
                    attn_body(l, 2 * r + 1, 1)
                attn_body(l, NT - 2, 0, 1)
                attn_body(l, NT - 1, 1, 0)

                def out_proj(g):
                    if g >= 2:
                        pe.wait_ge(s["z_ready"], l * NG + g - 1)
                    for c in range(4):
                        i = mm(psQK[:, g % 2, :], wo[:, c, :], oT[:, c, gsl(g)], start=(c == 0), stop=(c == 3))
                    i.then_inc(s["wo_done"], 1)

                pe.wait_ge(s["ld_wl"], 16 * 4 * (l + 1))
                pe.wait_ge(s["oT_evac"], NT * (l + 1))
                out_proj(0)
                for g in range(NG):
                    n = l * NG + g
                    pe.wait_ge(s["hsM_ready"], 2 * (n + 1))
                    ln_t1(ln_no(2 + l, g), hsM[:, gsl(g)])
                    if g + 1 < NG:
                        out_proj(g + 1)
                    ln_t2(ln_no(2 + l, g))
                    pe.wait_ge(s["ln_out"], ln_no(2 + l, g) + 1)
                    for j, (o, m) in enumerate(HCH):
                        k = n * 3 + j
                        if k >= 2:
                            pe.wait_ge(s["gelu_done"], k - 1)
                            pe.wait_ge(s["hg_done"], k - 1)
                        mm(psS[0:m, k % 2, :], w1[:, HID + o:HID + o + m], hn[:, g % 2, :], start=True,
                           stop=True).then_inc(s["g_mm"], 1)
                        mm(psO[0:m, k % 2, :], w1[:, o:o + m], hn[:, g % 2, :], start=True, stop=True).then_inc(s["a_mm"], 1)
                    pe.wait_ge(s["zmid"], n + 1)
                    for j, (o, m) in enumerate(HCH):
                        pe.wait_ge(s["hg_done"], 3 * n + j + 1)
                        i = mm(psQK[:, g % 2, :], w2[0:m, j, :], hg[0:m, j, :], start=(j == 0), stop=(j == 2))
                    i.then_inc(s["w2_done"], 1)

            pe.wait_ge(s["ld_lru"], 32)
            for g in range(NG):
                pe.wait_ge(s["x_mixed"], NG + g + 1)
                ln_t1(ln_no(4, g), x_cm[:, gsl(g)])
                ln_t2(ln_no(4, g))
                pe.wait_ge(s["ln_out"], ln_no(4, g) + 1)
                if g == 0:
                    pe.wait_ge(s["gelu_done"], 3 * NG * LAYERS)
                    pe.wait_ge(s["hg_done"], 3 * NG * LAYERS)
                if g >= 2:
                    pe.wait_ge(s["bu_half"], 2 * (g - 1))
                mm(psS[:, g % 2, :], wlru[:, 0, :], hn[:, g % 2, :], start=True, stop=True).then_inc(s["bu_mm"], 1)
                mm(psO[:, g % 2, :], wlru[:, 1, :], hn[:, g % 2, :], start=True, stop=True).then_inc(s["bu_mm"], 1)
                if g >= 2:
                    pe.wait_ge(s["xmid_ready"], g - 1)
                else:
                    pe.wait_ge(s["z_ready"], NG * LAYERS)
                mm(psQK[:, g % 2, :], wlru[:, 4, :], hn[:, g % 2, :], start=True, stop=False)
                pe.wait_ge(s["lru_m1"], g + 1)
                mm(psQK[:, g % 2, :], wcs[:, 0, :], hg[:, 0, :], start=False, stop=False)
                pe.wait_ge(s["lru_m2"], g + 1)
                mm(psQK[:, g % 2, :], wcs[:, 1, :], hg[:, 1, :], start=False, stop=True).then_inc(s["y_done"], 1)

            for g in range(NG):
                pe.wait_ge(s["xmid_ready"], g + 1)
                ln_t1(ln_no(5, g), x_cm[:, gsl(g)])
                ln_t2(ln_no(5, g))
            pe.wait_ge(s["ln_out"], ln_no(5, NG - 1) + 1)
            pe.wait_ge(s["ln_norm"], TPG * NG * 6)
            pe.wait_ge(s["ld_moe"], 16 * 5)
            pe.wait_ge(s["ld_ew"], 32)
            for n in range(NT):
                i = mm(psT0[:, n * NE:(n + 1) * NE], hsA[:, n * P:(n + 1) * P], wrt[:, :], start=True, stop=True)
            i.then_inc(s["rt_mm"], 1)
            pe.wait_ge(s["sig_done"], 1)
            for b in range(B):
                mm(psT0[:, b * P:(b + 1) * P], mod[:, 1, GB, b:b + 1].to_broadcast([P, P]), ident[:, :], start=True,
                   stop=True).then_inc(s["gb_mm"], 1)
            for g in range(NG):
                for j in range(2):
                    k = 2 * g + j
                    if k >= 2:
                        pe.wait_ge(s["sh_act"], k - 1)
                        pe.wait_ge(s["sh_h"], k - 1)
                    mm(psS[:, k % 2, :], wsh[:, 0, j * P:(j + 1) * P], hsA[:, gsl(g)], start=True, stop=True).then_inc(s["sh_mm"], 1)
                    mm(psO[:, k % 2, :], wsh[:, 1, j * P:(j + 1) * P], hsA[:, gsl(g)], start=True, stop=True).then_inc(s["sh_mm"], 1)
                pe.wait_ge(s["sh_h"], 2 * g + 2)
                if g:
                    pe.wait_ge(s["ey_used"], g)
                for n in range(TPG):
                    for j in range(2):
                        i = mm(psT1[:, n * P:(n + 1) * P], hg[:, j, n * P:(n + 1) * P], wsh2[:, j, :], start=(j == 0), stop=(j == 1))
                i.then_inc(s["ey_done"], 1)

            def expert_up(k):
                g, e = divmod(k, NE)
                if k >= 2:
                    pe.wait_ge(s["eh_act"], k - 1)
                mm(psQK[:, k % 2, :], ew1[:, e, :], hsA[:, gsl(g)], start=True, stop=True).then_inc(s["eh_mm"], 1)

            pe.wait_ge(s["xmid_ready"], NG)
            expert_up(0)
            for k in range(NG * NE):
                g, e = divmod(k, NE)
                if k + 1 < NG * NE:
                    expert_up(k + 1)
                if e == 0:
                    if g == 0:
                        pe.wait_ge(s["comb_ready"], 1)
                        pe.wait_ge(s["ey_used"], NG)
                    else:
                        pe.wait_ge(s["out_ready"], TPG * g)
                    four(psT0, lambda j: x_cm[:, g * GW + j * P:g * GW + (j + 1) * P]).then_inc(s["fx_t"], 1)
                pe.wait_ge(s["eh_act"], k + 1)
                pe.wait_ge(s["ey_used"], NG + k - 1)
                yb = (psS, psO)[k % 2]
                for n in range(TPG):
                    i = mm(yb[:, 0, n * P:(n + 1) * P], gel[:, k % 2, n * P:(n + 1) * P], ew2[:, e, :], start=True, stop=True)
                i.then_inc(s["ey_done"], 1)


def shape_constants():
    bf = mybir.dt.np(BF16)
    q = np.arange(P)[:, None]
    col = np.arange(P)[None, :]
    key = np.where((q < W) & (col >= W), col - P, col)
    off = (q < key) | (q > key + W)
    masks = np.zeros((P, NT, P), np.float32)
    for n in range(NT):
        none = off | ((key < 0) if n % (NT // B) == 0 else False)
        masks[:, n, :] = np.where(none, -1e30, 0.0)
    half_idx = np.arange(0, DH, 2, dtype=np.float32)
    inv = (1.0 / np.float32(10000.0) ** (half_idx / np.float32(DH))).astype(np.float32)
    t = np.arange(T, dtype=np.float32)
    fr = t[:, None] * inv[None, :]
    fr = np.concatenate([fr, fr], -1).astype(np.float32)
    base = ((half_idx + np.float32(0.4 * DH)) / np.float32(1.4 * DH)).astype(np.float32)
    power = ((t - T // 2) / np.float32(W // 2)).astype(np.float32)
    scl = base[None, :].astype(np.float64) ** power[:, None].astype(np.float64)
    scl = np.concatenate([scl, scl], -1)
    sign = np.where(np.arange(DH) < DH // 2, -1.0, 1.0)
    cos, sin = np.cos(fr.astype(np.float64)), np.sin(fr.astype(np.float64)) * sign
    tab = np.stack([cos * scl * 8.0, sin * scl * 8.0, cos / scl, sin / scl], 1)
    rope = tab.reshape(T // P, P, 4, DH).transpose(1, 0, 2, 3).astype(np.float32)
    before = np.broadcast_to((np.arange(NE)[None, :] < np.arange(NE)[:, None]).astype(np.float32), (P, NE, NE))
    return {
        "ident": np.eye(P, dtype=np.float32), "identb": np.eye(P).astype(bf), "masks": masks.astype(bf),
        "rope": np.ascontiguousarray(rope), "before": np.ascontiguousarray(before),
        "tvec": np.arange(T, dtype=np.float32)[None, :],
    }


def layout(i):
    def pad(v):
        return np.concatenate([v, np.zeros(P - v.shape[0], np.float32)])

    def col(n):
        return np.asarray(i[n])

    cols = [col("L0_attn_b_r"), col("L0_attn_b_k"), col("L0_attn_b_v"), col("L0_attn_b_td"), col("L0_attn_global_decay")]
    cols += [*col("L0_ffn_ln_g"), *col("L0_ffn_ln_b"), *col("L0_ffn_b2")]
    for l in range(LAYERS):
        b1 = col("L0_ffn_b1")[l]
        for side in range(2):
            cols += [pad(b1[side * HID + o:side * HID + o + m]) for o, m in HCH]
    cols += [*col("L0_c"), *col("L1_c")]
    for n in ("nu_log", "theta_log", "gamma_log"):
        v = col("L1_attn_" + n)
        cols.append(np.concatenate([v, v]))
    cols.append(np.concatenate([np.ones(64, np.float32), -np.ones(64, np.float32)]))
    br, bi, cr, ci = (col("L1_attn_" + n).T for n in ("B_re", "B_im", "C_re", "C_im"))
    arr = {
        "x": col("L0_attn_x"),
        "vec": np.stack(cols, 1),
        "wrkv": np.stack([col("L0_attn_W_" + n).T for n in "rkv"], 1),
        "wmod": np.stack([col("L0_wmod"), col("L1_wmod")], 1),
        "wqkv": col("L0_ffn_wqkv"), "wo": col("L0_ffn_wo"), "w1": col("L0_ffn_w1"), "w2": col("L0_ffn_w2"),
        "qks": np.stack([col("L0_ffn_q_scale"), col("L0_ffn_k_scale")], 1)[None],
        "wlru": np.stack([np.concatenate([br, bi], 1), np.concatenate([bi, br], 1),
                          np.concatenate([cr, ci], 0), np.concatenate([ci, cr], 0), col("L1_attn_D").T], 1),
        "wsh": np.stack([col("L1_ffn_sw1"), col("L1_ffn_sw3")], 1),
        "wsh2": col("L1_ffn_sw2").reshape(2, P, P).transpose(1, 0, 2),
        "wrt": col("L1_ffn_router_w").T,
        "rbias": col("L1_ffn_router_bias")[None],
        "ew1": col("L1_ffn_ew1").transpose(1, 0, 2),
        "ew2": col("L1_ffn_ew2").transpose(1, 0, 2),
    }
    arr.update(shape_constants())
    return {k: np.ascontiguousarray(v) for k, v in arr.items()}


def kernel(**inputs):
    import concourse.bacc as _bacc
    from concourse.bass_utils import run_bass_kernel_spmd as _run

    nc = _bacc.Bacc("TRN2", target_bir_lowering=False, num_devices=1)
    arrays = layout(inputs)
    args = {n: nc.dram_tensor(f"in_{n}", v.shape, mybir.dt.from_np(v.dtype), kind="ExternalInput").ap() for n, v in arrays.items()}
    out = nc.dram_tensor("out_0", (B, T, P), F32, kind="ExternalOutput").ap()
    program(nc, args, out)
    r = _run(nc, [{f"in_{n}": v for n, v in arrays.items()}], core_ids=[0])
    return r.results[0]["out_0"]
```

```python
from contextlib import ExitStack

import numpy as np
import concourse.bass as bass
from concourse import mybir

F32 = mybir.dt.float32
BF16 = mybir.dt.bfloat16
I32 = mybir.dt.int32
ALU = mybir.AluOpType
ACT = mybir.ActivationFunctionType
AX = mybir.AxisListType

P = 128
B, T = 2, 1024
NTOK = B * T
NT = NTOK // P
GW = 512
NG = NTOK // GW
GPB = NG // B
TPG = GW // P
LAYERS = 2
H, DH = 8, 64
W = 64
INNER = H * DH
HID = 341
HCH = [(0, 128), (128, 128), (256, 85)]
NE = 8
SEQ = 16
NCH = T // SEQ
PASSES = 4
EPS = 1e-5
TWO_PI = 6.283185

V_BR, V_BK, V_BV, V_BTD, V_GD = range(5)
V_LNG, V_LNB, V_B2 = 5, 7, 9
V_B1 = 11
V_C = 23
V_NU, V_TH, V_GAM, V_SGN = 27, 28, 29, 30
NV = 31

SA, CA, GA, SB, CB, GB = range(6)


class Steps:

    def __init__(self, eng, sem):
        self.eng, self.sem, self.base, self.n = eng, sem, 0, 0

    def did(self, ins):
        ins.then_inc(self.sem, 1)
        self.n += 1

    def sync(self):
        self.eng.wait_ge(self.sem, self.base + self.n)

    def one(self, ins):
        self.did(ins)
        self.sync()

    def enter(self, i, per):
        self.start, self.per = self.base + self.n, per
        self.base, self.n = self.start + i * per, 0

    def leave(self, times):
        assert self.n == self.per, (self.n, self.per)
        self.base, self.n = self.start + times * self.per, 0


def program(nc, a, out):
    with ExitStack() as ctx:
        def sb(name, shape, dt=F32):
            return ctx.enter_context(nc.sbuf_tensor(name, shape, dt))

        def ps(name, shape):
            return ctx.enter_context(nc.psum_tensor(name, shape, F32))

        def sem(name):
            return ctx.enter_context(nc.semaphore(name))

        ident = sb("ident", [P, P])
        identb = sb("identb", [P, P], BF16)
        masks = sb("masks", [P, NT, P], BF16)
        vec = sb("vec", [P, NV])
        wrkv = sb("wrkv", [P, 3, P])
        wmod = sb("wmod", [P, 2, 6 * P])
        wqkv = sb("wqkv", [P, 3 * INNER])
        wo = sb("wo", [P, 4, P])
        w1 = sb("w1", [P, 2 * HID])
        w2 = sb("w2", [P, 3, P])
        wlru = sb("wlru", [P, 5, P])
        wcs = sb("wcs", [P, 2, P])
        wsh = sb("wsh", [P, 2, 256])
        wsh2 = sb("wsh2", [P, 2, P])
        wrt = sb("wrt", [P, NE])
        rbias = sb("rbias", [P, NE])
        before = sb("before", [P, NE, NE])
        ropeb = sb("ropeb", [P, NT // B, 4, DH])
        qks = sb("qks", [P, 2, 2, DH])
        rope = sb("rope", [P, NT, 4, DH])
        half = sb("half", [P, 16])
        mod = sb("mod", [P, 2, 6, 2])
        modt = sb("modt", [P, 2, 2, 2])
        silc = sb("silc", [P, 4])
        sc = sb("sc", [P, 16])
        fr = sb("fr", [P, 16])
        zero = sb("zero", [P, 1])
        zeros = sb("zeros", [P, P])
        zeros2 = sb("zeros2", [P, 4])

        x_cm = sb("x_cm", [P, NTOK])
        z = sb("z", [P, NTOK])
        hsA = sb("hsA", [P, NTOK])
        big = sb("big", [P, 7, NTOK])
        xt = big[:, 6, :].rearrange("p (n d) -> p n d", n=NT)
        tvec = big[:, 5, 0:T]
        ek, gek, ekv, sab, sbb, _, rsg = (big[:, i, :] for i in range(7))
        oT = big[:, 0:4, :]
        hsM = big[:, 4, :]
        ew1 = big[:, 6, 0:NE * P].rearrange("p (e n) -> p e n", e=NE)
        ew2 = big[:, 6, NE * P:].rearrange("p (e n) -> p e n", e=NE)
        tcos = big[:, 5, T:]
        tsin = sb("tsin", [P, T])

        lnx = sb("lnx", [P, 2, TPG, P])
        st6 = sb("st6", [P, TPG, 6])
        mv = sb("mv", [P, 2, TPG, 2])
        nmean = sb("nmean", [P, 2, TPG])
        nmr = sb("nmr", [P, 2, TPG])
        rst = sb("rst", [P, 2, TPG])
        hn = sb("hn", [P, 2, GW])

        hst = sb("hst", [P, 2, P])
        sq = sb("sq", [P, 2 * INNER])
        ra = sb("ra", [P, 2 * INNER])
        rb = sb("rb", [P, 2 * INNER])
        qkn = sb("qkn", [P, 2 * INNER])
        nw = sb("nw", [P, 4, 16])
        nwi = sb("nwi", [P, 16], I32)
        qTp = sb("qTp", [P, H, P])
        kT2 = sb("kT2", [P, 4, 4, W])
        nmx = sb("nmx", [P, H])
        prob = sb("prob", [P, H, P])
        pT = sb("pT", [P, H, P])
        vAB = sb("vAB", [P, 2, 2, H * (DH + 1)])
        vA, vB = (vAB[:, k, :, :].rearrange("p u (h d) -> p u h d", h=H) for k in range(2))
        ph = vAB[:, :, :, :].rearrange("p k u n -> p (k u n)")[:, 0:B * (T + 1)].rearrange("p (b t) -> p b t", b=B)
        orc = sb("orc", [P, H])
        osb = sb("osb", [P, INNER])

        gel = sb("gel", [P, 2, GW])
        hg = sb("hg", [P, 3, GW])

        vst = sb("vst", [P, B, NCH])
        cend = sb("cend", [P, B, NCH])
        cnt = sb("cnt", [P, 32])
        cntT = sb("cntT", [P, 32])
        cnti = sb("cnti", [1, 8], I32)
        cntf = sb("cntf", [1, 8])

        psQK = ps("psQK", [P, 2, GW])
        psS = ps("psS", [P, 2, GW])
        psO = ps("psO", [P, 2, GW])
        psT0 = ps("psT0", [P, GW])
        psT1 = ps("psT1", [P, GW])

        names = """ld_x ld_ew ld_c ld_wr ld_wa ld_wq ld_wl ld_lru ld_moe ld_out st_out
            init silu_c mod_mm mod_fin mod_sc
            ln_t1 ln_var ln_rstd ln_norm ln_t2 ln_out
            xT_fill xT_evac
            kv_mm ek_ready gek_ready ekv_ready sb_ready den_ready r_mm r_ready rcp_ready quot_ready cur_ready x_mixed
            dve dve_b act_own pool_own fallback fallback_b rope_ready tabs_phase tabs_ready z_ready hsA_ready
            staged qk_mm sq_done ssq_done rope_ab rope_c rn_ready q_ready k_ready
            v_fill v_evac qT_fill qT_evac kT_fill kT_evac pT_fill pT_evac oT_fill oT_evac
            s_done negmax p_ready pv_done va_up va_low o_norm
            wo_done zmid hsM_ready g_mm a_mm gelu_done hg_done w2_done
            bu_mm bu_half lru_g lru_m1 lru_m2 lru_a y_done xmid_ready
            rt_mm sig_done pairs_ready better_ready comb_ready sh_mm sh_act sh_h ey_done eh_mm eh_act ey_used acc_done
            gb_mm gb_ready fx_t out_ready""".split()
        s = {n: sem(n) for n in names}

        block = ctx.enter_context(nc.Block())

        def gsl(g):
            return slice(g * GW, (g + 1) * GW)

        def bof(g):
            return g // GPB

        def ln_no(stage, g):
            return stage * NG + g

        def stat_bank(n):
            if n >= 4 * NG:
                bank = psS[:, 1, :] if late_kind(n) else psT0[:, :]
            elif n in (2 * NG, 3 * NG):
                bank = psQK[:, 1, :]
            else:
                bank = psS[:, 0, :] if n // NG == 1 and n % 2 else psT0[:, :]
            return bank.rearrange("p (n d) -> p n d", n=TPG)

        def stat_flat(n):
            return stat_bank(n).rearrange("p n d -> p (n d)")

        def w2_bank(l, g):
            return psT0[:, :] if g >= NG - 2 and l + 1 < LAYERS else psQK[:, 1, :]

        def out_bank(n):
            return psO[:, 1, :] if n >= 4 * NG and late_kind(n) else psT1[:, :]

        late_order = [(0, 0), (0, 1)]
        for g in range(NG + 1):
            late_order += [(k, h) for k, h in ((1, g - 1), (0, g + 2)) if 0 <= h < NG and (k or h > 1)]

        def late_ln(kind, g):
            return 4 * NG + late_order.index((kind, g))

        def late_kind(n):
            return late_order[n - 4 * NG][0] if n < 6 * NG - 1 else 0

        def bank_before(n):
            if n < 4 * NG + 2:
                return n
            return max([k + 1 for k in range(4 * NG, n) if late_kind(k) == late_kind(n)], default=4 * NG)

        def passed(l, i):
            return l * (NT - 1) + i + 1

        def tile(i):
            return slice(i * P, (i + 1) * P) if isinstance(i, int) else bass.ds(i * P, P)

        def some(count):
            return not (isinstance(count, int) and count <= 0)

        UNR = 3

        sg = sq[:, 0:P].rearrange("p (n e) -> p n e", n=NT)
        sel = sq[:, P:2 * P].rearrange("p (n e) -> p n e", n=NT)
        comb = sq[:, 2 * P:3 * P].rearrange("p (n e) -> p n e", n=NT)
        den = sq[:, 3 * P:3 * P + NT]
        big4 = ra[:, :].rearrange("p (n e j) -> p n e j", n=NT, e=NE)
        big5 = rb[:, :].rearrange("p (n e j) -> p n e j", n=NT, e=NE)
        sh4 = [P, NT, NE, NE]

        @block.sync
        def _(sp):
            xr = a["x"].rearrange("b t d -> (b t) d").rearrange("(n p) d -> p n d", p=P)
            for g in range(NG):
                sp.dma_start(xt[:, g * TPG:(g + 1) * TPG, :], xr[:, g * TPG:(g + 1) * TPG, :]).then_inc(s["ld_x"], 16)
            sp.dma_start(wrkv[:, :, :], a["wrkv"]).then_inc(s["ld_wr"], 16)
            sp.dma_start(tvec, a["tvec"].to_broadcast([P, T])).then_inc(s["ld_lru"], 16)
            sp.dma_start(wlru[:, :, :], a["wlru"]).then_inc(s["ld_lru"], 16)
            sp.dma_start(identb[:, :], a["identb"]).then_inc(s["ld_wa"], 16)
            sp.dma_start(ropeb[:, :, :, :], a["rope"]).then_inc(s["ld_wa"], 16)
            sp.dma_start(masks[:, :, :], a["masks"]).then_inc(s["ld_wa"], 16)
            sp.dma_start(qks[:, :, :, :], a["qks"].to_broadcast([P, 2, 2, DH])).then_inc(s["ld_wa"], 16)
            for l in range(LAYERS):
                if l:
                    sp.wait_ge(s["v_fill"], NT * l)
                sp.dma_start(wqkv[:, :], a["wqkv"][l]).then_inc(s["ld_wq"], 16)
                if l:
                    sp.wait_ge(s["z_ready"], NG * l)
                sp.dma_start(wo[:, :, :], a["wo"][l].rearrange("(c p) n -> p c n", p=P)).then_inc(s["ld_wl"], 16)
                sp.dma_start(w1[:, :], a["w1"][l]).then_inc(s["ld_wl"], 16)
                sp.dma_start(w2[:, 0:2, :], a["w2"][l, 0:256, :].rearrange("(c p) n -> p c n", p=P)).then_inc(s["ld_wl"], 16)
                sp.dma_start(w2[0:HID - 256, 2, :], a["w2"][l, 256:HID, :]).then_inc(s["ld_wl"], 16)
                if l == 0:
                    for dst, name in ((wsh[:, :, :], "wsh"), (wsh2[:, :, :], "wsh2"), (wrt[:, :], "wrt"),
                                      (before[:, :, :], "before")):
                        sp.dma_start(dst, a[name]).then_inc(s["ld_moe"], 16)
                    sp.dma_start(rbias[:, :], a["rbias"].to_broadcast([P, NE])).then_inc(s["ld_moe"], 16)
                    sp.wait_ge(s["x_mixed"], NG)
                    sp.dma_start(ew1, a["ew1"]).then_inc(s["ld_ew"], 16)
                    sp.dma_start(ew2, a["ew2"]).then_inc(s["ld_ew"], 16)
            outr = out.rearrange("b t d -> (b t) d").rearrange("(n p) d -> p n d", p=P)
            for g in range(NG):
                sp.wait_ge(s["out_ready"], TPG * (g + 1))
                sp.dma_start(outr[:, g * TPG:(g + 1) * TPG, :], big[:, 4, gsl(g)].rearrange("p (n d) -> p n d", n=TPG)).then_inc(s["st_out"], 16)
            sp.wait_ge(s["st_out"], 16 * NG)

        @block.scalar
        def _(act):
            act.dma_start(ident[:, :], a["ident"]).then_inc(s["ld_c"], 16)
            act.dma_start(vec[:, :], a["vec"]).then_inc(s["ld_c"], 16)
            act.dma_start(wmod[:, :, :], a["wmod"]).then_inc(s["ld_c"], 16)
            own = Steps(act, s["act_own"])

            act.wait_ge(s["ld_c"], 48)
            act.activation(silc[:, :], vec[:, V_C:V_C + 4], ACT.Silu).then_inc(s["silu_c"], 1)

            def ln_norm(n, src=None):
                act.wait_ge(s["ln_rstd"], n + 1)
                if n >= 2:
                    act.wait_ge(s["ln_t2"], n - 1)
                src = stat_bank(n) if src is None else src
                for k in range(TPG):
                    act.activation(lnx[:, n % 2, k, :], src[:, k, :], ACT.Identity, bias=nmr[:, n % 2, k:k + 1],
                                   scale=rst[:, n % 2, k:k + 1]).then_inc(s["ln_norm"], 1)

            def ln_out(n, dst, scale, bias):
                act.wait_ge(s["ln_t2"], n + 1)
                act.activation(dst, out_bank(n), ACT.Identity, bias=bias, scale=scale).then_inc(s["ln_out"], 1)

            def mixer_norm(g):
                ln_norm(ln_no(0, g), xt[:, g * TPG:(g + 1) * TPG, :])

            def mixer_out(g):
                act.wait_ge(s["xT_fill"], g + 1)
                act.activation(x_cm[:, gsl(g)], psT0[:, :], ACT.Copy).then_inc(s["xT_evac"], 1)
                if g == 0:
                    act.wait_ge(s["mod_sc"], 1)
                b = bof(g)
                ln_out(ln_no(0, g), hsA[:, gsl(g)], mod[:, 0, CA, b:b + 1], mod[:, 0, SA, b:b + 1])

            mixer_norm(0)
            mixer_out(0)
            mixer_norm(1)
            for g in range(NG):
                act.wait_ge(s["kv_mm"], 2 * g + 1)
                own.one(act.activation(ek[:, gsl(g)], psS[:, g % 2, :], ACT.Exp, bias=vec[:, V_BK:V_BK + 1]))
                act.activation(ek[:, gsl(g)], ek[:, gsl(g)], ACT.Identity, bias=0.0, scale=sc[:, 1:2]).then_inc(s["ek_ready"], 1)
                act.wait_ge(s["ek_ready"], g + 1)
                act.activation(gek[:, gsl(g)], ek[:, gsl(g)], ACT.Identity, bias=sc[:, 3:4], scale=sc[:, 2:3]).then_inc(s["gek_ready"], 1)
                if g + 1 < NG:
                    mixer_out(g + 1)
                if g + 2 < NG:
                    mixer_norm(g + 2)
            for g in range(NG):
                act.wait_ge(s["r_mm"], g + 1)
                own.one(act.activation(rsg[:, gsl(g)], psQK[:, g % 2, :], ACT.Sigmoid, bias=vec[:, V_BR:V_BR + 1]))
                act.activation(rsg[:, gsl(g)], rsg[:, gsl(g)], ACT.Copy, scale=20.0).then_inc(s["r_ready"], 1)

            def squares(n, part):
                act.wait_ge(s["qk_mm"], 2 * n + part + 1)
                if some(n):
                    act.wait_ge(s["ssq_done"], 2 * n - 1 + part)
                act.activation(sq[:, part * INNER:(part + 1) * INNER], psQK[:, part, :], ACT.Square).then_inc(s["sq_done"], 1)

            def stack_out(g):
                b = bof(g)
                ln_out(ln_no(1, g), z[:, gsl(g)], mod[:, 0, CB, b:b + 1], mod[:, 0, SB, b:b + 1])

            act.wait_ge(s["tabs_phase"], 1)
            act.activation(tcos, tcos, ACT.Sin, scale=TWO_PI).then_inc(s["tabs_ready"], 1)
            act.activation(tsin[:, :], tsin[:, :], ACT.Sin, scale=sc[:, 8:9]).then_inc(s["tabs_ready"], 1)

            ln_norm(ln_no(1, 0))
            for g in range(NG):
                stack_out(g)
                if g + 1 < NG:
                    ln_norm(ln_no(1, g + 1))
                if g == 1:
                    squares(0, 0)
                    squares(0, 1)

            def four(bank):
                return bank[:, :].rearrange("p (c t) -> p c t", c=4)

            def v_copy(l, i, u):
                n = l * NT + i
                act.wait_ge(s["v_fill"], n + 1)
                src = psT1[:, :].rearrange("p (h d) -> p h d", h=H)
                if some(i - 1):
                    act.wait_ge(s["va_up"], passed(l, i - 2))
                act.activation(vB[:, u, :, 0:DH], src, ACT.Copy).then_inc(s["v_evac"], 1)

            def v_low(n, u):
                act.wait_ge(s["v_evac"], n + 1)
                act.activation(vA[0:64, u, :, 0:DH], vB[0:64, u, :, 0:DH], ACT.Copy).then_inc(s["va_low"], 1)

            def qk_copy(n, u):
                act.wait_ge(s["qT_fill"], n + 1)
                qd = qTp[:, :, :].rearrange("p (c e) t -> p c e t", e=2)
                for e in range(2):
                    r = slice(64 * e, 64 * e + 64)
                    act.activation(qd[r, :, e, :], four(psT0)[r], ACT.Copy).then_inc(s["qT_evac"], 1)
                act.wait_ge(s["kT_fill"], n + 1)
                act.activation(kT2[:, :, u::2, :], psT1[:, :].rearrange("p (c w t) -> p c w t", c=4, w=2),
                               ACT.Copy).then_inc(s["kT_evac"], 1)

            def exps(n, hb):
                act.wait_ge(s["negmax"], 2 * n + hb + 1)
                for h in range(4 * hb, 4 * hb + 4):
                    act.activation(prob[:, h, :], psS[:, hb, (h % 4) * P:(h % 4 + 1) * P], ACT.Exp,
                                   bias=nmx[:, h:h + 1]).then_inc(s["p_ready"], 1)

            def attn_body(l, i, u, left=2):
                n = l * NT + i
                exps(n, 1)
                act.wait_ge(s["pT_fill"], 2 * n + 1)
                act.activation(pT[:, 0:4, :], four(psT1), ACT.Copy).then_inc(s["pT_evac"], 1)
                if left > 1:
                    squares(n + 2, 0)
                act.wait_ge(s["pT_fill"], 2 * n + 2)
                act.activation(pT[:, 4:8, :], four(psT0), ACT.Copy).then_inc(s["pT_evac"], 1)
                if left > 1:
                    squares(n + 2, 1)
                if left:
                    v_copy(l, i + 1, 1 - u)
                    qk_copy(n + 1, 1 - u)
                    v_low(n + 1, 1 - u)
                    exps(n + 1, 0)
                if left == 0:
                    ln_norm(ln_no(2 + l, 0))
                act.wait_ge(s["oT_fill"], n + 1)
                act.activation(oT[:, :, tile(i)], four(psT0), ACT.Copy).then_inc(s["oT_evac"], 1)

            def mlp_ln_out(l, g):
                ln_out(ln_no(2 + l, g), hn[:, g % 2, :], vec[:, V_LNG + l:V_LNG + l + 1], vec[:, V_LNB + l:V_LNB + l + 1])

            def mlp_gelus(l, g):
                for j, (o, m) in enumerate(HCH):
                    if j == 1 and g + 1 < NG:
                        ln_norm(ln_no(2 + l, g + 1))
                    elif j == 1 and l + 1 == LAYERS:
                        ln_norm(late_ln(0, 0))
                    k = (l * NG + g) * 3 + j
                    act.wait_ge(s["g_mm"], k + 1)
                    if k >= 2:
                        act.wait_ge(s["hg_done"], k - 1)
                    c = V_B1 + 6 * l + 3 + j
                    act.activation(gel[0:m, k % 2, :], psS[0:m, k % 2, :], ACT.Gelu, bias=vec[0:m, c:c + 1]).then_inc(s["gelu_done"], 1)

            for l in range(LAYERS):
                n = l * NT
                v_copy(l, 0, 0)
                squares(n + 1, 0)
                squares(n + 1, 1)
                qk_copy(n, 0)
                v_low(n, 0)
                exps(n, 0)
                attn_body(l, 0, 0)
                attn_body(l, 1, 1)
                with act.Fori(1, NT // 2 - 1) as r:
                    attn_body(l, 2 * r, 0)
                    attn_body(l, 2 * r + 1, 1)
                attn_body(l, NT - 2, 0, 1)
                attn_body(l, NT - 1, 1, 0)
                mlp_ln_out(l, 0)
                for g in range(NG):
                    if g == NG - 1 and l + 1 < LAYERS:
                        squares((l + 1) * NT, 0)
                        squares((l + 1) * NT, 1)
                    mlp_gelus(l, g)
                    if g + 1 < NG:
                        mlp_ln_out(l, g + 1)

            def lru_out(g):
                b = bof(g)
                ln_out(late_ln(0, g), hn[:, g % 2, :], mod[:, 1, CA, b:b + 1], mod[:, 1, SA, b:b + 1])

            def expert_out(g):
                b = bof(g)
                ln_out(late_ln(1, g), hsA[:, gsl(g)], mod[:, 1, CB, b:b + 1], mod[:, 1, SB, b:b + 1])

            def shared_silu(k):
                act.wait_ge(s["sh_mm"], 2 * k + 1)
                if k >= 2:
                    act.wait_ge(s["sh_h"], k - 1)
                act.activation(gel[:, k % 2, :], psS[:, k % 2, :], ACT.Silu).then_inc(s["sh_act"], 1)

            lru_out(0)
            ln_norm(late_ln(0, 1))
            for g in range(NG + 2):
                if g >= 2:
                    expert_out(g - 2)
                if g + 1 < NG:
                    lru_out(g + 1)
                if g == NG:
                    shared_silu(0)
                if 0 <= g - 1 < NG:
                    ln_norm(late_ln(1, g - 1))
                if g == NG:
                    shared_silu(1)
                if g + 2 < NG:
                    ln_norm(late_ln(0, g + 2))

            act.wait_ge(s["rt_mm"], NG)
            act.activation(sq[:, 0:P], psQK[:, 1, 0:P], ACT.Sigmoid).then_inc(s["sig_done"], 1)
            for k in range(2, 2 * NG):
                shared_silu(k)
            for g in range(NG):
                for e in range(NE):
                    k = g * NE + e
                    act.wait_ge(s["eh_mm"], k + 1)
                    if k >= 2:
                        act.wait_ge(s["ey_done"], NG + k - 1)
                    else:
                        act.wait_ge(s["sh_h"], 2 * NG)
                    act.activation(gel[:, k % 2, :], psQK[:, k % 2, :], ACT.Gelu).then_inc(s["eh_act"], 1)

        @block.gpsimd
        def _(pool):
            own = Steps(pool, s["pool_own"])
            pool.memset(zeros[:, :], 0.0).then_inc(s["init"], 1)
            pool.memset(half[:, :], -0.5).then_inc(s["init"], 1)
            pool.memset(kT2[:, :, :, :], 0.0).then_inc(s["init"], 1)
            pool.memset(qTp[:, :, :], 0.0).then_inc(s["init"], 1)
            pool.wait_ge(s["init"], 4)

            def copy(dst, src):
                return pool.tensor_scalar(dst, src, 1.0, 0.0, ALU.mult, ALU.add)

            def alone(k):
                pool.tensor_tensor(zeros2[:, k:k + 1], zeros[:, 0:1], zeros[:, 1:2], ALU.add)

            def ln_rstd(n):
                pool.wait_ge(s["ln_var"], n + 1)
                if n >= 2:
                    pool.wait_ge(s["ln_norm"], TPG * (n - 1))
                own.one(pool.tensor_tensor(rst[:, n % 2, :], mv[:, n % 2, :, 1], half[:, 0:TPG], ALU.pow))
                pool.tensor_tensor(nmr[:, n % 2, :], nmean[:, n % 2, :], rst[:, n % 2, :], ALU.mult).then_inc(s["ln_rstd"], 1)

            def rope_tables(l):
                for b in range(B):
                    for c in range(4):
                        dst = rope[:, b * 8:(b + 1) * 8, c, :]
                        src = ropeb[:, :, c, :]
                        scl = qks[:, l, c // 2, :]
                        if c % 2 == 0:
                            i = pool.tensor_tensor(dst, src, scl.unsqueeze(1).to_broadcast([P, 8, DH]), ALU.mult)
                        else:
                            r = scl.rearrange("p (a d) -> p a d", a=2)[:, ::-1, :]
                            i = pool.tensor_tensor(dst.rearrange("p n (a d) -> p n a d", a=2),
                                                   src.rearrange("p n (a d) -> p n a d", a=2),
                                                   r.unsqueeze(1).to_broadcast([P, 8, 2, DH // 2]), ALU.mult)
                        i.then_inc(s["rope_ready"], 1)

            pool.wait_ge(s["ld_c"], 48)
            own.one(pool.memset(fr[:, 0:1], float(np.e)))
            for dst, src in ((4, V_NU), (5, V_TH), (6, V_GAM)):
                own.did(pool.tensor_tensor(sc[:, dst:dst + 1], fr[:, 0:1], vec[:, src:src + 1], ALU.pow))
            own.did(pool.tensor_tensor(sc[:, 0:1], fr[:, 0:1], vec[:, V_BTD:V_BTD + 1], ALU.pow))
            own.did(pool.tensor_tensor(sc[:, 2:3], fr[:, 0:1], vec[:, V_GD:V_GD + 1], ALU.pow))
            ln_rstd(ln_no(0, 0))
            own.one(pool.tensor_scalar(fr[:, 1:2], vec[:, V_BTD:V_BTD + 1], 0.0, -T / 2, ALU.max, ALU.mult))
            own.one(pool.tensor_tensor(sc[:, 1:2], fr[:, 0:1], fr[:, 1:2], ALU.pow))
            own.did(pool.tensor_scalar(sc[:, 3:4], sc[:, 1:2], 1e-6, 0.0, ALU.mult, ALU.add))
            own.one(pool.tensor_scalar(fr[:, 2:3], sc[:, 4:5], -1.0, 0.0, ALU.mult, ALU.add))
            own.one(pool.tensor_tensor(sc[:, 7:8], fr[:, 0:1], fr[:, 2:3], ALU.pow))
            ln_rstd(ln_no(0, 1))
            pool.wait_ge(s["mod_fin"], 1)
            copy(fr[:, 3:4], sc[:, 7:8]).then_inc(s["mod_sc"], 1)
            for g in range(2, NG):
                ln_rstd(ln_no(0, g))

            def quotient(g):
                c = gsl(g)
                pool.wait_ge(s["rcp_ready"], g + 1)
                pool.tensor_tensor(ekv[:, c], ekv[:, c], gek[:, c], ALU.mult).then_inc(s["quot_ready"], 1)

            def current(g):
                c = gsl(g)
                pool.wait_ge(s["quot_ready"], g + 1)
                pool.wait_ge(s["r_ready"], g + 1)
                pool.tensor_tensor(ekv[:, c], ekv[:, c], rsg[:, c], ALU.mult).then_inc(s["cur_ready"], 1)

            for g in range(NG):
                pool.wait_ge(s["gek_ready"], g + 1)
                pool.wait_ge(s["sb_ready"], g + 1)
                pool.tensor_tensor(gek[:, gsl(g)], gek[:, gsl(g)], sbb[:, gsl(g)], ALU.add).then_inc(s["den_ready"], 1)
                if g == 1:
                    quotient(0)
                elif g == 2:
                    quotient(1)
                    current(0)
                    current(1)
                    quotient(2)
            current(2)
            pool.wait_ge(s["ld_wa"], 64)
            rope_tables(0)
            pool.wait_ge(s["ld_lru"], 32)
            C1 = 1.0 / (2 * np.pi)
            CH = float(np.round(C1 * 4096 * 4) / (4096 * 4))
            CL = C1 - CH
            MAGIC = 1.5 * 2 ** 23
            th = sc[:, 5:6]

            def ts(dst, src, s1, s2, o0, o1):
                own.one(pool.tensor_scalar(dst, src, s1, s2, o0, o1))

            def tt(dst, x0, x1, op):
                own.one(pool.tensor_tensor(dst, x0, x1, op))

            c = lambda i: fr[:, i:i + 1]
            ts(sc[:, 8:9], vec[:, V_SGN:V_SGN + 1], TWO_PI, 0.0, ALU.mult, ALU.add)
            ts(c(4), th, 4097.0, 0.0, ALU.mult, ALU.add)
            tt(c(5), c(4), th, ALU.subtract)
            tt(c(4), c(4), c(5), ALU.subtract)
            tt(c(5), th, c(4), ALU.subtract)
            ts(c(6), c(4), CH, 0.0, ALU.mult, ALU.add)
            ts(c(7), c(4), CL, 0.0, ALU.mult, ALU.add)
            ts(c(8), c(5), C1, 0.0, ALU.mult, ALU.add)
            tt(c(7), c(7), c(8), ALU.add)
            ts(c(8), c(6), 4096.0, MAGIC, ALU.mult, ALU.add)
            ts(c(8), c(8), -MAGIC, 1.0 / 4096, ALU.add, ALU.mult)
            tt(c(6), c(6), c(8), ALU.subtract)
            tt(c(9), c(6), c(7), ALU.add)
            ts(tcos[:, :], tvec, c(8), 0.0, ALU.mult, ALU.add)
            ts(tsin[:, :], tcos[:, :], MAGIC, -MAGIC, ALU.add, ALU.add)
            tt(tcos[:, :], tcos[:, :], tsin[:, :], ALU.subtract)
            ts(tsin[:, :], tvec, c(9), 0.0, ALU.mult, ALU.add)
            tt(tsin[:, :], tcos[:, :], tsin[:, :], ALU.add)
            ts(tcos[:, :], tsin[:, :], MAGIC, -MAGIC, ALU.add, ALU.add)
            tt(tsin[:, :], tsin[:, :], tcos[:, :], ALU.subtract)
            ts(tcos[:, :], tsin[:, :], 1.0, 0.25, ALU.mult, ALU.add)
            ts(tvec, tcos[:, :], MAGIC, -MAGIC, ALU.add, ALU.add)
            pool.tensor_tensor(tcos[:, :], tcos[:, :], tvec, ALU.subtract).then_inc(s["tabs_phase"], 1)
            ts(c(10), sc[:, 6:7], vec[:, V_SGN:V_SGN + 1], 1.0, ALU.mult, ALU.mult)
            ts(c(11), c(10), -1.0, 0.0, ALU.mult, ALU.add)
            ts(wcs[:, 0, :], wlru[:, 2, :], c(10), 0.0, ALU.mult, ALU.add)
            ts(wcs[:, 1, :], wlru[:, 3, :], c(11), 0.0, ALU.mult, ALU.add)
            def stage(l, i, u):
                n = l * NT + i
                if some(i - 1):
                    pool.wait_ge(s["v_fill"], n - 1)
                alone(u)
                pool.tensor_tensor(hst[:, u, :], hsA[:, tile(i)], zeros[:, :], ALU.add).then_inc(s["staged"], 1)

            for g in range(NG):
                ln_rstd(ln_no(1, g))
                if g == 1:
                    pool.wait_ge(s["hsA_ready"], 2)
                    stage(0, 0, 0)
                    stage(0, 1, 1)
            pool.wait_ge(s["x_mixed"], NG)
            pool.memset(vAB[:, :, :, :].rearrange("p k u (h d) -> p (k u h) d", h=H)[:, :, DH:], 1.0).then_inc(s["init"], 1)
            pool.wait_ge(s["init"], 5)

            def heads(x, part):
                return x[:, part * INNER:(part + 1) * INNER].rearrange("p (h d) -> p h d", h=H)

            def rope_sum(n, part):
                r = slice(part * INNER, (part + 1) * INNER)
                pool.wait_ge(s["rope_ab"], 4 * n + 2 * part + 2)
                pool.tensor_tensor(ra[:, r], ra[:, r], rb[:, r], ALU.add).then_inc(s["rope_c"], 1)

            def k_normed(n):
                pool.wait_ge(s["rope_c"], 2 * n + 2)
                pool.wait_ge(s["rn_ready"], n + 1)
                if some(n):
                    pool.wait_ge(s["kT_fill"], n)
                pool.tensor_tensor(heads(qkn, 1), heads(ra, 1), nw[:, 0, 8:16].unsqueeze(2).to_broadcast([P, H, DH]),
                                   ALU.mult).then_inc(s["k_ready"], 1)

            def pool_body(l, i, u, left=2):
                n = l * NT + i
                if left > 1:
                    stage(l, i + 2, u)
                if left:
                    rope_sum(n + 1, 0)
                    pool.wait_ge(s["rope_c"], 2 * n + 3)
                    pool.wait_ge(s["v_evac"], n + 1)
                    if some(n):
                        pool.wait_ge(s["pv_done"], n)
                    pool.tensor_tensor(vA[64:128, 1 - u, :, 0:DH], vB[64:128, u, :, 0:DH],
                                       zeros[64:128, 0:1].unsqueeze(2).to_broadcast([64, H, DH]), ALU.add).then_inc(s["va_up"], 1)
                    pool.wait_ge(s["va_up"], passed(l, i))
                    rope_sum(n + 1, 1)
                    k_normed(n + 1)

            for l in range(LAYERS):
                n = l * NT
                if l:
                    pool.wait_ge(s["hsA_ready"], 2 * NG * l + 2)
                    stage(l, 0, 0)
                    stage(l, 1, 1)
                for part in range(2):
                    rope_sum(n, part)
                k_normed(n)
                pool.wait_ge(s["hsA_ready"], 2 * NG * (l + 1))
                pool_body(l, 0, 0)
                pool_body(l, 1, 1)
                with pool.Fori(1, NT // 2 - 1) as r:
                    pool_body(l, 2 * r, 0)
                    pool_body(l, 2 * r + 1, 1)
                pool_body(l, NT - 2, 0, 1)
                ln_rstd(ln_no(2 + l, 0))
                if l + 1 < LAYERS:
                    pool.wait_ge(s["rope_ab"], 4 * NT * (l + 1))
                    rope_tables(l + 1)
                for g in range(1, NG):
                    ln_rstd(ln_no(2 + l, g))

            ln_rstd(late_ln(0, 0))
            ln_rstd(late_ln(0, 1))
            for g in range(NG):
                t = slice((g % GPB) * GW, (g % GPB + 1) * GW)
                pool.wait_ge(s["bu_half"], 2 * g + 2)
                pool.tensor_tensor(ra[:, 0:GW], ra[:, 0:GW], rb[:, 0:GW], ALU.add).then_inc(s["lru_a"], 1)
                pool.wait_ge(s["lru_g"], g + 1)
                if g:
                    pool.wait_ge(s["y_done"], g)
                pool.tensor_tensor(hg[:, 1, :], z[:, gsl(g)], tsin[:, t], ALU.mult).then_inc(s["lru_m2"], 1)
                if g:
                    ln_rstd(late_ln(1, g - 1))
                if g + 2 < NG:
                    ln_rstd(late_ln(0, g + 2))
            ln_rstd(late_ln(1, NG - 1))

            pool.wait_ge(s["pairs_ready"], 2)
            own.one(pool.tensor_tensor(big4, big4, before[:, :, :].unsqueeze(1).to_broadcast(sh4), ALU.mult))
            pool.tensor_tensor(big4, big4, big5, ALU.add).then_inc(s["better_ready"], 1)

        @block.vector
        def _(dve):
            own = Steps(dve, s["dve"])
            def ln_stats(n, src):
                if n >= 2:
                    dve.wait_ge(s["ln_norm"], TPG * (n - 1))
                for k in range(TPG):
                    own.did(dve.bn_stats(st6[:, k, :], src[:, k, :]))
                own.sync()
                for k in range(TPG):
                    own.did(dve.bn_aggr(mv[:, n % 2, k, :], st6[:, k, :]))
                own.sync()
                own.did(dve.tensor_scalar(nmean[:, n % 2, :], mv[:, n % 2, :, 0], -1.0, None, ALU.mult))
                dve.tensor_scalar(mv[:, n % 2, :, 1], mv[:, n % 2, :, 1], EPS, None, ALU.add).then_inc(s["ln_var"], 1)

            own.one(dve.memset(ph[:, :, :], 0.0))
            own.one(dve.memset(cnt[:, :], 0.0))
            dve.wait_ge(s["ld_c"], 48)
            dve.wait_ge(s["ld_x"], 16 * NG)
            ln_stats(ln_no(0, 0), xt[:, 0:TPG, :])
            ln_stats(ln_no(0, 1), xt[:, TPG:2 * TPG, :])
            def modulation(k):
                dve.wait_ge(s["mod_mm"], k + 1)
                own.one(dve.tensor_copy(mod[:, k, :, :], psQK[:, k, 0:12].rearrange("p (k n) -> p k n", k=6)))
                own.did(dve.tensor_scalar(mod[:, k, CA::3, :], mod[:, k, CA::3, :], 1.0, None, ALU.add))
                gk = mod[:, k, GA::3, :]
                sgn, mag = modt[:, 0, :, :], modt[:, 1, :, :]
                own.did(dve.tensor_scalar(sgn, gk, 0.0, 2.0, ALU.is_ge, ALU.mult))
                own.one(dve.scalar_tensor_tensor(out=mag, in0=gk, scalar=-1.0, in1=gk, op0=ALU.mult, op1=ALU.max))
                own.one(dve.tensor_scalar(sgn, sgn, -1.0, None, ALU.add))
                own.one(dve.scalar_tensor_tensor(out=gk, in0=mag, scalar=0.25, in1=sgn, op0=ALU.max, op1=ALU.mult))
                dve.tensor_copy(zero[:, 0:1], mod[:, k, 0, 0:1]).then_inc(s["mod_fin"], 1)

            modulation(0)

            def ln(n):
                dve.wait_ge(s["ln_t1"], n - NG + 1)
                ln_stats(n, stat_bank(n))

            for g in range(2, NG):
                ln_stats(ln_no(0, g), xt[:, g * TPG:(g + 1) * TPG, :])
            for g in range(NG):
                c = gsl(g)
                dve.wait_ge(s["kv_mm"], 2 * g + 2)
                dve.wait_ge(s["ek_ready"], g + 1)
                dve.scalar_tensor_tensor(out=ekv[:, c], in0=psO[:, g % 2, :], scalar=vec[:, V_BV:V_BV + 1],
                                         in1=ek[:, c], op0=ALU.add, op1=ALU.mult).then_inc(s["ekv_ready"], 1)
                dve.wait_ge(s["ekv_ready"], g + 1)
                td = sc[:, 0:1].to_broadcast([P, GW])
                last = g * GW - 1
                first = g % GPB == 0
                dve.tensor_tensor_scan(sbb[:, c], td, ek[:, c], 0.0 if first else sbb[:, last:last + 1],
                                       ALU.mult, ALU.add).then_inc(s["sb_ready"], 1)
                own.did(dve.tensor_tensor_scan(sab[:, c], td, ekv[:, c], 0.0 if first else sab[:, last:last + 1],
                                               ALU.mult, ALU.add))
                own.sync()
                own.one(dve.scalar_tensor_tensor(out=ekv[:, c], in0=ekv[:, c], scalar=sc[:, 2:3], in1=sab[:, c],
                                                 op0=ALU.mult, op1=ALU.add))
                dve.wait_ge(s["den_ready"], g + 1)
                dve.reciprocal(gek[:, c], gek[:, c]).then_inc(s["rcp_ready"], 1)
                if g == 0:
                    modulation(1)
            cur = ekv.rearrange("p (b c j) -> p b c j", b=B, c=NCH)

            def at(j):
                return ph[:, :, j:j + SEQ * (NCH - 1) + 1:SEQ]

            both = [own, Steps(dve, s["dve_b"])]
            both[1].did(dve.memset(vst[:, 1, :], 0.0))

            def membrane_pass(steps):
                for j in range(SEQ):
                    for b in range(B):
                        steps[b].sync()
                        steps[b].did(dve.scalar_tensor_tensor(out=vst[:, b, :], in0=at(j)[:, b, :], scalar=-0.3,
                                                              in1=cur[:, b, :, j], op0=ALU.mult, op1=ALU.add))
                    for b in range(B):
                        steps[b].sync()
                        steps[b].did(dve.scalar_tensor_tensor(out=at(j + 1)[:, b, :], in0=at(j)[:, b, :], scalar=-1.0,
                                                              in1=vst[:, b, :], op0=ALU.is_lt, op1=ALU.subtract))

            dve.wait_ge(s["rcp_ready"], NG)
            own.one(dve.tensor_tensor(ekv[:, c], ekv[:, c], gek[:, c], ALU.mult))
            dve.wait_ge(s["r_ready"], NG)
            own.one(dve.tensor_tensor(ekv[:, c], ekv[:, c], rsg[:, c], ALU.mult))
            dve.wait_ge(s["cur_ready"], NG - 1)
            with dve.Fori(0, PASSES - 1) as k:
                for st in both:
                    st.enter(k, 2 * SEQ)
                membrane_pass(both)
            for st in both:
                st.leave(PASSES - 1)
                st.sync()

            def checked_pass(steps):
                one = steps[0].one
                one(dve.tensor_copy(cend[:, :, :], at(0)))
                membrane_pass(steps)
                for st in steps:
                    st.sync()
                one(dve.tensor_tensor(cend[:, :, :], cend[:, :, :], at(0), ALU.not_equal))
                one(dve.tensor_reduce(cnt[:, 0:1], cend[:, :, :], AX.XY, ALU.add))
                one(dve.transpose(cntT[:, :], cnt[:, :]))
                for q in range(4):
                    steps[0].did(dve.tensor_reduce(cntf[0:1, q:q + 1], cntT[32 * q:32 * q + 1, :], AX.X, ALU.add))
                steps[0].sync()
                one(dve.tensor_reduce(cntf[0:1, 4:5], cntf[0:1, 0:4], AX.X, ALU.add))
                one(dve.tensor_copy(cnti[0:1, 0:1], cntf[0:1, 4:5]))
                return dve.value_load(cnti[0:1, 0:1], min_val=0, max_val=P * B * NCH)

            changed = checked_pass(both)
            with dve.If(changed != 0):
                again = [Steps(dve, s["fallback"]), Steps(dve, s["fallback_b"])]
                for b in range(B):
                    again[b].did(dve.memset(vst[:, b, :], 0.0))
                changed = checked_pass(again)
                with dve.If(changed != 0):
                    with dve.Fori(0, NCH) as k:
                        for st in again:
                            st.enter(k, 2 * SEQ)
                        membrane_pass(again)
                    for st in again:
                        st.leave(NCH)
                        st.sync()
            def add_spikes(g):
                b, o = bof(g), (g % GPB) * GW
                own.one(dve.tensor_scalar(ekv[:, gsl(g)], ph[:, b, 1 + o:1 + o + GW], -1.0, mod[:, 0, GA, b:b + 1],
                                          ALU.is_lt, ALU.mult))
                dve.wait_ge(s["xT_evac"], g + 1)
                dve.tensor_tensor(x_cm[:, gsl(g)], x_cm[:, gsl(g)], ekv[:, gsl(g)], ALU.add).then_inc(s["x_mixed"], 1)

            add_spikes(0)
            add_spikes(1)
            ln(ln_no(1, 0))
            add_spikes(2)
            ln(ln_no(1, 1))
            add_spikes(3)
            dve.wait_ge(s["x_mixed"], NG)

            def shifted(dst, src, g, name):
                o = g * GW
                dve.tensor_copy(dst[0:64, o:o + GW], src[0:64, o:o + GW]).then_inc(s[name], 1)
                w = GW - (g % GPB == GPB - 1)
                dve.tensor_copy(dst[64:128, o + 1:o + 1 + w], src[64:128, o:o + w]).then_inc(s[name], 1)

            own.did(dve.memset(hsA[64:128, T:T + 1], 0.0))
            own.did(dve.memset(hsA[64:128, 0:1], 0.0))
            own.did(dve.memset(hsM[64:128, T:T + 1], 0.0))
            own.did(dve.memset(hsM[64:128, 0:1], 0.0))
            own.sync()
            def heads(x):
                return x.rearrange("p (h d) -> p h d", h=H)

            def rope_product(n, slot, part, c):
                r = slice(part * INNER, (part + 1) * INNER)
                dve.wait_ge(s["sq_done"], 2 * n + part + 1)
                if some(n):
                    dve.wait_ge(s[("q_ready", "k_ready")[part]], n)
                if c == 0:
                    i = dve.tensor_tensor(heads(ra[:, r]), heads(psQK[:, part, :]),
                                          rope[:, slot, 2 * part, :].unsqueeze(1).to_broadcast([P, H, DH]), ALU.mult)
                else:
                    i = dve.tensor_tensor(rb[:, r].rearrange("p (h a d) -> p h a d", h=H, a=2),
                                          psQK[:, part, :].rearrange("p (h a d) -> p h a d", h=H, a=2)[:, :, ::-1, :],
                                          rope[:, slot, 2 * part + 1, :].rearrange("p (a d) -> p a d", a=2).unsqueeze(1)
                                          .to_broadcast([P, H, 2, DH // 2]), ALU.mult)
                i.then_inc(s["rope_ab"], 1)

            y, y2 = nw[:, 2, :], nw[:, 1, :]

            def norm_first(n, slot):
                for part in range(2):
                    dve.wait_ge(s["sq_done"], 2 * n + part + 1)
                    dve.tensor_reduce(nw[:, 1, 8 * part:8 * part + 8], heads(sq[:, part * INNER:(part + 1) * INNER]),
                                      AX.X, ALU.add).then_inc(s["ssq_done"], 1)
                dve.wait_ge(s["ssq_done"], 2 * n + 2)
                own.did(dve.tensor_scalar(y2, y2, 1e-24, None, ALU.max))
                rope_product(n, slot, 0, 0)
                own.sync()
                own.did(dve.tensor_scalar(nwi[:, :], y2.bitcast(I32), 1, None, ALU.logical_shift_right))
                own.did(dve.tensor_scalar(nw[:, 3, :], y2, -0.5, None, ALU.mult))
                rope_product(n, slot, 0, 1)
                own.sync()
                own.did(dve.tensor_scalar(y.bitcast(I32), nwi[:, :], -1.0, float(0x5F3759DF), ALU.mult, ALU.add))

            def newton(n, k):
                own.sync()
                if k % 3 == 0:
                    own.did(dve.tensor_tensor(y2, y, y, ALU.mult))
                elif k % 3 == 1:
                    own.did(dve.tensor_tensor(y2, y2, nw[:, 3, :], ALU.mult))
                elif k < 3 * UNR - 1:
                    own.did(dve.scalar_tensor_tensor(out=y, in0=y2, scalar=1.5, in1=y, op0=ALU.add, op1=ALU.mult))
                else:
                    if some(n):
                        dve.wait_ge(s["k_ready"], n)
                    dve.scalar_tensor_tensor(out=nw[:, 0, :], in0=y2, scalar=1.5, in1=y, op0=ALU.add,
                                             op1=ALU.mult).then_inc(s["rn_ready"], 1)

            def first_newton(n):
                newton(n, 0)
                newton(n, 1)

            def norm_rest(n, slot, between):
                newton(n, 2)
                rope_product(n, slot, 1, 0)
                newton(n, 3)
                if between:
                    between()
                newton(n, 4)
                rope_product(n, slot, 1, 1)
                for k in range(5, 3 * UNR):
                    newton(n, k)

                dve.wait_ge(s["rn_ready"], n + 1)
                dve.wait_ge(s["rope_c"], 2 * n + 1)
                if some(n):
                    dve.wait_ge(s["qT_fill"], n)
                dve.tensor_tensor(heads(qkn[:, 0:INNER]), heads(ra[:, 0:INNER]),
                                  nw[:, 0, 0:8].unsqueeze(2).to_broadcast([P, H, DH]), ALU.mult).then_inc(s["q_ready"], 1)

            for g in range(NG):
                if g == 2:
                    dve.wait_ge(s["rope_ready"], 8)
                    norm_first(0, 0)
                dve.wait_ge(s["ln_out"], ln_no(1, g) + 1)
                shifted(hsA, z, g, "hsA_ready")
                if g + 2 < NG:
                    ln(ln_no(1, g + 2))

            NORM_STEPS = 4 + 3 * UNR - 1

            def mid(l, g):
                n = l * NG + g
                dve.wait_ge(s["wo_done"], n + 1)
                dve.tensor_tensor(z[:, gsl(g)], z[:, gsl(g)], psQK[:, 0, :], ALU.add).then_inc(s["zmid"], 1)
                dve.wait_ge(s["zmid"], n + 1)
                shifted(hsM, z, g, "hsM_ready")

            def attn_body(l, i, left=2):
                n = l * NT + i

                def negmax(hb):
                    dve.wait_ge(s["s_done"], 2 * n + hb + 1)
                    dve.tensor_reduce(nmx[:, 4 * hb:4 * hb + 4], psS[:, hb, :].rearrange("p (h k) -> p h k", h=4),
                                      AX.X, ALU.max, negate=True).then_inc(s["negmax"], 1)
                negmax(0)
                if left:
                    norm_rest(n + 1, i + 1, lambda: negmax(1))
                else:
                    negmax(1)
                    ln(ln_no(2 + l, 0))
                if left == 1:
                    mid(l, 0)
                if left > 1:
                    norm_first(n + 2, i + 2)
                ov = psO[:, :, 0:4 * (DH + 1)].rearrange("p b (h d) -> p b h d", h=4)
                dve.wait_ge(s["pv_done"], n + 1)
                own.did(dve.reciprocal(orc[:, :].rearrange("p (b h) -> p b h", b=2), ov[:, :, :, DH]))
                if left > 1:
                    newton(n + 2, 0)
                own.sync()
                if some(n):
                    dve.wait_ge(s["oT_fill"], n)
                dve.tensor_tensor(osb[:, :].rearrange("p (b h d) -> p b h d", b=2, h=4), ov[:, :, :, 0:DH],
                                  orc[:, :].rearrange("p (b h) -> p b h", b=2).unsqueeze(3).to_broadcast([P, 2, 4, DH]),
                                  ALU.mult).then_inc(s["o_norm"], 1)
                if left > 1:
                    newton(n + 2, 1)
            for l in range(LAYERS):
                if l == 0:
                    first_newton(0)
                    norm_rest(0, 0, None)
                norm_first(l * NT + 1, 1)
                first_newton(l * NT + 1)
                attn_body(l, 0)
                attn_body(l, 1)
                with dve.Fori(1, NT // 2 - 1) as r:
                    own.enter(r - 1, 2 * (NORM_STEPS + 1))
                    attn_body(l, 2 * r)
                    attn_body(l, 2 * r + 1)
                own.leave(NT // 2 - 2)
                attn_body(l, NT - 2, 1)
                attn_body(l, NT - 1, 0)

                def gated(g, j):
                    o, m = HCH[j]
                    n = l * NG + g
                    k = n * 3 + j
                    dve.wait_ge(s["gelu_done"], k + 1)
                    dve.wait_ge(s["a_mm"], k + 1)
                    if n:
                        dve.wait_ge(s["w2_done"], n)
                    c = V_B1 + 6 * l + j
                    dve.scalar_tensor_tensor(out=hg[0:m, j, :], in0=psO[0:m, k % 2, :], scalar=vec[0:m, c:c + 1],
                                             in1=gel[0:m, k % 2, :], op0=ALU.add, op1=ALU.mult).then_inc(s["hg_done"], 1)

                mid(l, 1)
                for g in range(NG):
                    n = l * NG + g
                    if g + 1 < NG:
                        ln(ln_no(2 + l, g + 1))
                    elif l + 1 < LAYERS:
                        dve.wait_ge(s["rope_ready"], 8 * (l + 2))
                        norm_first((l + 1) * NT, 0)
                    else:
                        ln(late_ln(0, 0))
                    gated(g, 0)
                    gated(g, 1)
                    gated(g, 2)
                    if g + 2 < NG:
                        mid(l, g + 2)
                    if g == NG - 1:
                        if l + 1 < LAYERS:
                            first_newton((l + 1) * NT)
                            norm_rest((l + 1) * NT, 0, None)
                        else:
                            ln(late_ln(0, 1))
                    dve.wait_ge(s["w2_done"], n + 1)
                    dve.scalar_tensor_tensor(out=z[:, gsl(g)], in0=w2_bank(l, g), scalar=vec[:, V_B2 + l:V_B2 + l + 1],
                                             in1=z[:, gsl(g)], op0=ALU.add, op1=ALU.add).then_inc(s["z_ready"], 1)
                    dve.wait_ge(s["z_ready"], n + 1)
                    if l + 1 < LAYERS:
                        shifted(hsA, z, g, "hsA_ready")
                    else:
                        b = bof(g)
                        dve.scalar_tensor_tensor(out=x_cm[:, gsl(g)], in0=z[:, gsl(g)], scalar=mod[:, 0, GB, b:b + 1],
                                                 in1=x_cm[:, gsl(g)], op0=ALU.mult, op1=ALU.add).then_inc(s["x_mixed"], 1)

            dve.wait_ge(s["x_mixed"], 2 * NG)
            for g in range(NG):
                b = bof(g)
                t = slice((g % GPB) * GW, (g % GPB + 1) * GW)
                dve.wait_ge(s["bu_mm"], 2 * g + 1)
                if g == 0:
                    dve.wait_ge(s["tabs_ready"], 2)
                else:
                    dve.wait_ge(s["lru_g"], g)
                dve.tensor_tensor(ra[:, 0:GW], psS[:, 0, :], tcos[:, t], ALU.mult).then_inc(s["bu_half"], 1)
                dve.wait_ge(s["bu_mm"], 2 * g + 2)
                dve.tensor_tensor(rb[:, 0:GW], psO[:, 0, :], tsin[:, t], ALU.mult).then_inc(s["bu_half"], 1)
                if g:
                    ln(late_ln(1, g - 1))
                dve.wait_ge(s["lru_a"], g + 1)
                last = g * GW - 1
                dve.tensor_tensor_scan(z[:, gsl(g)], sc[:, 7:8].to_broadcast([P, GW]), ra[:, 0:GW],
                                       0.0 if g % GPB == 0 else z[:, last:last + 1], ALU.mult, ALU.add).then_inc(s["lru_g"], 1)
                dve.wait_ge(s["lru_g"], g + 1)
                if g:
                    dve.wait_ge(s["y_done"], g)
                dve.tensor_tensor(hg[:, 0, :], z[:, gsl(g)], tcos[:, t], ALU.mult).then_inc(s["lru_m1"], 1)
                if g + 2 < NG:
                    ln(late_ln(0, g + 2))
                dve.wait_ge(s["y_done"], g + 1)
                dve.scalar_tensor_tensor(out=x_cm[:, gsl(g)], in0=psQK[:, 0, :], scalar=mod[:, 1, GA, b:b + 1],
                                         in1=x_cm[:, gsl(g)], op0=ALU.mult, op1=ALU.add).then_inc(s["xmid_ready"], 1)
            ln(late_ln(1, NG - 1))

            def compare_scores():
                dve.wait_ge(s["sig_done"], 1)
                dve.wait_ge(s["gb_mm"], 2)
                own.did(dve.tensor_copy(osb[:, 0:2 * P], psQK[:, 1, P:3 * P]))
                own.one(dve.tensor_tensor(sel, sg, rbias[:, :].unsqueeze(1).to_broadcast([P, NT, NE]), ALU.add))
                for pairs, op in ((big4, ALU.is_equal), (big5, ALU.is_gt)):
                    dve.tensor_tensor(pairs, sel.unsqueeze(2).to_broadcast(sh4), sel.unsqueeze(3).to_broadcast(sh4),
                                      op).then_inc(s["pairs_ready"], 1)

            def weigh_experts():
                dve.wait_ge(s["better_ready"], 1)
                own.one(dve.tensor_reduce(sel, big4, AX.X, ALU.add))
                own.one(dve.tensor_scalar(sel, sel, 1.5, None, ALU.is_lt))
                own.one(dve.tensor_tensor(comb, sel, sg, ALU.mult))
                own.one(dve.tensor_reduce(den, comb, AX.X, ALU.add))
                dn2 = sq[:, 3 * P + NT:3 * P + 2 * NT]
                dn3 = sq[:, 3 * P + 2 * NT:3 * P + 3 * NT]
                own.did(dve.tensor_scalar(dn2, den, 1e-9, None, ALU.is_gt))
                own.one(dve.tensor_scalar(den, den, 1e-9, None, ALU.add))
                own.one(dve.reciprocal(den, den))
                own.one(dve.tensor_tensor(den, den, dn2, ALU.mult))
                own.did(dve.tensor_scalar(dn3, dn2, -0.5, 0.5, ALU.mult, ALU.add))
                own.one(dve.tensor_tensor(comb, comb, den.unsqueeze(2).to_broadcast([P, NT, NE]), ALU.mult))
                own.one(dve.tensor_tensor(sel, sel, dn3.unsqueeze(2).to_broadcast([P, NT, NE]), ALU.mult))
                dve.tensor_tensor(comb, comb, sel, ALU.add).then_inc(s["comb_ready"], 1)
                dve.wait_ge(s["comb_ready"], 1)
            acc = big[:, 4, :].rearrange("p (n d) -> p n d", n=NT)
            for g in range(NG):
                for j in range(2):
                    k = 2 * g + j
                    dve.wait_ge(s["sh_act"], k + 1)
                    dve.wait_ge(s["sh_mm"], 2 * k + 2)
                    if g:
                        dve.wait_ge(s["ey_done"], g)
                    dve.tensor_tensor(hg[:, j, :], psO[:, k % 2, :], gel[:, k % 2, :], ALU.mult).then_inc(s["sh_h"], 1)
                if g == 1:
                    compare_scores()
                dve.wait_ge(s["ey_done"], g + 1)
                dve.tensor_copy(big[:, 4, gsl(g)], psT1[:, :]).then_inc(s["ey_used"], 1)
                if g == 3:
                    weigh_experts()
            dve.wait_ge(s["ey_used"], NG)
            for g in range(NG):
                for e in range(NE):
                    k = g * NE + e
                    dve.wait_ge(s["ey_done"], NG + k + 1)
                    yb = (psS, psO)[k % 2]
                    for j in range(TPG):
                        i = dve.scalar_tensor_tensor(out=acc[:, g * TPG + j, :], in0=yb[:, 0, j * P:(j + 1) * P],
                                                     scalar=comb[:, g * TPG + j, e:e + 1], in1=acc[:, g * TPG + j, :],
                                                     op0=ALU.mult, op1=ALU.add)
                        if j == TPG - 1:
                            i.then_inc(s["ey_used"], 1)
                        else:
                            own.did(i)
                    own.sync()
                    dve.wait_ge(s["ey_used"], NG + k + 1)
                own.one(dve.tensor_tensor(acc[:, g * TPG:(g + 1) * TPG, :], acc[:, g * TPG:(g + 1) * TPG, :],
                                          osb[:, bof(g) * P:(bof(g) + 1) * P].unsqueeze(1).to_broadcast([P, TPG, P]), ALU.mult))
                dve.wait_ge(s["fx_t"], g + 1)
                i = dve.tensor_tensor(big[:, 4, gsl(g)], big[:, 4, gsl(g)], (psT0, psT1)[g % 2][:, :], ALU.add)
                i.then_inc(s["out_ready"], TPG)

        @block.tensor
        def _(pe):
            mm = pe.matmul
            def four(dst, src):
                for k in range(TPG):
                    i = pe.transpose(dst[:, k * P:(k + 1) * P], src(k), ident[:, :])
                return i

            def ln_t1(n, src):
                if n > 2 * NG:
                    pe.wait_ge(s["ln_norm"], TPG * bank_before(n))
                four(stat_flat(n), lambda k: src[:, k * P:(k + 1) * P]).then_inc(s["ln_t1"], 1)

            def ln_t2(n):
                pe.wait_ge(s["ln_norm"], TPG * (n + 1))
                if n:
                    pe.wait_ge(s["ln_out"], bank_before(n))
                four(out_bank(n), lambda k: lnx[:, n % 2, k, :]).then_inc(s["ln_t2"], 1)

            pe.wait_ge(s["ld_c"], 48)
            pe.wait_ge(s["ld_x"], 16 * NG)

            def mixer_turn(g):
                if g:
                    pe.wait_ge(s["xT_evac"], g)
                four(psT0, lambda k: xt[:, g * TPG + k, :]).then_inc(s["xT_fill"], 1)

            def receptance(g):
                if g >= 2:
                    pe.wait_ge(s["r_ready"], g - 1)
                pe.wait_ge(s["mod_fin"], min(g, 1) + 1)
                mm(psQK[:, g % 2, :], wrkv[:, 0, :], hsA[:, gsl(g)], start=True, stop=True).then_inc(s["r_mm"], 1)

            mixer_turn(0)
            pe.wait_ge(s["silu_c"], 1)
            def modulation(k):
                for j in range(6):
                    i = mm(psQK[:, k, j * 2:j * 2 + 2], wmod[:, k, j * P:(j + 1) * P],
                           silc[:, 2 * k:2 * k + 2], start=True, stop=True)
                i.then_inc(s["mod_mm"], 1)

            modulation(0)

            ln_t2(ln_no(0, 0))
            pe.wait_ge(s["ld_wr"], 16)
            for g in range(NG):
                pe.wait_ge(s["ln_out"], ln_no(0, g) + 1)
                if g >= 2:
                    pe.wait_ge(s["ek_ready"], g - 1)
                mm(psS[:, g % 2, :], wrkv[:, 1, :], hsA[:, gsl(g)], start=True, stop=True).then_inc(s["kv_mm"], 1)
                if g >= 2:
                    pe.wait_ge(s["ekv_ready"], g - 1)
                mm(psO[:, g % 2, :], wrkv[:, 2, :], hsA[:, gsl(g)], start=True, stop=True).then_inc(s["kv_mm"], 1)
                if g + 1 < NG:
                    mixer_turn(g + 1)
                    ln_t2(ln_no(0, g + 1))
                if g == 1:
                    modulation(1)
            for g in range(NG):
                receptance(g)

            def proj_qk(n, u, part):
                pe.wait_ge(s["staged"], n + 1)
                if some(n):
                    pe.wait_ge(s["rope_ab"], 4 * n - 2 + 2 * part)
                    pe.wait_ge(s["sq_done"], 2 * n - 1 + part)
                mm(psQK[:, part, :], hst[:, u, :], wqkv[:, part * INNER:(part + 1) * INNER], start=True,
                   stop=True).then_inc(s["qk_mm"], 1)

            def keep_clock(times, bank):
                for _ in range(times):
                    mm(bank, identb[:, :], masks[:, 0:4, :], start=True, stop=True)

            pe.wait_ge(s["xT_evac"], NG)
            pe.wait_ge(s["r_ready"], NG)
            pe.wait_ge(s["ld_wa"], 64)
            pe.wait_ge(s["tabs_ready"], 2)
            keep_clock(12, psO[:, 0, :])
            for g in range(NG):
                n = ln_no(1, g)
                pe.wait_ge(s["x_mixed"], g + 1)
                if g >= 2:
                    pe.wait_ge(s["ln_norm"], TPG * (n - 1))
                four((psT0[:, :], psS[:, 0, :])[g % 2], lambda k: x_cm[:, g * GW + k * P:g * GW + (k + 1) * P]).then_inc(s["ln_t1"], 1)
                if g == 3:
                    pe.wait_ge(s["ld_wa"], 64)
                    pe.wait_ge(s["ld_wq"], 16)
                    proj_qk(0, 0, 0)
                    proj_qk(0, 0, 1)
                if g:
                    ln_t2(n - 1)
            ln_t2(ln_no(1, NG - 1))

            def proj_v(n, u, first=False):
                if not first:
                    pe.wait_ge(s["pT_evac"], 2 * n - 1)
                mm(psT1[:, :], hst[:, u, :], wqkv[:, 2 * INNER:3 * INNER], start=True, stop=True).then_inc(s["v_fill"], 1)

            def turn_qk(n, first=False):
                pe.wait_ge(s["q_ready"], n + 1)
                if not first:
                    pe.wait_ge(s["pT_evac"], 2 * n)
                four(psT0, lambda k: qkn[:, k * P:(k + 1) * P]).then_inc(s["qT_fill"], 1)
                pe.wait_ge(s["k_ready"], n + 1)
                pe.wait_ge(s["v_evac"], n + 1)
                four(psT1, lambda k: qkn[:, INNER + k * P:INNER + (k + 1) * P]).then_inc(s["kT_fill"], 1)

            def scores(n, i, u):
                pe.wait_ge(s["qT_evac"], 2 * n + 2)
                pe.wait_ge(s["kT_evac"], n + 1)
                for hb in range(2):
                    mm(psS[:, hb, :], identb[:, :], masks[:, i, :].unsqueeze(1).to_broadcast([P, 4, P]), start=True, stop=False,
                       skip_group_check=True)
                    for h in range(4 * hb, 4 * hb + 4):
                        c = slice((h % 4) * P, (h % 4 + 1) * P)
                        kA = kT2[:, h // 2, 1:3, :] if u else kT2[:, h // 2, 0::3, :]
                        mm(psS[0:64, hb, c], qTp[:, h, 0:64], kA, start=False, stop=True, skip_group_check=True)
                        j = mm(psS[64:128, hb, c], qTp[:, h, 64:128], kT2[:, h // 2, u::2, :], start=False, stop=True,
                               skip_group_check=True)
                    j.then_inc(s["s_done"], 1)

            def out_proj(l, g):
                if g:
                    pe.wait_ge(s["zmid"], l * NG + g)
                for c in range(4):
                    i = mm(psQK[:, 0, :], wo[:, c, :], oT[:, c, gsl(g)], start=(c == 0), stop=(c == 3))
                i.then_inc(s["wo_done"], 1)

            def turn(l, g):
                pe.wait_ge(s["hsM_ready"], 2 * (l * NG + g + 1))
                ln_t1(ln_no(2 + l, g), hsM[:, gsl(g)])

            def attn_body(l, i, u, left=2):
                n = l * NT + i
                if left > 1:
                    proj_qk(n + 2, u, 0)
                if left == 1:
                    pe.wait_ge(s["ld_wl"], 16 * 4 * (l + 1))
                    pe.wait_ge(s["rope_ab"], 4 * NT * (l + 1) - 2)
                    out_proj(l, 0)
                if left == 0:
                    pe.wait_ge(s["rope_ab"], 4 * NT * (l + 1))
                    turn(l, 0)
                pe.wait_ge(s["p_ready"], 8 * n + 4)
                pe.wait_ge(s["kT_evac"], n + 1)
                four(psT1, lambda k: prob[:, k, :]).then_inc(s["pT_fill"], 1)
                if left > 1:
                    proj_qk(n + 2, u, 1)
                pe.wait_ge(s["p_ready"], 8 * n + 8)
                if some(n):
                    pe.wait_ge(s["oT_evac"], n)
                four(psT0, lambda k: prob[:, 4 + k, :]).then_inc(s["pT_fill"], 1)
                if left == 0:
                    out_proj(l, 1)
                if left:
                    proj_v(n + 1, 1 - u)
                    turn_qk(n + 1)
                if some(i):
                    pe.wait_ge(s["va_up"], passed(l, i - 1))
                if some(n):
                    pe.wait_ge(s["o_norm"], n)
                pe.wait_ge(s["pT_evac"], 2 * n + 2)
                pe.wait_ge(s["va_low"], n + 1)
                for w in range(2):
                    for h in range(H):
                        j = mm(psO[64 * w:64 * w + 64, h // 4, (h % 4) * (DH + 1):(h % 4 + 1) * (DH + 1)],
                               pT[:, h, 64 * w:64 * w + 64], (vA, vB)[w][:, u, h, :], start=True, stop=True)
                j.then_inc(s["pv_done"], 1)
                if left:
                    scores(n + 1, i + 1, 1 - u)
                    pe.wait_ge(s["qT_evac"], 2 * n + 4)
                else:
                    pe.wait_ge(s["pT_evac"], 2 * n + 2)
                    keep_clock(4, psS[:, 0, :])
                pe.wait_ge(s["o_norm"], n + 1)
                four(psT0, lambda k: osb[:, k * P:(k + 1) * P]).then_inc(s["oT_fill"], 1)

            def late_t1(kind, g):
                if kind == 0:
                    pe.wait_ge(s["x_mixed"], NG + g + 1)
                else:
                    pe.wait_ge(s["xmid_ready"], g + 1)
                ln_t1(late_ln(kind, g), x_cm[:, gsl(g)])

            for l in range(LAYERS):
                n = l * NT
                pe.wait_ge(s["ln_out"], ln_no(1 + l, NG - 1) + 1)
                proj_v(n, 0, True)
                proj_qk(n + 1, 1, 0)
                proj_qk(n + 1, 1, 1)
                if l:
                    pe.wait_ge(s["z_ready"], NG * l)
                turn_qk(n, True)
                scores(n, 0, 0)
                attn_body(l, 0, 0)
                attn_body(l, 1, 1)
                with pe.Fori(1, NT // 2 - 1) as r:
                    attn_body(l, 2 * r, 0)
                    attn_body(l, 2 * r + 1, 1)
                attn_body(l, NT - 2, 0, 1)
                attn_body(l, NT - 1, 1, 0)

                keep_clock(3, psS[:, 0, :])
                pe.wait_ge(s["oT_evac"], NT * (l + 1))
                ln_t2(ln_no(2 + l, 0))
                turn(l, 1)
                for g in range(NG):
                    n = l * NG + g
                    if g == NG - 1 and l + 1 < LAYERS:
                        pe.wait_ge(s["ld_wq"], 16 * (l + 2))
                        pe.wait_ge(s["zmid"], n + 1)
                        pe.wait_ge(s["z_ready"], n - 1)
                        proj_qk((l + 1) * NT, 0, 0)
                        proj_qk((l + 1) * NT, 0, 1)
                    elif g == NG - 1:
                        late_t1(0, 0)
                    pe.wait_ge(s["ln_out"], ln_no(2 + l, g) + 1)
                    for j, (o, m) in enumerate(HCH):
                        k = n * 3 + j
                        if k >= 2:
                            pe.wait_ge(s["gelu_done"], k - 1)
                            pe.wait_ge(s["hg_done"], k - 1)
                        mm(psS[0:m, k % 2, :], w1[:, HID + o:HID + o + m], hn[:, g % 2, :], start=True,
                           stop=True).then_inc(s["g_mm"], 1)
                        mm(psO[0:m, k % 2, :], w1[:, o:o + m], hn[:, g % 2, :], start=True, stop=True).then_inc(s["a_mm"], 1)
                    if g + 2 < NG:
                        out_proj(l, g + 2)
                    if g + 1 < NG:
                        ln_t2(ln_no(2 + l, g + 1))
                    if n:
                        pe.wait_ge(s["z_ready"], n)
                    if g == NG - 2 and l + 1 < LAYERS:
                        pe.wait_ge(s["ln_norm"], TPG * (ln_no(2 + l, NG - 1) + 1))
                    if g == NG - 1 and l + 1 == LAYERS:
                        ln_t2(late_ln(0, 0))
                        late_t1(0, 1)
                    for j, (o, m) in enumerate(HCH):
                        pe.wait_ge(s["hg_done"], 3 * n + j + 1)
                        i = mm(w2_bank(l, g), w2[0:m, j, :], hg[0:m, j, :], start=(j == 0), stop=(j == 2))
                    i.then_inc(s["w2_done"], 1)
                    if g + 2 < NG:
                        turn(l, g + 2)

            pe.wait_ge(s["ld_lru"], 32)
            pe.wait_ge(s["gelu_done"], 3 * NG * LAYERS)
            pe.wait_ge(s["hg_done"], 3 * NG * LAYERS)

            def router(g):
                pe.wait_ge(s["ln_out"], late_ln(1, g) + 1)
                for n in range(g * TPG, (g + 1) * TPG):
                    i = mm(psQK[:, 1, n * NE:(n + 1) * NE], hsA[:, n * P:(n + 1) * P], wrt[:, :], start=True, stop=True)
                i.then_inc(s["rt_mm"], 1)

            pe.wait_ge(s["ld_moe"], 16 * 5)
            pe.wait_ge(s["z_ready"], NG * LAYERS)
            for b in range(B):
                mm(psQK[:, 1, (b + 1) * P:(b + 2) * P], mod[:, 1, GB, b:b + 1].to_broadcast([P, P]), ident[:, :], start=True,
                   stop=True).then_inc(s["gb_mm"], 1)
            for g in range(NG + 1):
                if g < NG:
                    pe.wait_ge(s["ln_out"], late_ln(0, g) + 1)
                    if g:
                        pe.wait_ge(s["bu_half"], 2 * g)
                    mm(psS[:, 0, :], wlru[:, 0, :], hn[:, g % 2, :], start=True, stop=True).then_inc(s["bu_mm"], 1)
                    mm(psO[:, 0, :], wlru[:, 1, :], hn[:, g % 2, :], start=True, stop=True).then_inc(s["bu_mm"], 1)
                if g:
                    late_t1(1, g - 1)
                if g < NG:
                    mm(psQK[:, 0, :], wlru[:, 4, :], hn[:, g % 2, :], start=True, stop=False)
                if g >= 2:
                    ln_t2(late_ln(1, g - 2))
                if g + 1 < NG:
                    ln_t2(late_ln(0, g + 1))
                if g + 2 < NG:
                    late_t1(0, g + 2)
                if g >= 3:
                    router(g - 3)
                if g < NG:
                    pe.wait_ge(s["lru_m1"], g + 1)
                    mm(psQK[:, 0, :], wcs[:, 0, :], hg[:, 0, :], start=False, stop=False)
                    pe.wait_ge(s["lru_m2"], g + 1)
                    mm(psQK[:, 0, :], wcs[:, 1, :], hg[:, 1, :], start=False, stop=True).then_inc(s["y_done"], 1)
            router(NG - 2)

            def shared_up(k):
                g, j = divmod(k, 2)
                if k >= 2:
                    pe.wait_ge(s["sh_act"], k - 1)
                    pe.wait_ge(s["sh_h"], k - 1)
                mm(psS[:, k % 2, :], wsh[:, 0, j * P:(j + 1) * P], hsA[:, gsl(g)], start=True, stop=True).then_inc(s["sh_mm"], 1)
                mm(psO[:, k % 2, :], wsh[:, 1, j * P:(j + 1) * P], hsA[:, gsl(g)], start=True, stop=True).then_inc(s["sh_mm"], 1)

            def expert_up(k):
                g, e = divmod(k, NE)
                if k >= 2:
                    pe.wait_ge(s["eh_act"], k - 1)
                mm(psQK[:, k % 2, :], ew1[:, e, :], hsA[:, gsl(g)], start=True, stop=True).then_inc(s["eh_mm"], 1)

            pe.wait_ge(s["bu_half"], 2 * NG)
            shared_up(0)
            shared_up(1)
            ln_t2(late_ln(1, NG - 1))

            shared_up(2)
            router(NG - 1)
            pe.wait_ge(s["ld_ew"], 32)
            for g in range(NG):
                if g == NG - 1:
                    pe.wait_ge(s["xmid_ready"], NG)
                    expert_up(0)
                elif g:
                    shared_up(2 * g + 2)
                pe.wait_ge(s["sh_h"], 2 * g + 2)
                if g:
                    pe.wait_ge(s["ey_used"], g)
                for n in range(TPG):
                    for j in range(2):
                        i = mm(psT1[:, n * P:(n + 1) * P], hg[:, j, n * P:(n + 1) * P], wsh2[:, j, :], start=(j == 0), stop=(j == 1))
                i.then_inc(s["ey_done"], 1)
                if g + 1 < NG:
                    shared_up(2 * g + 3)

            pe.wait_ge(s["pairs_ready"], 1)
            for k in range(NG * NE):
                g, e = divmod(k, NE)
                if k + 1 < NG * NE:
                    expert_up(k + 1)
                if e == 0:
                    if g == 0:
                        pe.wait_ge(s["ey_used"], NG)
                    elif g >= 2:
                        pe.wait_ge(s["out_ready"], TPG * (g - 1))
                    four((psT0, psT1)[g % 2], lambda j: x_cm[:, g * GW + j * P:g * GW + (j + 1) * P]).then_inc(s["fx_t"], 1)
                pe.wait_ge(s["eh_act"], k + 1)
                pe.wait_ge(s["ey_used"], NG + k - 1)
                yb = (psS, psO)[k % 2]
                for n in range(TPG):
                    i = mm(yb[:, 0, n * P:(n + 1) * P], gel[:, k % 2, n * P:(n + 1) * P], ew2[:, e, :], start=True, stop=True)
                i.then_inc(s["ey_done"], 1)


def shape_constants():
    bf = mybir.dt.np(BF16)
    q = np.arange(P)[:, None]
    col = np.arange(P)[None, :]
    key = np.where((q < W) & (col >= W), col - P, col)
    off = (q < key) | (q > key + W)
    masks = np.zeros((P, NT, P), np.float32)
    for n in range(NT):
        none = off | ((key < 0) if n % (NT // B) == 0 else False)
        masks[:, n, :] = np.where(none, -1e30, 0.0)
    half_idx = np.arange(0, DH, 2, dtype=np.float32)
    inv = (1.0 / np.float32(10000.0) ** (half_idx / np.float32(DH))).astype(np.float32)
    t = np.arange(T, dtype=np.float32)
    fr = t[:, None] * inv[None, :]
    fr = np.concatenate([fr, fr], -1).astype(np.float32)
    base = ((half_idx + np.float32(0.4 * DH)) / np.float32(1.4 * DH)).astype(np.float32)
    power = ((t - T // 2) / np.float32(W // 2)).astype(np.float32)
    scl = base[None, :].astype(np.float64) ** power[:, None].astype(np.float64)
    scl = np.concatenate([scl, scl], -1)
    sign = np.where(np.arange(DH) < DH // 2, -1.0, 1.0)
    cos, sin = np.cos(fr.astype(np.float64)), np.sin(fr.astype(np.float64)) * sign
    tab = np.stack([cos * scl * 8.0, sin * scl * 8.0, cos / scl, sin / scl], 1)
    rope = tab.reshape(T // P, P, 4, DH).transpose(1, 0, 2, 3).astype(np.float32)
    before = np.broadcast_to((np.arange(NE)[None, :] < np.arange(NE)[:, None]).astype(np.float32), (P, NE, NE))
    return {
        "ident": np.eye(P, dtype=np.float32), "identb": np.eye(P).astype(bf), "masks": masks.astype(bf),
        "rope": np.ascontiguousarray(rope), "before": np.ascontiguousarray(before),
        "tvec": np.arange(T, dtype=np.float32)[None, :],
    }


def layout(i):
    def pad(v):
        return np.concatenate([v, np.zeros(P - v.shape[0], np.float32)])

    def col(n):
        return np.asarray(i[n])

    cols = [col("L0_attn_b_r"), col("L0_attn_b_k"), col("L0_attn_b_v"), col("L0_attn_b_td"), col("L0_attn_global_decay")]
    cols += [*col("L0_ffn_ln_g"), *col("L0_ffn_ln_b"), *col("L0_ffn_b2")]
    for l in range(LAYERS):
        b1 = col("L0_ffn_b1")[l]
        for side in range(2):
            cols += [pad(b1[side * HID + o:side * HID + o + m]) for o, m in HCH]
    cols += [*col("L0_c"), *col("L1_c")]
    for n in ("nu_log", "theta_log", "gamma_log"):
        v = col("L1_attn_" + n)
        cols.append(np.concatenate([v, v]))
    cols.append(np.concatenate([np.ones(64, np.float32), -np.ones(64, np.float32)]))
    br, bi, cr, ci = (col("L1_attn_" + n).T for n in ("B_re", "B_im", "C_re", "C_im"))
    arr = {
        "x": col("L0_attn_x"),
        "vec": np.stack(cols, 1),
        "wrkv": np.stack([col("L0_attn_W_" + n).T for n in "rkv"], 1),
        "wmod": np.stack([col("L0_wmod"), col("L1_wmod")], 1),
        "wqkv": col("L0_ffn_wqkv"), "wo": col("L0_ffn_wo"), "w1": col("L0_ffn_w1"), "w2": col("L0_ffn_w2"),
        "qks": np.stack([col("L0_ffn_q_scale"), col("L0_ffn_k_scale")], 1)[None],
        "wlru": np.stack([np.concatenate([br, bi], 1), np.concatenate([bi, br], 1),
                          np.concatenate([cr, ci], 0), np.concatenate([ci, cr], 0), col("L1_attn_D").T], 1),
        "wsh": np.stack([col("L1_ffn_sw1"), col("L1_ffn_sw3")], 1),
        "wsh2": col("L1_ffn_sw2").reshape(2, P, P).transpose(1, 0, 2),
        "wrt": col("L1_ffn_router_w").T,
        "rbias": col("L1_ffn_router_bias")[None],
        "ew1": col("L1_ffn_ew1").transpose(1, 0, 2),
        "ew2": col("L1_ffn_ew2").transpose(1, 0, 2),
    }
    arr.update(shape_constants())
    return {k: np.ascontiguousarray(v) for k, v in arr.items()}


def kernel(**inputs):
    import concourse.bacc as _bacc
    from concourse.bass_utils import run_bass_kernel_spmd as _run

    nc = _bacc.Bacc("TRN2", target_bir_lowering=False, num_devices=1)
    arrays = layout(inputs)
    args = {n: nc.dram_tensor(f"in_{n}", v.shape, mybir.dt.from_np(v.dtype), kind="ExternalInput").ap() for n, v in arrays.items()}
    out = nc.dram_tensor("out_0", (B, T, P), F32, kind="ExternalOutput").ap()
    program(nc, args, out)
    r = _run(nc, [{f"in_{n}": v for n, v in arrays.items()}], core_ids=[0])
    return r.results[0]["out_0"]
```
